# Optimizing a Trainium2 kernel written in Bass

```python
import numpy as np
import jax
import jax.numpy as jnp

def _softmax(x, axis=-1):
    return jax.nn.softmax(x, axis=axis)

def _gelu(x):
    return jax.nn.gelu(x, approximate=True)

def _silu(x):
    return jax.nn.silu(x)

def _sigmoid(x):
    return jax.nn.sigmoid(x)

def _layernorm(x, axis=-1, eps=1e-05):
    m = jnp.mean(x, axis=axis, keepdims=True)
    v = jnp.var(x, axis=axis, keepdims=True)
    return (x - m) / jnp.sqrt(v + eps)

def _scatter_add(tgt, idx, src, axis=0):
    return tgt.at[idx].add(src)

def _segment_sum(src, seg, n):
    return jax.ops.segment_sum(src, seg, n)
kernel_name = 'mk_xattn_ffn_d2_seqx_r4_3cdecd'

def setup_inputs(seed: int=0):
    np.random.seed(seed)
    _w = jnp.asarray

    def _rec_inputs():
        import jax
        import jax.numpy as jnp
        _rk = jax.random.key(seed)
        x = -0.000125 + 0.9999 * jax.random.normal(jax.random.fold_in(_rk, 1), (16, 128, 256), jnp.float32)
        _lenS = 128 - jax.random.randint(jax.random.fold_in(_rk, 7), (16,), 0, max(1, 128 // 4) + 1, jnp.int32)
        _lenS2 = 128 - jax.random.randint(jax.random.fold_in(_rk, 8), (16,), 0, max(1, 128 // 4) + 1, jnp.int32)
        _ctx_1024P = jax.random.normal(jax.random.fold_in(_rk, 11), (16, 16, 256), jnp.float32)
        _ctx_1024c = jax.random.dirichlet(jax.random.fold_in(_rk, 511), 0.3 * jnp.ones((16,), jnp.float32), (16, 128))
        _ctx_1024t = jnp.einsum('bsk,bkd->bsd', _ctx_1024c, _ctx_1024P)
        _ctx_1024t = _ctx_1024t * jax.lax.rsqrt(jnp.mean(jnp.square(_ctx_1024t)) + 1e-12) * 0.953939
        ctx_1024 = -1.52775e-05 + 0.999936 * (_ctx_1024t + 0.3 * jax.random.normal(jax.random.fold_in(_rk, 611), (16, 128, 256), jnp.float32))
        _validS = jnp.arange(128)[None, :] < _lenS[:, None]
        _validS2 = jnp.arange(128)[None, :] < _lenS2[:, None]
        _causal = jnp.tril(jnp.ones((128, 128), dtype=bool))
        mask_Bx1xS2_ik1 = jnp.where(jnp.broadcast_to(_validS2[:, None, :], (16, 1, 128)), 1, 0).astype(jnp.int32)
        return (x, ctx_1024, mask_Bx1xS2_ik1)
    x, ctx_1024, mask_Bx1xS2_ik1 = _rec_inputs()

    def _L0_xattn_setup():
        import jax, jax.numpy as jnp
        import numpy as np
        BATCH, NUM, DIMS = (16, 512, 256)
        DROPOUT = 0.1
        DROPOUT_P = DROPOUT / (DIMS * NUM)
        SCALE = 1.0 / float(np.sqrt(BATCH))
        NEG = jnp.float32(-10000000000.0)
        key = jax.random.key(seed)
        kq, kk, kv, km = jax.random.split(key, 4)
        q = jax.random.normal(kq, (BATCH, NUM, DIMS), dtype=jnp.float32)
        k = jax.random.normal(kk, (BATCH, NUM, DIMS), dtype=jnp.float32)
        v = jax.random.normal(kv, (BATCH, NUM, DIMS), dtype=jnp.float32)
        mask = jax.random.randint(km, (BATCH, 1, NUM), 0, 2, dtype=jnp.int32)
        return {'q': q, 'k': k, 'v': v, 'mask': mask}
    _L0_xattn_all = _L0_xattn_setup()
    _L0_xattn_in = {k: v for k, v in _L0_xattn_all.items() if k in ()}
    del _L0_xattn_all

    def _L0_ffn_setup():
        import jax, jax.numpy as jnp
        import numpy as np
        B, S, D = (8, 128, 256)
        H = 16
        DFF = 1024
        E = 4
        K = 2
        EPS = 1e-05

        def _layernorm(x, w, b):
            m = x.mean(-1, keepdims=True)
            v = ((x - m) ** 2).mean(-1, keepdims=True)
            return (x - m) / jnp.sqrt(v + EPS) * w + b

        def _encoder_layer(x, iw, ib, ow, ob, l1w, l1b, l2w, l2b, n1w, n1b, n2w, n2b):
            b, s, d = x.shape
            hd = d // H
            qkv = x @ iw.T + ib
            q, k, v = jnp.split(qkv, 3, axis=-1)
            rs = lambda t: t.reshape(b, s, H, hd).transpose(0, 2, 1, 3)
            q, k, v = (rs(q), rs(k), rs(v))
            scale = jnp.asarray(hd, x.dtype) ** 0.5
            scores = jnp.einsum('bhqd,bhkd->bhqk', q, k) / scale
            attn = jax.nn.softmax(scores, axis=-1)
            o = jnp.einsum('bhqk,bhkd->bhqd', attn, v).transpose(0, 2, 1, 3).reshape(b, s, d)
            o = o @ ow.T + ob
            x = _layernorm(x + o, n1w, n1b)
            ff = jax.nn.relu(x @ l1w.T + l1b) @ l2w.T + l2b
            return _layernorm(x + ff, n2w, n2b)
        key = jax.random.key(seed)
        ks = jax.random.split(key, 12)
        g = lambda k, shape: jax.random.normal(k, shape, dtype=jnp.float32) * 0.02
        return {'x': jax.random.normal(ks[0], (B, S, D), dtype=jnp.float32), 'in_proj_w': g(ks[1], (E, 3 * D, D)), 'in_proj_b': g(ks[2], (E, 3 * D)), 'out_proj_w': g(ks[3], (E, D, D)), 'out_proj_b': g(ks[4], (E, D)), 'ln1_w': jnp.ones((E, D), jnp.float32), 'ln1_b': jnp.zeros((E, D), jnp.float32), 'lin1_w': g(ks[5], (E, DFF, D)), 'lin1_b': g(ks[6], (E, DFF)), 'lin2_w': g(ks[7], (E, D, DFF)), 'lin2_b': g(ks[8], (E, D)), 'ln2_w': jnp.ones((E, D), jnp.float32), 'ln2_b': jnp.zeros((E, D), jnp.float32), 'gate_w': g(ks[9], (E, D)), 'gate_b': g(ks[10], (E,))}
    _L0_ffn_all = _L0_ffn_setup()
    _L0_ffn_in = {k: v for k, v in _L0_ffn_all.items() if k in ('in_proj_w', 'in_proj_b', 'out_proj_w', 'out_proj_b', 'ln1_w', 'ln1_b', 'lin1_w', 'lin1_b', 'lin2_w', 'lin2_b', 'ln2_w', 'ln2_b', 'gate_w', 'gate_b')}
    del _L0_ffn_all

    def _L1_xattn_setup():
        import jax, jax.numpy as jnp
        import numpy as np
        EMBED_DIM = 256
        NUM_HEADS = 16
        HEAD_DIM = EMBED_DIM // NUM_HEADS
        key = jax.random.key(seed)
        ks = jax.random.split(key, 11)
        s = 1.0 / np.sqrt(EMBED_DIM)
        inp = {'query': jax.random.normal(ks[0], (4, 512, EMBED_DIM), jnp.float32), 'key': jax.random.normal(ks[1], (4, 512, EMBED_DIM), jnp.float32), 'value': jax.random.normal(ks[2], (4, 512, EMBED_DIM), jnp.float32), 'Wq': jax.random.uniform(ks[3], (EMBED_DIM, EMBED_DIM), jnp.float32, -s, s), 'bq': jax.random.uniform(ks[4], (EMBED_DIM,), jnp.float32, -s, s), 'Wk': jax.random.uniform(ks[5], (EMBED_DIM, EMBED_DIM), jnp.float32, -s, s), 'bk': jax.random.uniform(ks[6], (EMBED_DIM,), jnp.float32, -s, s), 'Wv': jax.random.uniform(ks[7], (EMBED_DIM, EMBED_DIM), jnp.float32, -s, s), 'bv': jax.random.uniform(ks[8], (EMBED_DIM,), jnp.float32, -s, s), 'Wo': jax.random.uniform(ks[9], (EMBED_DIM, EMBED_DIM), jnp.float32, -s, s), 'bo': jax.random.uniform(ks[10], (EMBED_DIM,), jnp.float32, -s, s)}
        return inp
    _L1_xattn_all = _L1_xattn_setup()
    _L1_xattn_in = {k: v for k, v in _L1_xattn_all.items() if k in ('Wq', 'bq', 'Wk', 'bk', 'Wv', 'bv', 'Wo', 'bo')}
    del _L1_xattn_all

    def _L1_ffn_setup():
        import jax, jax.numpy as jnp
        import numpy as np
        EPS = 1e-05

        def _ln(x, g, b):
            mu = jnp.mean(x, axis=-1, keepdims=True)
            var = jnp.mean(jnp.square(x - mu), axis=-1, keepdims=True)
            return (x - mu) * jax.lax.rsqrt(var + EPS) * g + b

        def _forward(x, index_b, index_t, sw1, sb1, sw2, sb2, sw3, sb3, s_ln_g, s_ln_b, sg_w, sg_b, eg_w, eg_b, exp_bias, ew1, eb1, ew2, eb2, ew3, eb3, sel_ln_g, sel_ln_b):
            x1 = jnp.einsum('btd,hd->bth', x, sw1) + sb1
            x2 = jnp.einsum('btd,hd->bth', x, sw2) + sb2
            sh = _ln(jax.nn.silu(x1) * x2, s_ln_g, s_ln_b)
            shared_out = jnp.einsum('bth,dh->btd', sh, sw3) + sb3
            x_moe = x[index_b, index_t]
            shared_scores = jax.nn.sigmoid(x_moe @ sg_w.T + sg_b)
            expert_scores = jax.nn.sigmoid(x_moe @ eg_w.T + eg_b)
            top1_idx = jnp.argmax(expert_scores + exp_bias, axis=-1)
            top1_score = jnp.take_along_axis(expert_scores, top1_idx[:, None], axis=-1)
            weights = jax.nn.softmax(jnp.concatenate([shared_scores, top1_score], axis=-1), axis=-1)
            shared_w, expert_w = (weights[:, 0], weights[:, 1])
            shared_moe_out = shared_out[index_b, index_t] * shared_w[:, None]
            h1 = jnp.einsum('md,ehd->meh', x_moe, ew1) + eb1
            h2 = jnp.einsum('md,ehd->meh', x_moe, ew2) + eb2
            z = _ln(jax.nn.silu(h1) * h2, sel_ln_g, sel_ln_b)
            out_all = jnp.einsum('meh,edh->med', z, ew3) + eb3
            expert_out = jnp.take_along_axis(out_all, top1_idx[:, None, None], axis=1)[:, 0]
            expert_moe_out = expert_out * expert_w[:, None]
            final_out = shared_out.at[index_b, index_t].set(shared_moe_out + expert_moe_out)
            return final_out
        B, T, D, E, H, M = (2, 512, 256, 8, 128, 512)
        key = jax.random.key(seed)
        ks = jax.random.split(key, 24)
        s = 0.02
        inp = {}
        inp['x'] = jax.random.normal(ks[0], (B, T, D), jnp.float32)
        flat = jnp.arange(M, dtype=jnp.int32) * 2
        inp['index_b'] = flat // T
        inp['index_t'] = flat % T
        inp['sw1'] = jax.random.normal(ks[1], (H, D), jnp.float32) * s
        inp['sb1'] = jnp.zeros((H,), jnp.float32)
        inp['sw2'] = jax.random.normal(ks[2], (H, D), jnp.float32) * s
        inp['sb2'] = jnp.zeros((H,), jnp.float32)
        inp['sw3'] = jax.random.normal(ks[3], (D, H), jnp.float32) * s
        inp['sb3'] = jnp.zeros((D,), jnp.float32)
        inp['s_ln_g'] = jnp.ones((H,), jnp.float32)
        inp['s_ln_b'] = jnp.zeros((H,), jnp.float32)
        inp['sg_w'] = jax.random.normal(ks[4], (1, D), jnp.float32) * s
        inp['sg_b'] = jnp.zeros((1,), jnp.float32)
        inp['eg_w'] = jax.random.normal(ks[5], (E, D), jnp.float32) * s
        inp['eg_b'] = jnp.zeros((E,), jnp.float32)
        inp['exp_bias'] = jnp.zeros((E,), jnp.float32)
        inp['ew1'] = jax.random.normal(ks[6], (E, H, D), jnp.float32) * s
        inp['eb1'] = jnp.zeros((E, H), jnp.float32)
        inp['ew2'] = jax.random.normal(ks[7], (E, H, D), jnp.float32) * s
        inp['eb2'] = jnp.zeros((E, H), jnp.float32)
        inp['ew3'] = jax.random.normal(ks[8], (E, D, H), jnp.float32) * s
        inp['eb3'] = jnp.zeros((E, D), jnp.float32)
        inp['sel_ln_g'] = jnp.ones((H,), jnp.float32)
        inp['sel_ln_b'] = jnp.zeros((H,), jnp.float32)
        return inp
    _L1_ffn_all = _L1_ffn_setup()
    _L1_ffn_in = {k: v for k, v in _L1_ffn_all.items() if k in ('index_b', 'index_t', 'sw1', 'sb1', 'sw2', 'sb2', 'sw3', 'sb3', 's_ln_g', 's_ln_b', 'sg_w', 'sg_b', 'eg_w', 'eg_b', 'exp_bias', 'ew1', 'eb1', 'ew2', 'eb2', 'ew3', 'eb3', 'sel_ln_g', 'sel_ln_b')}
    del _L1_ffn_all
    return {'x': x, 'ctx_1024': ctx_1024, 'mask_Bx1xS2_ik1': mask_Bx1xS2_ik1, 'L0_ffn_in_proj_w': _L0_ffn_in['in_proj_w'], 'L0_ffn_in_proj_b': _L0_ffn_in['in_proj_b'], 'L0_ffn_out_proj_w': _L0_ffn_in['out_proj_w'], 'L0_ffn_out_proj_b': _L0_ffn_in['out_proj_b'], 'L0_ffn_ln1_w': _L0_ffn_in['ln1_w'], 'L0_ffn_ln1_b': _L0_ffn_in['ln1_b'], 'L0_ffn_lin1_w': _L0_ffn_in['lin1_w'], 'L0_ffn_lin1_b': _L0_ffn_in['lin1_b'], 'L0_ffn_lin2_w': _L0_ffn_in['lin2_w'], 'L0_ffn_lin2_b': _L0_ffn_in['lin2_b'], 'L0_ffn_ln2_w': _L0_ffn_in['ln2_w'], 'L0_ffn_ln2_b': _L0_ffn_in['ln2_b'], 'L0_ffn_gate_w': _L0_ffn_in['gate_w'], 'L0_ffn_gate_b': _L0_ffn_in['gate_b'], 'L1_xattn_Wq': _L1_xattn_in['Wq'], 'L1_xattn_bq': _L1_xattn_in['bq'], 'L1_xattn_Wk': _L1_xattn_in['Wk'], 'L1_xattn_bk': _L1_xattn_in['bk'], 'L1_xattn_Wv': _L1_xattn_in['Wv'], 'L1_xattn_bv': _L1_xattn_in['bv'], 'L1_xattn_Wo': _L1_xattn_in['Wo'], 'L1_xattn_bo': _L1_xattn_in['bo'], 'L1_ffn_index_b': _L1_ffn_in['index_b'], 'L1_ffn_index_t': _L1_ffn_in['index_t'], 'L1_ffn_sw1': _L1_ffn_in['sw1'], 'L1_ffn_sb1': _L1_ffn_in['sb1'], 'L1_ffn_sw2': _L1_ffn_in['sw2'], 'L1_ffn_sb2': _L1_ffn_in['sb2'], 'L1_ffn_sw3': _L1_ffn_in['sw3'], 'L1_ffn_sb3': _L1_ffn_in['sb3'], 'L1_ffn_s_ln_g': _L1_ffn_in['s_ln_g'], 'L1_ffn_s_ln_b': _L1_ffn_in['s_ln_b'], 'L1_ffn_sg_w': _L1_ffn_in['sg_w'], 'L1_ffn_sg_b': _L1_ffn_in['sg_b'], 'L1_ffn_eg_w': _L1_ffn_in['eg_w'], 'L1_ffn_eg_b': _L1_ffn_in['eg_b'], 'L1_ffn_exp_bias': _L1_ffn_in['exp_bias'], 'L1_ffn_ew1': _L1_ffn_in['ew1'], 'L1_ffn_eb1': _L1_ffn_in['eb1'], 'L1_ffn_ew2': _L1_ffn_in['ew2'], 'L1_ffn_eb2': _L1_ffn_in['eb2'], 'L1_ffn_ew3': _L1_ffn_in['ew3'], 'L1_ffn_eb3': _L1_ffn_in['eb3'], 'L1_ffn_sel_ln_g': _L1_ffn_in['sel_ln_g'], 'L1_ffn_sel_ln_b': _L1_ffn_in['sel_ln_b']}

def reference(x, ctx_1024, mask_Bx1xS2_ik1, L0_ffn_in_proj_w, L0_ffn_in_proj_b, L0_ffn_out_proj_w, L0_ffn_out_proj_b, L0_ffn_ln1_w, L0_ffn_ln1_b, L0_ffn_lin1_w, L0_ffn_lin1_b, L0_ffn_lin2_w, L0_ffn_lin2_b, L0_ffn_ln2_w, L0_ffn_ln2_b, L0_ffn_gate_w, L0_ffn_gate_b, L1_xattn_Wq, L1_xattn_bq, L1_xattn_Wk, L1_xattn_bk, L1_xattn_Wv, L1_xattn_bv, L1_xattn_Wo, L1_xattn_bo, L1_ffn_index_b, L1_ffn_index_t, L1_ffn_sw1, L1_ffn_sb1, L1_ffn_sw2, L1_ffn_sb2, L1_ffn_sw3, L1_ffn_sb3, L1_ffn_s_ln_g, L1_ffn_s_ln_b, L1_ffn_sg_w, L1_ffn_sg_b, L1_ffn_eg_w, L1_ffn_eg_b, L1_ffn_exp_bias, L1_ffn_ew1, L1_ffn_eb1, L1_ffn_ew2, L1_ffn_eb2, L1_ffn_ew3, L1_ffn_eb3, L1_ffn_sel_ln_g, L1_ffn_sel_ln_b):
    import jax
    import jax.numpy as jnp

    def _L0_xattn_ref(q, k, v, mask):
        import jax, jax.numpy as jnp
        import numpy as np
        BATCH, NUM, DIMS = (16, 512, 256)
        DROPOUT = 0.1
        DROPOUT_P = DROPOUT / (DIMS * NUM)
        SCALE = 1.0 / float(np.sqrt(BATCH))
        NEG = jnp.float32(-10000000000.0)
        scores = jnp.einsum('bqd,bkd->bqk', q, k) * SCALE
        scores = jnp.where(mask == 0, NEG, scores)
        probs = jax.nn.softmax(scores, axis=-1)
        probs = probs * (1.0 / (1.0 - DROPOUT_P))
        return jnp.einsum('bqk,bkd->bqd', probs, v)

    def _L0_ffn_ref(x, in_proj_w, in_proj_b, out_proj_w, out_proj_b, ln1_w, ln1_b, lin1_w, lin1_b, lin2_w, lin2_b, ln2_w, ln2_b, gate_w, gate_b):
        import jax, jax.numpy as jnp
        import numpy as np
        B, S, D = (8, 128, 256)
        H = 16
        DFF = 1024
        E = 4
        K = 2
        EPS = 1e-05

        def _layernorm(x, w, b):
            m = x.mean(-1, keepdims=True)
            v = ((x - m) ** 2).mean(-1, keepdims=True)
            return (x - m) / jnp.sqrt(v + EPS) * w + b

        def _encoder_layer(x, iw, ib, ow, ob, l1w, l1b, l2w, l2b, n1w, n1b, n2w, n2b):
            b, s, d = x.shape
            hd = d // H
            qkv = x @ iw.T + ib
            q, k, v = jnp.split(qkv, 3, axis=-1)
            rs = lambda t: t.reshape(b, s, H, hd).transpose(0, 2, 1, 3)
            q, k, v = (rs(q), rs(k), rs(v))
            scale = jnp.asarray(hd, x.dtype) ** 0.5
            scores = jnp.einsum('bhqd,bhkd->bhqk', q, k) / scale
            attn = jax.nn.softmax(scores, axis=-1)
            o = jnp.einsum('bhqk,bhkd->bhqd', attn, v).transpose(0, 2, 1, 3).reshape(b, s, d)
            o = o @ ow.T + ob
            x = _layernorm(x + o, n1w, n1b)
            ff = jax.nn.relu(x @ l1w.T + l1b) @ l2w.T + l2b
            return _layernorm(x + ff, n2w, n2b)
        gate_logits = x.mean(axis=1) @ gate_w.T + gate_b
        _, top_idx = jax.lax.top_k(gate_logits, K)
        gate_weights = jax.nn.softmax(gate_logits, axis=-1)
        mask = jnp.zeros_like(gate_weights).at[jnp.arange(x.shape[0])[:, None], top_idx].set(1.0)
        expert_outs = jax.vmap(_encoder_layer, in_axes=(None, 0, 0, 0, 0, 0, 0, 0, 0, 0, 0, 0, 0))(x, in_proj_w, in_proj_b, out_proj_w, out_proj_b, lin1_w, lin1_b, lin2_w, lin2_b, ln1_w, ln1_b, ln2_w, ln2_b)
        return jnp.einsum('be,ebsd->bsd', gate_weights * mask, expert_outs)

    def _L1_xattn_ref(query, key, value, Wq, bq, Wk, bk, Wv, bv, Wo, bo):
        import jax, jax.numpy as jnp
        import numpy as np
        EMBED_DIM = 256
        NUM_HEADS = 16
        HEAD_DIM = EMBED_DIM // NUM_HEADS
        B, T, E = query.shape
        S = key.shape[1]
        H, D = (NUM_HEADS, HEAD_DIM)
        q = (query @ Wq.T + bq).reshape(B, T, H, D).transpose(0, 2, 1, 3)
        k = (key @ Wk.T + bk).reshape(B, S, H, D).transpose(0, 2, 1, 3)
        v = (value @ Wv.T + bv).reshape(B, S, H, D).transpose(0, 2, 1, 3)
        scores = jnp.einsum('bhtd,bhsd->bhts', q, k) / np.sqrt(D)
        causal = jnp.triu(jnp.full((T, S), -jnp.inf, jnp.float32), k=1)
        scores = scores + causal[None, None]
        attn = jax.nn.softmax(scores, axis=-1)
        out = jnp.einsum('bhts,bhsd->bhtd', attn, v)
        out = out.transpose(0, 2, 1, 3).reshape(B, T, E)
        out = out @ Wo.T + bo
        return out

    def _L1_ffn_ref(x, index_b, index_t, sw1, sb1, sw2, sb2, sw3, sb3, s_ln_g, s_ln_b, sg_w, sg_b, eg_w, eg_b, exp_bias, ew1, eb1, ew2, eb2, ew3, eb3, sel_ln_g, sel_ln_b):
        import jax, jax.numpy as jnp
        import numpy as np
        EPS = 1e-05

        def _ln(x, g, b):
            mu = jnp.mean(x, axis=-1, keepdims=True)
            var = jnp.mean(jnp.square(x - mu), axis=-1, keepdims=True)
            return (x - mu) * jax.lax.rsqrt(var + EPS) * g + b

        def _forward(x, index_b, index_t, sw1, sb1, sw2, sb2, sw3, sb3, s_ln_g, s_ln_b, sg_w, sg_b, eg_w, eg_b, exp_bias, ew1, eb1, ew2, eb2, ew3, eb3, sel_ln_g, sel_ln_b):
            x1 = jnp.einsum('btd,hd->bth', x, sw1) + sb1
            x2 = jnp.einsum('btd,hd->bth', x, sw2) + sb2
            sh = _ln(jax.nn.silu(x1) * x2, s_ln_g, s_ln_b)
            shared_out = jnp.einsum('bth,dh->btd', sh, sw3) + sb3
            x_moe = x[index_b, index_t]
            shared_scores = jax.nn.sigmoid(x_moe @ sg_w.T + sg_b)
            expert_scores = jax.nn.sigmoid(x_moe @ eg_w.T + eg_b)
            top1_idx = jnp.argmax(expert_scores + exp_bias, axis=-1)
            top1_score = jnp.take_along_axis(expert_scores, top1_idx[:, None], axis=-1)
            weights = jax.nn.softmax(jnp.concatenate([shared_scores, top1_score], axis=-1), axis=-1)
            shared_w, expert_w = (weights[:, 0], weights[:, 1])
            shared_moe_out = shared_out[index_b, index_t] * shared_w[:, None]
            h1 = jnp.einsum('md,ehd->meh', x_moe, ew1) + eb1
            h2 = jnp.einsum('md,ehd->meh', x_moe, ew2) + eb2
            z = _ln(jax.nn.silu(h1) * h2, sel_ln_g, sel_ln_b)
            out_all = jnp.einsum('meh,edh->med', z, ew3) + eb3
            expert_out = jnp.take_along_axis(out_all, top1_idx[:, None, None], axis=1)[:, 0]
            expert_moe_out = expert_out * expert_w[:, None]
            final_out = shared_out.at[index_b, index_t].set(shared_moe_out + expert_moe_out)
            return final_out
        return _forward(x, index_b, index_t, sw1, sb1, sw2, sb2, sw3, sb3, s_ln_g, s_ln_b, sg_w, sg_b, eg_w, eg_b, exp_bias, ew1, eb1, ew2, eb2, ew3, eb3, sel_ln_g, sel_ln_b)
    x = x + _L0_xattn_ref(_layernorm(x, axis=-1), ctx_1024, ctx_1024, mask_Bx1xS2_ik1)
    x = x + _L0_ffn_ref(_layernorm(x, axis=-1), L0_ffn_in_proj_w, L0_ffn_in_proj_b, L0_ffn_out_proj_w, L0_ffn_out_proj_b, L0_ffn_ln1_w, L0_ffn_ln1_b, L0_ffn_lin1_w, L0_ffn_lin1_b, L0_ffn_lin2_w, L0_ffn_lin2_b, L0_ffn_ln2_w, L0_ffn_ln2_b, L0_ffn_gate_w, L0_ffn_gate_b)
    x = x + _L1_xattn_ref(_layernorm(x, axis=-1), ctx_1024, ctx_1024, L1_xattn_Wq, L1_xattn_bq, L1_xattn_Wk, L1_xattn_bk, L1_xattn_Wv, L1_xattn_bv, L1_xattn_Wo, L1_xattn_bo)
    x = x + _L1_ffn_ref(_layernorm(x, axis=-1), L1_ffn_index_b, L1_ffn_index_t, L1_ffn_sw1, L1_ffn_sb1, L1_ffn_sw2, L1_ffn_sb2, L1_ffn_sw3, L1_ffn_sb3, L1_ffn_s_ln_g, L1_ffn_s_ln_b, L1_ffn_sg_w, L1_ffn_sg_b, L1_ffn_eg_w, L1_ffn_eg_b, L1_ffn_exp_bias, L1_ffn_ew1, L1_ffn_eb1, L1_ffn_ew2, L1_ffn_eb2, L1_ffn_ew3, L1_ffn_eb3, L1_ffn_sel_ln_g, L1_ffn_sel_ln_b)
    return x

_drawn_inputs = setup_inputs


def setup_inputs(seed=0):
    import zlib

    import numpy as np

    out = dict(_drawn_inputs(seed))
    spreads = {'L0_ffn_ln1_w': (1.0, 0.2),
     'L0_ffn_ln1_b': (0.0, 0.415),
     'L0_ffn_ln2_w': (1.0, 0.2),
     'L0_ffn_ln2_b': (0.0, 0.405),
     'L1_ffn_sb1': (0.0, 0.1),
     'L1_ffn_sb2': (0.0, 0.1),
     'L1_ffn_sb3': (0.0, 0.1),
     'L1_ffn_s_ln_g': (1.0, 0.6),
     'L1_ffn_s_ln_b': (0.0, 0.8),
     'L1_ffn_eg_b': (0.0, 0.8),
     'L1_ffn_exp_bias': (0.0, 0.371),
     'L1_ffn_eb1': (0.0, 0.8),
     'L1_ffn_eb2': (0.0, 0.8),
     'L1_ffn_eb3': (0.0, 0.8),
     'L1_ffn_sel_ln_g': (1.0, 0.6),
     'L1_ffn_sel_ln_b': (0.0, 0.8)}
    factors = {'L0_ffn_in_proj_w': 7.163,
     'L0_ffn_in_proj_b': 8.0,
     'L0_ffn_out_proj_w': 7.28,
     'L0_ffn_out_proj_b': 50.822,
     'L0_ffn_lin1_b': 30.446,
     'L0_ffn_lin2_b': 8.0,
     'L0_ffn_gate_b': 4.634,
     'L1_xattn_Wq': 4.496,
     'L1_xattn_bq': 8.0,
     'L1_xattn_Wk': 4.586,
     'L1_xattn_bk': 64.0,
     'L1_xattn_bv': 5.538,
     'L1_xattn_bo': 2.947,
     'L1_ffn_sg_w': 24.7,
     'L1_ffn_eg_w': 8.0,
     'L1_ffn_ew1': 4.088,
     'L1_ffn_ew2': 4.179,
     'L1_ffn_ew3': 3.95}
    for name, (base, spread) in spreads.items():
        noise = np.random.default_rng([zlib.crc32(name.encode()), seed]).standard_normal(out[name].shape)
        drawn = base * np.exp(spread * noise) if base else spread * noise
        out[name] = jnp.asarray(drawn.astype(out[name].dtype))
    for name, factor in factors.items():
        out[name] = (out[name] * factor).astype(out[name].dtype)
    return out
```

```python
import concourse.bass as bass
from concourse import mybir
from contextlib import ExitStack

B, S, D = 16, 128, 256
KC = D // 128
H, HD = 16, 16
E, TOPK = 4, 2
DFF = 1024
FC = DFF // 128
EM, HM, M = 8, 128, 512
MT = M // 128
UNITS = B * TOPK
EPS = 1e-5
NEG = -1e10
SCALE_A = 0.25
KEEP = 1.0 / (1.0 - 0.1 / (256 * 512))
SCALE_H = HD ** -0.5

W_QKV, W_OUT, W_L1, W_L2 = 0, KC * 3 * D, KC * 4 * D, KC * 4 * D + KC * DFF
W_EXP = W_L2 + FC * D
W_ALL = E * W_EXP
WCH = W_ALL // B
W_CAUS = KC * 4 * D
T_S12, T_S3 = 0, KC * 2 * HM
T_E12 = T_S3 + D
T_E3 = T_E12 + KC * EM * 2 * HM
T_ALL = T_E3 + EM * D
TCH = T_ALL // B
V_QKV, V_OUT, V_L2, V_G1, V_B1, V_G2, V_B2 = 0, 768, 1024, 1280, 1536, 1792, 2048
V_EXP = 2304
V_ALL = E * V_EXP
U_S12, U_S3, U_SG, U_SB, U_EG, U_EB, U_GB, U_XB = 0, 256, 512, 640, 768, 896, 1024, 1033
U_ALL = U_XB + EM
R_STAGE, R_TVEC, R_COMB = 0, 2 * TCH + 160, 2304
R_ROWI = R_COMB + MT * 3 * D
R_ROWF = R_ROWI + 2 * M
R_FIN = R_ROWF + 2 * M
R_POS = R_FIN + MT * D
C_ID, C_ME, C_MO, C_RNK4, C_ID4, C_RNK8, C_M, C_HALF, C_EPS = 0, 128, 129, 130, 134, 138, 146, 150, 151
C_ALL = 152
K_SEL, K_CS, K_CT, K_ROW = 0, 512, 640, 768
K_ALL = K_ROW + E * 128


def encoder_kernel(nc, x_d, ctx_d, mask_d, w_d, wc_d, vec_d, vc_d, b1_d, gw_d, gb_d, tw_d, tvec_d, tg_d, tb_d,
                   ib_d, it_d, ibr_d, itr_d, cst_d, kst_d, pos_d, out, comb_d):
    f32, bf16, i32, u32 = mybir.dt.float32, mybir.dt.bfloat16, mybir.dt.int32, mybir.dt.uint32
    ALU = mybir.AluOpType
    ACT = mybir.ActivationFunctionType
    AX = mybir.AxisListType
    ds = bass.ds

    stack = ExitStack()
    with stack:
        def sb(name, shape, dt=f32):
            return stack.enter_context(nc.sbuf_tensor(name, shape, dt))

        ps = stack.enter_context(nc.psum_tensor("ps", [128, 8, 512], f32))

        x = sb("x", [128, B * D])
        w_hi = sb("w_hi", [128, W_ALL], bf16)
        w_lo = sb("w_lo", [128, W_ALL], bf16)
        vec = sb("vec", [128, V_ALL])
        b1hl = sb("b1hl", [64, DFF], bf16)
        cst = sb("cst", [128, C_ALL])
        identb = sb("identb", [128, 128], bf16)
        kst = sb("kst", [128, K_ALL], bf16)
        gate_b = sb("gate_b", [128, E])
        ones = sb("ones", [128, 128])
        gmean = sb("gmean", [128, KC, B])
        gprod = sb("gprod", [128, KC, B, E])
        gw = sb("gw", [128, KC, E])
        gs = sb("gs", [128, 8, B])
        gate_w = sb("gate_w", [128, UNITS])
        chosen = sb("chosen", [128, UNITS], i32)

        y = sb("y", [128, D])
        ycT_hi = sb("ycT_hi", [128, 2 * KC, 128], bf16)
        ycT_lo = sb("ycT_lo", [128, 2 * KC, 128], bf16)
        qk = sb("qk", [128, 2 * D])
        v = sb("v", [128, H, 32])
        qh = sb("qh", [128, KC, 128], bf16)
        ql = sb("ql", [128, KC, 128], bf16)
        khm = sb("khm", [128, KC, 2, 128], bf16)
        klm = sb("klm", [128, KC, 2, 128], bf16)
        mx = sb("mx", [128, H])
        mtile = sb("mtile", [128, 4, 2, H], bf16)
        mT = sb("mT", [128, 128], bf16)
        pT = sb("pT", [128, H, 128])
        oT = qk[:, :].rearrange("p (a q) -> p a q", q=128)
        o_rs = sb("o_rs", [128, H])
        o = sb("o", [128, D])
        ooh = sb("ooh", [128, KC, 128], bf16)
        ool = sb("ool", [128, KC, 128], bf16)
        ybo = sb("ybo", [128, D])
        t1 = sb("t1", [128, D])
        ctxb = sb("ctxb", [128, 2, D])
        x1 = sb("x1", [128, D])
        x1b = sb("x1b", [128, D])
        xh = sb("xh", [128, KC, 128], bf16)
        xl = sb("xl", [128, KC, 128], bf16)
        h = sb("h", [128, DFF])
        hh = sb("hh", [128, FC, 128], bf16)
        hl = sb("hl", [128, FC, 128], bf16)
        t2 = sb("t2", [128, D])
        y2 = sb("y2", [128, D])
        st = sb("st", [128, 4, 6])
        mv = sb("mv", [128, 4, 2])
        rs = sb("rs", [128, 4, 1])
        junk = sb("junk", [128, 3])
        mask_i = pT[:, :, :].rearrange("p h q -> p (h q)").bitcast(i32)
        stage = sb("stage", [128, 2, WCH])
        kraw = vec[:, 0:K_ALL]
        gl = h[:, 0:12 * B * E].rearrange("p (k j) -> p k j", j=B * E)
        wc_raw = pT[:, :, :].rearrange("p h q -> p (h q)")
        stage_b = stage[:, :, :].rearrange("p a w -> p (a w)").bitcast(bf16)
        wc_hi, wc_lo = stage_b[:, 0:W_CAUS], stage_b[:, W_CAUS:2 * W_CAUS]
        vc = stage[:, :, :].rearrange("p a w -> p (a w)")[:, W_CAUS:W_CAUS + 4 * D]
        tstage = vec[:, R_STAGE:R_STAGE + 2 * TCH].rearrange("p (a w) -> p a w", a=2)
        tvec = vec[:, R_TVEC:R_TVEC + U_ALL]
        acc, fin = x1b, x1
        comb = vec[:, R_COMB:R_COMB + MT * 3 * D]
        row_i = vec[:, R_ROWI:R_ROWI + 2 * M].rearrange("p (a m) -> p a m", a=2).bitcast(i32)
        row_f = vec[:, R_ROWF:R_ROWF + 2 * M].rearrange("p (a m) -> p a m", a=2)
        finD = vec[:, R_FIN:R_FIN + MT * D]
        pos = vec[:, R_POS:R_POS + M]
        idx_i = sb("idx_i", [128, 2, MT], i32)

        def sem(name):
            return stack.enter_context(nc.semaphore(name))

        (x_in0, x_in1, ctx_in0, ctx_in1, cst_in, kst_in, mask_in, w_in0, w_in1, vec_in, b1_in, gw_in, wc_in, vc_in,
         tvec_in) = (sem(n) for n in (
             "x_in0", "x_in1", "ctx_in0", "ctx_in1", "cst_in", "kst_in", "mask_in", "w_in0", "w_in1", "vec_in", "b1_in",
             "gw_in", "wc_in", "vc_in", "tvec_in"))
        cst_ready, ones_ready, vones_ready, b1_zero, b1_hi, b1_ready, w_hi_ready, w_lo_ready, wc_hi_ready, wc_ready = (
            sem(n) for n in ("cst_ready", "ones_ready", "vones_ready", "b1_zero", "b1_hi", "b1_ready", "w_hi_ready",
                             "w_lo_ready", "wc_hi_ready", "wc_ready"))
        (a_stats, a_var, a_veps, a_rstd, a_q, a_T, a_hi, a_split, a_s, a_m01, a_neg, a_sm, a_sn, a_max, a_bias,
         a_p, a_pT, a_pTs, a_pv, a_rsum, a_keep, a_x, a_gstats, a_gvar, a_gveps, a_grstd, a_g, a_gm, a_gmean) = (
            sem("a_" + n) for n in ("stats", "var", "veps", "rstd", "q", "T", "hi", "split", "s", "m01", "neg", "sm",
                                    "sn", "max", "bias", "p", "pT", "pTs", "pv", "rsum", "keep", "x", "gstats", "gvar",
                                    "gveps", "grstd", "g", "gm", "gmean"))
        g_prod, g_log, g_fill, g_dve, g_exp, g_ready = (
            sem("g_" + n) for n in ("prod", "log", "fill", "dve", "exp", "ready"))
        (y_stats, y_var, y_veps, y_rstd, y_ready, yT_psum, yT_hi, yT_ready) = (
            sem("y_" + n) for n in ("stats", "var", "veps", "rstd", "ready", "T_psum", "T_hi", "T_ready"))
        (qkv_psum, qk_sb, v_sb, qkT_psum, qkT_hi, qk_split, s_psum, m_max, m_hi, m_split, mT_psum, mT_sb, st_psum,
         pT_a, pT_b, oT_psum, oT_sb, o_row, o_rsum, o_sb, oo_psum, oo_hi, oo_split, proj_psum, ybo_ready) = (
            sem(n) for n in ("qkv_psum", "qk_sb", "v_sb", "qkT_psum", "qkT_hi", "qk_split", "s_psum", "m_max", "m_hi",
                             "m_split", "mT_psum", "mT_sb", "st_psum", "pT_a", "pT_b", "oT_psum", "oT_sb", "o_row",
                             "o_rsum", "o_sb", "oo_psum", "oo_hi", "oo_split", "proj_psum", "ybo_ready"))
        (res1, l1_stats, l1_var, l1_veps, l1_rstd, l1_xn, l1_g, x1_ready, x1b_ready) = (
            sem(n) for n in ("res1", "l1_stats", "l1_var", "l1_veps", "l1_rstd", "l1_xn", "l1_g", "x1_ready",
                             "x1b_ready"))
        (x1T_psum, x1T_hi, x1T_split, h_a, h_b, h_sb_a, h_sb_b, hT_a, hT_b, hh_a, hh_b, hl_a, hl_b, ff_psum,
         res2, l2_stats, l2_var, l2_veps, l2_rstd, l2_xn, l2_g, y2_ready, x_acc) = (
            sem(n) for n in ("x1T_psum", "x1T_hi", "x1T_split", "h_a", "h_b", "h_sb_a", "h_sb_b", "hT_a", "hT_b",
                             "hh_a", "hh_b", "hl_a", "hl_b", "ff_psum", "res2", "l2_stats", "l2_var", "l2_veps",
                             "l2_rstd", "l2_xn", "l2_g", "y2_ready", "x_acc"))
        c_ctx, tw_in0, tw_in1, tw_hi, tw_lo, s_comb, s_out = (
            sem("c_" + n) for n in ("ctx", "tw_in0", "tw_in1", "tw_hi", "tw_lo", "comb", "out"))
        s_stats, s_var, s_veps, s_rstd, s_y, s_yT, s_yhi, s_ysplit, s_h, s_hb, s_e, s_e1, s_r, s_a = (
            l1_stats, l1_var, l1_veps, l1_rstd, l1_xn, x1T_psum, x1T_hi, x1T_split, h_a, h_sb_a, h_b, h_sb_b, l1_g, hT_a)
        s_g, s_gst, s_gvar, s_gveps, s_grs, s_gn, s_gg, s_z, s_zT, s_zhi, s_zsplit, s_o, s_sh, s_sum = (
            hT_b, l2_stats, l2_var, l2_veps, l2_rstd, l2_xn, l2_g, y2_ready, hh_b, hh_a, hl_a, ff_psum, res2, x1_ready)
        tg_in, tb_in, idx_in, tg_hi, tg_split, d_gidx, d_sidx, d_idx, d_gather, d_chain, d_out = (
            sem("d_" + n) for n in ("tg_in", "tb_in", "idx_in", "tg_hi", "tg_split", "gidx", "sidx", "idx", "gather",
                                    "chain", "out"))
        d_yT, d_yhi, d_ysplit, d_gl, d_gb, d_ge, d_sel, d_diff, d_we, d_oT, d_oTs, d_bias, d_bias_sb, d_h = (
            a_T, a_hi, a_split, a_s, a_bias, a_p, a_max, a_keep, a_pTs, a_pT, a_m01, a_pv, a_neg, a_gm)
        d_hsel, d_e, d_var, d_veps, d_rstd, d_gn, d_gg, d_z, d_zT, d_zhi, d_zsplit, d_o, d_fin = (
            a_x, a_rsum, a_var, a_veps, a_rstd, a_q, a_g, a_sm, a_sn, a_gstats, a_gvar, a_grstd, a_gmean)
        d_y = a_gveps
        C1, D1 = UNITS + 1, B + 1

        tg = sb("tg", [128, KC, EM + 1])
        tg_h = sb("tg_h", [128, KC, EM + 1], bf16)
        tg_l = sb("tg_l", [128, KC, EM + 1], bf16)
        tb = v[0:EM, :, :].rearrange("p h k -> p (h k)")
        ids = sb("ids", [128, 10, MT])
        gidx = sb("gidx", [128, MT], i32)
        sidx = sb("sidx", [128, MT], i32)
        dg = sb("dg", [128, 10, EM + 1])
        dsm = sb("dsm", [128, 8])
        ohT = ooh[0:EM, :, :].rearrange("p c k -> p (c k)").bitcast(f32)
        bsel = qk
        hsel = o
        de = y2

        ident = cst[:, C_ID:C_ID + 128]
        mask_eo = [cst[:, C_ME:C_ME + 1], cst[:, C_MO:C_MO + 1]]
        att = ps[:, 0:4, :].rearrange("p g (s k) -> p g s k", k=128)

        selb = kst[:, K_SEL:K_SEL + 512].rearrange("p (s k) -> p s k", k=128)
        causb = kst[:, K_CS:K_CS + 256].rearrange("p (s k) -> p s k", k=128)
        halves = cst[:, C_HALF:C_HALF + 1]

        def head(g, c, s):
            return 8 * c + 2 * g + s

        b1f = [v[0:E, :, :].rearrange("p h k -> p (h k)"), qk[0:E, :]]
        ya, ta, tb2 = (y, y2), (t1, o), (t2, ybo)
        yca_hi, yca_lo = (ycT_hi, hh), (ycT_lo, hl)

        block = stack.enter_context(nc.Block())

        @block.sync
        def _(sp):
            sp.dma_start(x[:, 0:2 * D], x_d[:, 0:2 * D]).then_inc(x_in0, 16)
            sp.dma_start(cst[:, :], cst_d).then_inc(cst_in, 16)
            sp.dma_start(ctxb[:, 0, :], ctx_d[:, 0:D]).then_inc(ctx_in0, 16)
            sp.dma_start(ctxb[:, 1, :], ctx_d[:, D:2 * D]).then_inc(ctx_in1, 16)
            sp.dma_start(kraw, kst_d).then_inc(kst_in, 16)
            sp.dma_start(mask_i, mask_d.broadcast_to([128, B * S])).then_inc(mask_in, 16)
            sp.dma_start(stage[:, 0, :], w_d[:, 0:WCH]).then_inc(w_in0, 16)
            sp.dma_start(stage[:, 1, :], w_d[:, WCH:2 * WCH]).then_inc(w_in1, 16)
            sp.dma_start(x[:, 2 * D:], x_d[:, 2 * D:]).then_inc(x_in1, 16)
            sp.dma_start(gw[:, :, :], gw_d).then_inc(gw_in, 16)
            sp.dma_start(gate_b[:, :], gb_d.broadcast_to([128, E])).then_inc(gw_in, 16)
            for half in range(2):
                sp.dma_start(b1f[half], b1_d[:, 512 * half:512 * half + 512]).then_inc(b1_in, 16)
            sp.wait_ge(cst_ready, 1)
            for e in range(E):
                sp.dma_start(vec[:, e * V_EXP:(e + 1) * V_EXP],
                             vec_d[:, e * V_EXP:(e + 1) * V_EXP].broadcast_to([128, V_EXP])).then_inc(vec_in, 16)
            with sp.Fori(0, B // 2 - 1) as i:
                for j in range(2):
                    sp.wait_ge(w_lo_ready, i * 2 + (j + 1))
                    sp.dma_start(stage[:, j, :], w_d[:, ds(i * (2 * WCH) + (2 + j) * WCH, WCH)]).then_inc(
                        w_in1 if j else w_in0, 16)
                for j in range(2):
                    sp.wait_ge(a_x, i * 2 + (j + 1))
                    sp.dma_start(ctxb[:, j, :], ctx_d[:, ds(i * (2 * D) + (2 + j) * D, D)]).then_inc(
                        ctx_in1 if j else ctx_in0, 16)
            sp.wait_ge(a_neg, B)
            sp.dma_start(wc_raw, wc_d).then_inc(wc_in, 16)
            sp.wait_ge(w_lo_ready, B)
            sp.dma_start(vc, vc_d.broadcast_to([128, 4 * D])).then_inc(vc_in, 16)
            sp.wait_ge(a_x, B)
            sp.dma_start(ctxb[:, 0, :], ctx_d[:, 0:D]).then_inc(c_ctx, 16)
            sp.wait_ge(x_acc, UNITS)
            sp.dma_start(tstage[:, 0, :], tw_d[:, 0:TCH]).then_inc(tw_in0, 16)
            sp.dma_start(tstage[:, 1, :], tw_d[:, TCH:2 * TCH]).then_inc(tw_in1, 16)
            sp.dma_start(tvec, tvec_d.broadcast_to([128, U_ALL])).then_inc(tvec_in, 16)
            sp.dma_start(tg[:, :, :], tg_d).then_inc(tg_in, 16)
            sp.dma_start(pos, pos_d.broadcast_to([128, M])).then_inc(idx_in, 16)
            sp.dma_start(idx_i[:, 0, :], ib_d).then_inc(idx_in, 16)
            sp.dma_start(idx_i[:, 1, :], it_d).then_inc(idx_in, 16)
            sp.dma_start(row_i[:, 0, :], ibr_d.broadcast_to([128, M])).then_inc(idx_in, 16)
            sp.dma_start(row_i[:, 1, :], itr_d.broadcast_to([128, M])).then_inc(idx_in, 16)
            with sp.Fori(0, B // 2 - 1) as i:
                for j in range(2):
                    sp.wait_ge(tw_lo, i * 2 + (j + 1))
                    sp.dma_start(tstage[:, j, :], tw_d[:, ds(i * (2 * TCH) + (2 + j) * TCH, TCH)]).then_inc(
                        tw_in1 if j else tw_in0, 16)

            def put(b):
                sp.wait_ge(s_y, b + C1)
                sp.dma_start(comb_d[ds(b * S, S), 0:D], x[:, ds(b * D, D)]).then_inc(s_comb, 16)
                sp.dma_start(comb_d[ds(b * S, S), D:2 * D], t2[:, :]).then_inc(s_comb, 16)
                sp.wait_ge(s_sum, b + C1)
                sp.dma_start(comb_d[ds(b * S, S), 2 * D:3 * D], acc[:, :]).then_inc(s_comb, 16)
                sp.dma_start(out[ds(b * S, S), :], fin[:, :]).then_inc(s_out, 16)

            with sp.Fori(0, B - 1) as b:
                sp.wait_ge(yT_psum, b + (B + 1))
                sp.dma_start(ctxb[:, 0, :], ctx_d[:, ds(b * D + D, D)]).then_inc(c_ctx, 16)
                put(b)
            put(B - 1)
            sp.wait_ge(oT_psum, UNITS + B)
            sp.dma_start(tb, tb_d).then_inc(tb_in, 16)
            sp.wait_ge(s_comb, 16 * 3 * B)
            sp.wait_ge(s_out, 16 * B)
            sp.wait_ge(d_out, 16 * MT)

        @block.tensor
        def _(pe):
            mm = nc.tensor.matmul

            def transposed(src, bank, c0, n):
                for j in range(n):
                    last = nc.tensor.transpose(ps[:, bank, c0 + 128 * j:c0 + 128 * (j + 1)], src(j), ident)
                return last

            def split_products(dst, lhs_hi, lhs_lo, rhs_hi, rhs_lo, chunks, first=True, final=True):
                for j in range(chunks):
                    mm(dst, lhs_hi(j), rhs_hi(j), start=(first and j == 0), stop=False)
                    mm(dst, lhs_lo(j), rhs_hi(j), start=False, stop=False)
                    last = mm(dst, lhs_hi(j), rhs_lo(j), start=False, stop=(final and j == chunks - 1))
                return last

            pe.wait_ge(cst_ready, 1)
            pe.wait_ge(ones_ready, 1)
            with pe.Fori(0, B // 2) as i:
                n = [i * 2 + (j + 1) for j in range(2)]
                for j in range(2):
                    pe.wait_ge(a_q, n[j])
                    pe.wait_ge(ctx_in1 if j else ctx_in0, i * 16 + 16)
                    transposed(lambda c: ya[j][:, 128 * c:128 * c + 128], 4 * j, 0, KC)
                    transposed(lambda c: ctxb[:, j, 128 * c:128 * c + 128], 4 * j, 256, KC).then_inc(a_T, 1)
                for j in range(2):
                    pe.wait_ge(a_split, n[j])
                    split_products(ps[:, 4 * j + 1, 0:128], lambda c: yca_hi[j][:, c, :], lambda c: yca_lo[j][:, c, :],
                                   lambda c: yca_hi[j][:, KC + c, :], lambda c: yca_lo[j][:, KC + c, :],
                                   KC).then_inc(a_s, 1)
                for j in range(2):
                    pe.wait_ge(a_p, n[j])
                    transposed(lambda c: ta[j][:, 0:128], 4 * j + 2, 0, 1).then_inc(a_pT, 1)
                for j in range(2):
                    pe.wait_ge(a_pTs, n[j])
                    mm(ps[:, 4 * j + 3, 0:D], h[:, 512 + 128 * j:640 + 128 * j], ctxb[:, j, :],
                       start=True, stop=True).then_inc(a_pv, 1)
                for j in range(2):
                    pe.wait_ge(a_g, n[j])
                    for c in range(KC):
                        last = mm(ps[:, 4 * j + 2, c:c + 1], tb2[j][:, 128 * c:128 * c + 128], ones[:, 0:1],
                                  start=True, stop=True)
                    last.then_inc(a_gm, 1)
            pe.wait_ge(g_prod, 1)
            for c in range(KC):
                last = mm(ps[:, 5, 0:B * E], ones[:, :], gprod[:, c, :, :].rearrange("p b e -> p (b e)"),
                          start=(c == 0), stop=(c == KC - 1))
            last.then_inc(g_log, 1)

            def prep(k, with_ctx):
                pe.wait_ge(y_ready, k + 1)
                last = transposed(lambda c: y[:, 128 * c:128 * c + 128], 4, 0, KC)
                if with_ctx:
                    pe.wait_ge(c_ctx, (k - (B - 1)) * 16)
                    last = transposed(lambda c: ctxb[:, 0, 128 * c:128 * c + 128], 4, 256, KC)
                last.then_inc(yT_psum, 1)

            def proj(n, k, base, waited=True):
                pe.wait_ge(yT_ready, k + 1)
                if waited:
                    pe.wait_ge(res1, n)

                def w(t, off, width):
                    return lambda c: t[:, ds(base + (W_QKV + off) + c * 3 * D, width)]
                yh, yl = (lambda c: ycT_hi[:, c, :]), (lambda c: ycT_lo[:, c, :])
                split_products(ps[:, 4, :], yh, yl, w(w_hi, 0, 2 * D), w(w_lo, 0, 2 * D), KC)
                last = split_products(ps[:, 5, 0:D], yh, yl, w(w_hi, 2 * D, D), w(w_lo, 2 * D, D), KC)
                last.then_inc(qkv_psum, 1)

            def proj_c(n, k):
                pe.wait_ge(yT_ready, k + 1)
                pe.wait_ge(res1, n)

                def w(t, off):
                    return lambda c: t[:, W_QKV + off + c * 3 * D:W_QKV + off + c * 3 * D + D]
                for bank, c0, off, src in ((4, 0, 0, 0), (4, D, D, KC), (5, 0, 2 * D, KC)):
                    last = split_products(ps[:, bank, c0:c0 + D], lambda c: ycT_hi[:, src + c, :],
                                          lambda c: ycT_lo[:, src + c, :], w(wc_hi, off), w(wc_lo, off), KC)
                last.then_inc(qkv_psum, 1)

            def qk_transposes(n):
                pe.wait_ge(qk_sb, n + 1)
                transposed(lambda c: qk[:, 128 * c:128 * c + 128], 4, 0, 2 * KC).then_inc(qkT_psum, 1)

            def scores(n, causal):
                pe.wait_ge(qkT_hi, n + 1)
                if causal:
                    for g in range(4):
                        mm(ps[:, g, :], identb[:, :], causb[:, 0:1, :].broadcast_to([128, 4, 128]),
                           start=True, stop=False)
                for c in range(KC):
                    for g in range(4):
                        r = slice(32 * g, 32 * g + 32)
                        last = mm(att[:, g, 2 * c:2 * c + 2, :], qh[r, c, :], khm[r, c, :, :],
                                  start=not causal, stop=(not causal or c == KC - 1))
                last.then_inc(s_psum, 1)

            def shift_transpose(n):
                pe.wait_ge(m_split, n + 1)
                nc.tensor.transpose(ps[:, 5, 0:64].bitcast(bf16),
                                    mtile[:, :, :, :].rearrange("p r a h -> p (r a h)"), identb[:, :]).then_inc(mT_psum, 1)

            def scores_T(n, causal):
                pe.wait_ge(qk_split, n + 1)
                pe.wait_ge(mT_sb, n + 1)
                if causal:
                    for g in range(4):
                        mm(ps[:, g, :], identb[:, :], causb[:, 1:2, :].broadcast_to([128, 4, 128]),
                           start=True, stop=False)
                for c in range(KC):
                    for s in range(2):
                        terms = ((khm, qh), (khm, ql), (klm, qh), (None, None))
                        for k, (kt, qt) in enumerate(terms):
                            for g in range(4):
                                r = slice(32 * g, 32 * g + 32)
                                lhs = selb[r, 2 * c + s, :] if kt is None else kt[r, c, s, :]
                                rhs = mT[r, :] if qt is None else qt[r, c, :]
                                stop = k == 3 and (not causal or (c == KC - 1 and s == 1))
                                last = mm(att[:, g, 2 * c + s, :], lhs, rhs, start=(not causal and k == 0), stop=stop)
                last.then_inc(st_psum, 1)

            def values(n):
                for g in range(4):
                    if g == 0:
                        pe.wait_ge(pT_a, n + 1)
                    if g == 2:
                        pe.wait_ge(pT_b, n + 1)
                    for c in range(KC):
                        for s in range(2):
                            hd = head(g, c, s)
                            a, j = hd // 4, hd % 4
                            last = mm(ps[32 * j:32 * j + 32, 4, 128 * a:128 * a + 128], v[:, hd, :],
                                      pT[:, 4 * g + 2 * c + s, :], start=True, stop=True)
                last.then_inc(oT_psum, 1)

            def o_rows(n):
                pe.wait_ge(oT_sb, n + 1)
                transposed(lambda a: oT[:, a, :], 5, 0, 4).then_inc(o_row, 1)

            def o_transposes(n):
                pe.wait_ge(o_sb, n + 1)
                transposed(lambda c: o[:, 128 * c:128 * c + 128], 4, 0, KC).then_inc(oo_psum, 1)

            def out_proj(n, base):
                pe.wait_ge(oo_split, n + 1)

                def w(t):
                    return lambda c: t[:, ds(base + W_OUT + c * D, D)]
                split_products(ps[:, 5, 0:D], lambda c: ooh[:, c, :], lambda c: ool[:, c, :], w(w_hi), w(w_lo),
                               KC).then_inc(proj_psum, 1)

            def x1_transposes(n):
                pe.wait_ge(x1_ready, n + 1)
                transposed(lambda c: x1[:, 128 * c:128 * c + 128], 6, 0, KC).then_inc(x1T_psum, 1)

            def hidden(n, half, base, e):
                if half == 0:
                    pe.wait_ge(x1T_split, n + 1)
                dst = ps[:, 6 + half, :]
                mm(dst, kst[0:64, ds(e * 128 + K_ROW, 128)], b1hl[:, 512 * half:512 * half + 512],
                   start=True, stop=False)

                def w(t):
                    return lambda c: t[:, ds(base + (W_L1 + 512 * half) + c * DFF, 512)]
                split_products(dst, lambda c: xh[:, c, :], lambda c: xl[:, c, :], w(w_hi), w(w_lo), KC,
                               first=False).then_inc(h_b if half else h_a, 1)

            def hidden_T(n, half):
                pe.wait_ge(h_sb_b if half else h_sb_a, n + 1)
                transposed(lambda j: h[:, 512 * half + 128 * j:512 * half + 128 * j + 128], 6 + half, 0,
                           4).then_inc(hT_b if half else hT_a, 1)

            def second(n, j0, j1, base):
                if j0 == 0:
                    pe.wait_ge(hl_a, n + 1)
                if j0 == 4:
                    pe.wait_ge(hl_b, n + 1)
                last = split_products(ps[:, 6, 0:D], lambda j: hh[:, j0 + j, :], lambda j: hl[:, j0 + j, :],
                                      lambda j: w_hi[:, ds(base + (W_L2 + (j0 + j) * D), D)],
                                      lambda j: w_lo[:, ds(base + (W_L2 + (j0 + j) * D), D)],
                                      j1 - j0, first=(j0 == 0), final=(j1 == FC))
                if j1 == FC:
                    last.then_inc(ff_psum, 1)

            def expert(u):
                return pe.value_load(chosen[0:1, ds(u, 1)], min_val=0, max_val=E - 1)

            def both(n, k, f, prep_next):
                en, ef = expert(n), expert(f)
                bn, bf = en * W_EXP, ef * W_EXP
                proj(n, k, bn)
                x1_transposes(f)
                qk_transposes(n)
                hidden(f, 0, bf, ef)
                scores(n, False)
                hidden(f, 1, bf, ef)
                hidden_T(f, 0)
                hidden_T(f, 1)
                shift_transpose(n)
                second(f, 0, 4, bf)
                scores_T(n, False)
                second(f, 4, 6, bf)
                values(n)
                second(f, 6, 8, bf)
                o_rows(n)
                o_transposes(n)
                out_proj(n, bn)
                if prep_next is not None:
                    prep(prep_next, False)

            pe.wait_ge(g_ready, 1)
            pe.wait_ge(w_lo_ready, B)
            pe.wait_ge(w_hi_ready, B)
            pe.wait_ge(b1_ready, 2)
            pe.wait_ge(vones_ready, 2)
            prep(0, False)
            e0 = expert(0)
            b0 = e0 * W_EXP
            proj(0, 0, b0, waited=False)
            qk_transposes(0)
            scores(0, False)
            shift_transpose(0)
            scores_T(0, False)
            values(0)
            o_rows(0)
            o_transposes(0)
            out_proj(0, b0)
            with pe.Fori(0, B - 1) as b:
                both(b * 2 + 1, b, b * 2, b + 1)
                both(b * 2 + 2, b + 1, b * 2 + 1, None)
            both(UNITS - 1, B - 1, UNITS - 2, None)
            el = expert(UNITS - 1)
            bl = el * W_EXP
            x1_transposes(UNITS - 1)
            hidden(UNITS - 1, 0, bl, el)
            hidden(UNITS - 1, 1, bl, el)
            hidden_T(UNITS - 1, 0)
            hidden_T(UNITS - 1, 1)
            second(UNITS - 1, 0, 4, bl)
            second(UNITS - 1, 4, FC, bl)

            def sh_transposes(b):
                pe.wait_ge(s_y, b + C1)
                transposed(lambda c: t2[:, 128 * c:128 * c + 128], 6, 0, KC).then_inc(s_yT, 1)

            def sh_hidden(b):
                pe.wait_ge(s_ysplit, b + C1)
                split_products(ps[:, 7, 0:2 * HM], lambda c: xh[:, c, :], lambda c: xl[:, c, :],
                               lambda c: w_hi[:, T_S12 + c * 2 * HM:T_S12 + (c + 1) * 2 * HM],
                               lambda c: w_lo[:, T_S12 + c * 2 * HM:T_S12 + (c + 1) * 2 * HM], KC).then_inc(s_h, 1)

            def sh_z(b):
                pe.wait_ge(s_z, b + C1)
                transposed(lambda c: h[:, 512:512 + HM], 6, 0, 1).then_inc(s_zT, 1)

            def sh_out(b):
                pe.wait_ge(s_zsplit, b + C1)
                split_products(ps[:, 7, 0:D], lambda c: hh[:, 0, :], lambda c: hl[:, 0, :],
                               lambda c: w_hi[:, T_S3:T_S3 + D], lambda c: w_lo[:, T_S3:T_S3 + D], 1).then_inc(s_o, 1)

            def att_c(b, beside):
                n, k = b + UNITS, b + B
                step = beside
                proj_c(n, k)
                step(sh_transposes)
                qk_transposes(n)
                scores(n, True)
                step(sh_hidden)
                shift_transpose(n)
                scores_T(n, True)
                step(sh_z)
                values(n)
                step(sh_out)
                o_rows(n)
                o_transposes(n)
                pe.wait_ge(oo_split, n + 1)

                def w(t):
                    return lambda c: t[:, W_OUT + c * D:W_OUT + (c + 1) * D]
                split_products(ps[:, 5, 0:D], lambda c: ooh[:, c, :], lambda c: ool[:, c, :], w(wc_hi), w(wc_lo),
                               KC).then_inc(proj_psum, 1)

            pe.wait_ge(wc_ready, 1)
            prep(B, True)
            att_c(0, lambda f: None)
            prep(B + 1, True)
            pe.wait_ge(tw_lo, B)
            pe.wait_ge(tw_hi, B)
            with pe.Fori(0, B - 2) as b:
                att_c(b + 1, lambda f: f(b))
                prep(b + (B + 2), True)
            att_c(B - 1, lambda f: f(B - 2))
            for f in (sh_transposes, sh_hidden, sh_z, sh_out):
                f(B - 1)

            pe.wait_ge(tg_split, 1)
            pe.wait_ge(tb_in, 16)
            with pe.Fori(0, MT) as t:
                pe.wait_ge(d_y, t + D1)
                transposed(lambda c: y[:, 128 * c:128 * c + 128], 4, 0, KC).then_inc(d_yT, 1)
                pe.wait_ge(d_ysplit, t + D1)
                split_products(ps[:, 5, 0:EM + 1], lambda c: xh[:, c, :], lambda c: xl[:, c, :],
                               lambda c: tg_h[:, c, :], lambda c: tg_l[:, c, :], KC).then_inc(d_gl, 1)
                for q in range(4):
                    last = split_products(ps[:, q, :], lambda c: xh[:, c, :], lambda c: xl[:, c, :],
                                          lambda c: w_hi[:, T_E12 + c * 2048 + 512 * q:T_E12 + c * 2048 + 512 * q + 512],
                                          lambda c: w_lo[:, T_E12 + c * 2048 + 512 * q:T_E12 + c * 2048 + 512 * q + 512], KC)
                last.then_inc(d_h, 1)
                pe.wait_ge(d_sel, t + D1)
                nc.tensor.transpose(ps[0:EM, 6, 0:128], dg[:, 7, 0:EM], ident).then_inc(d_oT, 1)
                pe.wait_ge(d_oTs, t + D1)
                mm(ps[:, 7, :], ohT, tb, start=True, stop=True).then_inc(d_bias, 1)
                pe.wait_ge(d_z, t + D1)
                transposed(lambda c: h[:, 512:512 + HM], 6, 0, 1).then_inc(d_zT, 1)
                pe.wait_ge(d_zsplit, t + D1)
                for q in range(4):
                    last = split_products(ps[:, q, :], lambda c: hh[:, 0, :], lambda c: hl[:, 0, :],
                                          lambda c: w_hi[:, T_E3 + 512 * q:T_E3 + 512 * q + 512],
                                          lambda c: w_lo[:, T_E3 + 512 * q:T_E3 + 512 * q + 512], 1)
                last.then_inc(d_o, 1)

        @block.scalar
        def _(act):
            A = nc.scalar.activation

            def copy(dst, src):
                return nc.scalar.copy(dst, src)

            act.wait_ge(cst_in, 16)
            copy(identb[:, :], ident)
            act.wait_ge(kst_in, 16)
            copy(kst[:, :], kraw).then_inc(cst_ready, 1)
            act.wait_ge(b1_zero, 1)
            act.wait_ge(b1_in, 32)
            copy(b1hl[0:E, 0:512], b1f[0])
            copy(b1hl[0:E, 512:1024], b1f[1]).then_inc(b1_hi, 1)
            with act.Fori(0, B // 2) as i:
                n = [i * 2 + (j + 1) for j in range(2)]
                for j in range(2):
                    act.wait_ge(a_T, n[j])
                    copy(yca_hi[j][:, 0:4, :], ps[:, 4 * j, :].rearrange("p (c k) -> p c k", k=128)).then_inc(a_hi, 1)
                act.wait_ge(w_in0, i * 16 + 16)
                copy(w_hi[:, ds(i * (2 * WCH), WCH)], stage[:, 0, :]).then_inc(w_hi_ready, 1)
                for j in range(2):
                    act.wait_ge(a_bias, n[j])
                    A(ta[j][:, 0:128], ta[j][:, 128:256], ACT.Exp, bias=mx[:, 8 * j + 1:8 * j + 2], scale=SCALE_A,
                      accum_out=mx[:, 8 * j + 2:8 * j + 3]).then_inc(a_p, 1)
                for j in range(2):
                    act.wait_ge(a_pT, n[j])
                    copy(h[:, 512 + 128 * j:640 + 128 * j], ps[:, 4 * j + 2, 0:128]).then_inc(a_pTs, 1)
                act.wait_ge(w_in1, i * 16 + 16)
                copy(w_hi[:, ds(i * (2 * WCH) + WCH, WCH)], stage[:, 1, :]).then_inc(w_hi_ready, 1)
            act.wait_ge(wc_in, 16)
            act.wait_ge(w_lo_ready, B)
            copy(wc_hi, wc_raw).then_inc(wc_hi_ready, 1)
            act.wait_ge(g_dve, 2)
            A(gl[:, 2, :], gl[:, 1, :], ACT.Exp).then_inc(g_exp, 1)

            def prep(k, n):
                act.wait_ge(yT_psum, k + 1)
                copy(ycT_hi[:, 0:n, :], ps[:, 4, 0:128 * n].rearrange("p (c k) -> p c k", k=128)).then_inc(yT_hi, 1)

            def qk_hi(n):
                act.wait_ge(qkT_psum, n + 1)
                copy(qh[:, :, :], ps[:, 4, 0:D].rearrange("p (c k) -> p c k", k=128))
                kk = ps[:, 4, D:2 * D].rearrange("p (c k) -> p c k", k=128)
                for s in range(2):
                    last = A(khm[:, :, s, :], kk, ACT.Copy, scale=mask_eo[s])
                last.then_inc(qkT_hi, 1)

            def shift(n):
                act.wait_ge(mT_psum, n + 1)
                copy(mT[:, :], ps[:, 5, 0:64].bitcast(bf16)).then_inc(mT_sb, 1)

            def exps(n):
                act.wait_ge(st_psum, n + 1)
                for a, done in ((0, pT_a), (1, pT_b)):
                    A(pT[:, 8 * a:8 * a + 8, :].rearrange("p h q -> p (h q)"),
                      ps[:, 2 * a:2 * a + 2, :].rearrange("p g k -> p (g k)"), ACT.Exp, scale=SCALE_H).then_inc(done, 1)

            def o_evict(n):
                act.wait_ge(oT_psum, n + 1)
                copy(oT[:, :, :], ps[:, 4, :].rearrange("p (a q) -> p a q", q=128)).then_inc(oT_sb, 1)

            def oo(n):
                act.wait_ge(oo_psum, n + 1)
                copy(ooh[:, :, :], ps[:, 4, 0:D].rearrange("p (c k) -> p c k", k=128)).then_inc(oo_hi, 1)

            def x1_hi(n):
                act.wait_ge(x1T_psum, n + 1)
                copy(xh[:, :, :], ps[:, 6, 0:D].rearrange("p (c k) -> p c k", k=128)).then_inc(x1T_hi, 1)

            def relu(n, half):
                act.wait_ge(h_b if half else h_a, n + 1)
                A(h[:, 512 * half:512 * half + 512], ps[:, 6 + half, :], ACT.Relu).then_inc(h_sb_b if half else h_sb_a, 1)

            def h_hi(n, half):
                act.wait_ge(hT_b if half else hT_a, n + 1)
                copy(hh[:, 4 * half:4 * half + 4, :], ps[:, 6 + half, :].rearrange("p (c k) -> p c k", k=128)).then_inc(
                    hh_b if half else hh_a, 1)

            def both(n, f, prep_next):
                x1_hi(f)
                qk_hi(n)
                relu(f, 0)
                relu(f, 1)
                h_hi(f, 0)
                h_hi(f, 1)
                shift(n)
                exps(n)
                o_evict(n)
                oo(n)
                if prep_next is not None:
                    prep(prep_next, KC)

            prep(0, KC)
            qk_hi(0)
            shift(0)
            exps(0)
            o_evict(0)
            oo(0)
            with act.Fori(0, B - 1) as b:
                both(b * 2 + 1, b * 2, b + 1)
                both(b * 2 + 2, b * 2 + 1, None)
            both(UNITS - 1, UNITS - 2, None)
            x1_hi(UNITS - 1)
            relu(UNITS - 1, 0)
            relu(UNITS - 1, 1)
            h_hi(UNITS - 1, 0)
            h_hi(UNITS - 1, 1)

            def tw(i):
                for j in range(2):
                    act.wait_ge(tw_in1 if j else tw_in0, i * 16 + 16)
                    copy(w_hi[:, ds(i * (2 * TCH) + j * TCH, TCH)], tstage[:, j, :]).then_inc(tw_hi, 1)

            def sh_y(b):
                act.wait_ge(s_yT, b + C1)
                copy(xh[:, :, :], ps[:, 6, 0:D].rearrange("p (c k) -> p c k", k=128)).then_inc(s_yhi, 1)

            def sh_e(b):
                act.wait_ge(s_hb, b + C1)
                A(de[:, 0:HM], h[:, 0:HM], ACT.Exp, scale=-1.0).then_inc(s_e, 1)

            def sh_zhi(b):
                act.wait_ge(s_zT, b + C1)
                copy(hh[:, 0, :], ps[:, 6, 0:128]).then_inc(s_zhi, 1)

            def att_c(b, beside):
                n = b + UNITS
                beside(sh_y)
                qk_hi(n)
                beside(sh_e)
                shift(n)
                exps(n)
                beside(sh_zhi)
                o_evict(n)
                oo(n)

            act.wait_ge(ff_psum, UNITS)
            with act.Fori(0, B // 2) as i:
                tw(i)
            prep(B, 2 * KC)
            att_c(0, lambda f: None)
            prep(B + 1, 2 * KC)
            with act.Fori(0, B - 2) as b:
                att_c(b + 1, lambda f: f(b))
                prep(b + (B + 2), 2 * KC)
            att_c(B - 1, lambda f: f(B - 2))
            for f in (sh_y, sh_e, sh_zhi):
                f(B - 1)

            act.wait_ge(tg_in, 16)
            copy(tg_h[:, :, :], tg[:, :, :]).then_inc(tg_hi, 1)
            act.wait_ge(d_gather, 16 * MT)
            with act.Fori(0, MT) as t:
                copy(y[:, :], comb[:, ds(t * (3 * D) + D, D)]).then_inc(d_y, 1)
                act.wait_ge(d_yT, t + D1)
                copy(xh[:, :, :], ps[:, 4, 0:D].rearrange("p (c k) -> p c k", k=128)).then_inc(d_yhi, 1)
                act.wait_ge(d_gb, t + D1)
                A(dg[:, 1, :], dg[:, 0, :], ACT.Exp, scale=-1.0).then_inc(d_ge, 1)
                act.wait_ge(d_oT, t + D1)
                copy(ohT, ps[0:EM, 6, 0:128]).then_inc(d_oTs, 1)
                act.wait_ge(d_bias, t + D1)
                copy(bsel[:, :], ps[:, 7, :]).then_inc(d_bias_sb, 1)
                act.wait_ge(d_diff, t + D1)
                A(dsm[:, 4:5], dsm[:, 3:4], ACT.Exp, scale=-1.0).then_inc(d_we, 1)
                act.wait_ge(d_hsel, t + D1)
                A(de[:, 0:HM], hsel[:, 0:HM], ACT.Exp, scale=-1.0).then_inc(d_e, 1)
                act.wait_ge(d_zT, t + D1)
                copy(hh[:, 0, :], ps[:, 6, 0:128]).then_inc(d_zhi, 1)

        @block.vector
        def _(dve):
            tt, ts, stt, cp = (nc.vector.tensor_tensor, nc.vector.tensor_scalar, nc.vector.scalar_tensor_tensor,
                               nc.vector.tensor_copy)

            def stats(src, i, n, done_stats, done_var):
                nc.vector.memset(junk[:, 0:1], 0.0)
                nc.vector.bn_stats(st[:, i, :], src).then_inc(done_stats, 1)
                dve.wait_ge(done_stats, n + 1)
                nc.vector.memset(junk[:, 1:2], 0.0)
                nc.vector.bn_aggr(mv[:, i, :], st[:, i, :]).then_inc(done_var, 1)

            def normalized(dst, src, i):
                return ts(dst, src, mv[:, i, 0:1], rs[:, i, :], ALU.subtract, ALU.mult)

            nc.vector.memset(ones[:, :], 1.0).then_inc(ones_ready, 1)
            nc.vector.memset(b1hl[:, :], 0.0).then_inc(b1_zero, 1)
            dve.wait_ge(b1_hi, 1)
            for half in range(2):
                tt(b1hl[32:32 + E, 512 * half:512 * half + 512], b1f[half], b1hl[0:E, 512 * half:512 * half + 512],
                   ALU.subtract).then_inc(b1_ready, 1)
            dve.wait_ge(b1_ready, 2)
            nc.vector.memset(v[:, :, :], 0.0).then_inc(vones_ready, 1)
            dve.wait_ge(vones_ready, 1)
            nc.vector.memset(v[:, :, HD:HD + 1], 1.0).then_inc(vones_ready, 1)

            dve.wait_ge(mask_in, 16)
            dve.wait_ge(x_in0, 16)
            dve.wait_ge(x_in1, 16)
            with dve.Fori(0, B // 2) as i:
                n = [i * 2 + (j + 1) for j in range(2)]
                xb = [x[:, ds(i * (2 * D) + j * D, D)] for j in range(2)]
                for j in range(2):
                    stats(xb[j], j, i * 2 + j, a_stats, a_var)
                for j in range(2):
                    m01, neg = h[:, 256 * j:256 * j + S], h[:, 256 * j + S:256 * j + 2 * S]
                    mi = mask_i[:, ds(i * (2 * S) + j * S, S)]
                    ts(m01, mi, 0.0, None, ALU.not_equal).then_inc(a_m01, 1)
                    dve.wait_ge(a_m01, n[j])
                    ts(neg, m01, 1.0, -NEG / SCALE_A, ALU.subtract, ALU.mult).then_inc(a_neg, 1)
                for j in range(2):
                    dve.wait_ge(a_rstd, n[j])
                    normalized(ya[j][:, :], xb[j], j).then_inc(a_q, 1)
                for j in range(2):
                    dve.wait_ge(a_hi, n[j])
                    tt(yca_lo[j][:, 0:4, :], ps[:, 4 * j, :].rearrange("p (c k) -> p c k", k=128),
                       yca_hi[j][:, 0:4, :], ALU.subtract).then_inc(a_split, 1)
                for j in range(2):
                    dve.wait_ge(a_s, n[j])
                    dve.wait_ge(a_neg, n[j])
                    tt(tb2[j][:, 0:S], ps[:, 4 * j + 1, 0:S], h[:, 256 * j:256 * j + S], ALU.mult).then_inc(a_sm, 1)
                for j in range(2):
                    dve.wait_ge(a_sm, n[j])
                    tt(ta[j][:, 128:256], tb2[j][:, 0:S], h[:, 256 * j + S:256 * j + 2 * S], ALU.add).then_inc(a_sn, 1)
                for j in range(2):
                    dve.wait_ge(a_sn, n[j])
                    nc.vector.tensor_reduce(mx[:, 8 * j:8 * j + 1], ta[j][:, 128:256], AX.X, ALU.max).then_inc(a_max, 1)
                for j in range(2):
                    dve.wait_ge(a_max, n[j])
                    ts(mx[:, 8 * j + 1:8 * j + 2], mx[:, 8 * j:8 * j + 1], -SCALE_A, None, ALU.mult).then_inc(a_bias, 1)
                for j in range(2):
                    dve.wait_ge(a_p, n[j])
                    nc.vector.reciprocal(mx[:, 8 * j + 3:8 * j + 4], mx[:, 8 * j + 2:8 * j + 3]).then_inc(a_rsum, 1)
                for j in range(2):
                    dve.wait_ge(a_rsum, n[j])
                    ts(mx[:, 8 * j + 4:8 * j + 5], mx[:, 8 * j + 3:8 * j + 4], KEEP, None, ALU.mult).then_inc(a_keep, 1)
                for j in range(2):
                    dve.wait_ge(a_keep, n[j])
                    dve.wait_ge(a_pv, n[j])
                    stt(xb[j], ps[:, 4 * j + 3, 0:D], mx[:, 8 * j + 4:8 * j + 5], xb[j], ALU.mult, ALU.add).then_inc(a_x, 1)
                for j in range(2):
                    dve.wait_ge(a_x, n[j])
                    stats(xb[j], 2 + j, i * 2 + j, a_gstats, a_gvar)
                for j in range(2):
                    dve.wait_ge(a_grstd, n[j])
                    normalized(tb2[j][:, :], xb[j], 2 + j).then_inc(a_g, 1)
                for j in range(2):
                    dve.wait_ge(a_gm, n[j])
                    ts(gmean[:, :, ds(i * 2 + j, 1)], ps[:, 4 * j + 2, 0:KC].rearrange("p (c o) -> p c o", o=1), 1.0 / S,
                       None, ALU.mult).then_inc(a_gmean, 1)

            count = [0]

            def g_link(ins):
                count[0] += 1
                ins.then_inc(g_dve, 1)
                dve.wait_ge(g_dve, count[0])
            dve.wait_ge(gw_in, 32)
            dve.wait_ge(a_gmean, B)
            for c in range(KC):
                last = tt(gprod[:, c, :, :], gmean[:, c, :].rearrange("p (b o) -> p b o", o=1).broadcast_to([128, B, E]),
                          gw[:, c:c + 1, :].broadcast_to([128, B, E]), ALU.mult)
            last.then_inc(g_prod, 1)
            dve.wait_ge(g_log, 1)

            def be(k):
                return gl[:, k, :].rearrange("p (b e) -> p b e", e=E)

            def per_b(k):
                return gs[:, k, :].rearrange("p (b o) -> p b o", o=1).broadcast_to([128, B, E])

            def const_e(c0):
                return cst[:, c0:c0 + E].rearrange("p (o e) -> p o e", o=1).broadcast_to([128, B, E])
            gb = gate_b[:, :].rearrange("p (o e) -> p o e", o=1).broadcast_to([128, B, E])
            nc.vector.tensor_tensor(be(0), ps[:, 5, 0:B * E].rearrange("p (b e) -> p b e", e=E), gb, ALU.add).then_inc(g_fill, 1)
            dve.wait_ge(g_fill, 1)
            g_link(nc.vector.tensor_reduce(gs[:, 0, :], be(0), AX.X, ALU.max))
            g_link(tt(be(1), be(0), per_b(0), ALU.subtract))
            g_link(tt(be(3), be(0), per_b(0), ALU.is_equal))
            g_link(tt(be(4), be(3), const_e(C_RNK4), ALU.mult))
            g_link(nc.vector.tensor_reduce(gs[:, 1, :], be(4), AX.X, ALU.max))
            g_link(tt(be(5), be(4), per_b(1), ALU.is_equal))
            g_link(ts(be(6), be(5), -3.0e38, None, ALU.mult))
            g_link(ts(be(7), be(5), -1.0, 1.0, ALU.mult, ALU.add))
            g_link(tt(be(8), be(0), be(7), ALU.mult))
            g_link(tt(be(8), be(8), be(6), ALU.add))
            g_link(nc.vector.tensor_reduce(gs[:, 2, :], be(8), AX.X, ALU.max))
            g_link(tt(be(3), be(8), per_b(2), ALU.is_equal))
            g_link(tt(be(4), be(3), const_e(C_RNK4), ALU.mult))
            g_link(nc.vector.tensor_reduce(gs[:, 3, :], be(4), AX.X, ALU.max))
            g_link(tt(be(9), be(4), per_b(3), ALU.is_equal))
            dve.wait_ge(g_exp, 1)
            g_link(nc.vector.tensor_reduce(gs[:, 4, :], be(2), AX.X, ALU.add))
            g_link(nc.vector.reciprocal(gs[:, 5, :], gs[:, 4, :]))
            g_link(tt(be(10), be(2), per_b(5), ALU.mult))
            slots = gate_w[:, :].rearrange("p (b s) -> p b s", s=TOPK)
            picks = chosen[:, :].rearrange("p (b s) -> p b s", s=TOPK)
            for s, k in ((0, 5), (1, 9)):
                g_link(tt(be(11), be(10), be(k), ALU.mult))
                g_link(nc.vector.tensor_reduce(slots[:, :, s], be(11), AX.X, ALU.add))
                g_link(tt(be(11), be(k), const_e(C_ID4), ALU.mult))
                g_link(nc.vector.tensor_reduce(gs[:, 6 + s, :], be(11), AX.X, ALU.add))
                g_link(cp(picks[:, :, s], gs[:, 6 + s, :]))
            dve.wait_ge(vec_in, 16 * E)
            nc.vector.memset(dsm[:, 7:8], 0.0).then_inc(g_ready, 1)

            def y_of(xb, k, ready):
                stats(xb, 0, k, y_stats, y_var)
                dve.wait_ge(y_rstd, k + 1)
                dve.wait_ge(ybo_ready, ready)
                normalized(y[:, :], xb, 0).then_inc(y_ready, 1)

            def y_low(k, n):
                dve.wait_ge(yT_hi, k + 1)
                tt(ycT_lo[:, 0:n, :], ps[:, 4, 0:128 * n].rearrange("p (c k) -> p c k", k=128), ycT_hi[:, 0:n, :],
                   ALU.subtract).then_inc(yT_ready, 1)

            def add_bias(n, t, base):
                dve.wait_ge(qkv_psum, n + 1)
                tt(qk[:, :], ps[:, 4, :], t[:, ds(base + V_QKV, 2 * D)], ALU.add).then_inc(qk_sb, 1)
                tt(v[:, :, 0:HD], ps[:, 5, 0:D].rearrange("p (h d) -> p h d", d=HD),
                   t[:, ds(base + (V_QKV + 2 * D), D)].rearrange("p (h d) -> p h d", d=HD), ALU.add).then_inc(v_sb, 1)

            def qk_low(n):
                dve.wait_ge(qkT_hi, n + 1)
                tt(ql[:, :, :], ps[:, 4, 0:D].rearrange("p (c k) -> p c k", k=128), qh[:, :, :], ALU.subtract)
                kk = ps[:, 4, D:2 * D].rearrange("p (c k) -> p c k", k=128)
                for s in range(2):
                    last = stt(klm[:, :, s, :], kk, mask_eo[s], khm[:, :, s, :], ALU.mult, ALU.subtract)
                last.then_inc(qk_split, 1)

            def maxima(n):
                dve.wait_ge(s_psum, n + 1)
                nc.vector.tensor_reduce(mx[:, :], att.rearrange("p g s k -> p (g s) k"), AX.X, ALU.max,
                                        negate=True).then_inc(m_max, 1)
                dve.wait_ge(m_max, n + 1)
                many = mx[:, :].rearrange("p (o h) -> p o h", o=1).broadcast_to([128, 4, H])
                cp(mtile[:, :, 0, :], many).then_inc(m_hi, 1)
                dve.wait_ge(m_hi, n + 1)
                tt(mtile[:, :, 1, :], many, mtile[:, :, 0, :], ALU.subtract).then_inc(m_split, 1)

            def o_norm(n):
                dve.wait_ge(o_row, n + 1)
                rows = ps[:, 5, :].rearrange("p (h k) -> p h k", k=32)
                nc.vector.reciprocal(o_rs[:, :].rearrange("p (h o) -> p h o", o=1), rows[:, :, HD:HD + 1]).then_inc(o_rsum, 1)
                dve.wait_ge(o_rsum, n + 1)
                tt(o[:, :].rearrange("p (h d) -> p h d", d=HD), rows[:, :, 0:HD],
                   o_rs[:, :].rearrange("p (h o) -> p h o", o=1).broadcast_to([128, H, HD]), ALU.mult).then_inc(o_sb, 1)

            def o_low(n):
                dve.wait_ge(oo_hi, n + 1)
                tt(ool[:, :, :], ps[:, 4, 0:D].rearrange("p (c k) -> p c k", k=128), ooh[:, :, :],
                   ALU.subtract).then_inc(oo_split, 1)

            def norm1(n):
                dve.wait_ge(proj_psum, n + 1)
                dve.wait_ge(ybo_ready, n + 1)
                tt(t1[:, :], ps[:, 5, 0:D], ybo[:, :], ALU.add).then_inc(res1, 1)
                dve.wait_ge(res1, n + 1)
                stats(t1[:, :], 1, n, l1_stats, l1_var)
                dve.wait_ge(l1_rstd, n + 1)
                normalized(x1[:, :], t1[:, :], 1).then_inc(l1_xn, 1)

            def x1_low(n):
                dve.wait_ge(x1T_hi, n + 1)
                tt(xl[:, :, :], ps[:, 6, 0:D].rearrange("p (c k) -> p c k", k=128), xh[:, :, :],
                   ALU.subtract).then_inc(x1T_split, 1)

            def h_low(n, half):
                dve.wait_ge(hh_b if half else hh_a, n + 1)
                tt(hl[:, 4 * half:4 * half + 4, :], ps[:, 6 + half, :].rearrange("p (c k) -> p c k", k=128),
                   hh[:, 4 * half:4 * half + 4, :], ALU.subtract).then_inc(hl_b if half else hl_a, 1)

            def norm2(n):
                dve.wait_ge(ff_psum, n + 1)
                dve.wait_ge(x1b_ready, n + 1)
                tt(t2[:, :], ps[:, 6, 0:D], x1b[:, :], ALU.add).then_inc(res2, 1)
                dve.wait_ge(res2, n + 1)
                stats(t2[:, :], 2, n, l2_stats, l2_var)
                dve.wait_ge(l2_rstd, n + 1)
                normalized(y2[:, :], t2[:, :], 2).then_inc(l2_xn, 1)

            def add_expert(n, xb):
                dve.wait_ge(y2_ready, n + 1)
                stt(xb, y2[:, :], gate_w[:, ds(n, 1)], xb, ALU.mult, ALU.add).then_inc(x_acc, 1)

            def expert(u):
                return dve.value_load(chosen[0:1, ds(u, 1)], min_val=0, max_val=E - 1)

            def at(b):
                return x[:, ds(b * D, D)]

            def both(n, f, xf, k_next, x_next):
                bias = expert(n) * V_EXP
                add_bias(n, vec, bias)
                x1_low(f)
                qk_low(n)
                maxima(n)
                h_low(f, 0)
                h_low(f, 1)
                if k_next is not None:
                    y_of(x_next, k_next, n + 1)
                norm2(f)
                o_norm(n)
                add_expert(f, xf)
                o_low(n)
                norm1(n)
                if k_next is not None:
                    y_low(k_next, KC)

            stats(at(0), 0, 0, y_stats, y_var)
            dve.wait_ge(y_rstd, 1)
            normalized(y[:, :], at(0), 0).then_inc(y_ready, 1)
            y_low(0, KC)
            add_bias(0, vec, expert(0) * V_EXP)
            qk_low(0)
            maxima(0)
            o_norm(0)
            o_low(0)
            norm1(0)
            with dve.Fori(0, B - 1) as b:
                both(b * 2 + 1, b * 2, at(b), b + 1, at(b + 1))
                both(b * 2 + 2, b * 2 + 1, at(b), None, None)
            both(UNITS - 1, UNITS - 2, at(B - 1), None, None)
            x1_low(UNITS - 1)
            h_low(UNITS - 1, 0)
            h_low(UNITS - 1, 1)
            norm2(UNITS - 1)
            add_expert(UNITS - 1, at(B - 1))

            def x3(n, b):
                dve.wait_ge(proj_psum, n + 1)
                dve.wait_ge(ybo_ready, n + 1)
                tt(at(b), ps[:, 5, 0:D], ybo[:, :], ALU.add).then_inc(res1, 1)

            def sh_y(b):
                dve.wait_ge(res1, b + (UNITS + 1))
                stats(at(b), 1, b + UNITS, s_stats, s_var)
                dve.wait_ge(s_rstd, b + C1)
                if not isinstance(b, int) or b > 0:
                    dve.wait_ge(s_comb, b * 48)
                normalized(t2[:, :], at(b), 1).then_inc(s_y, 1)

            def sh_low(b):
                dve.wait_ge(s_yhi, b + C1)
                tt(xl[:, :, :], ps[:, 6, 0:D].rearrange("p (c k) -> p c k", k=128), xh[:, :, :],
                   ALU.subtract).then_inc(s_ysplit, 1)

            def sh_bias(b):
                dve.wait_ge(s_h, b + C1)
                tt(h[:, 0:2 * HM], ps[:, 7, 0:2 * HM], tvec[:, U_S12:U_S12 + 2 * HM], ALU.add).then_inc(s_hb, 1)

            def sh_gated(b):
                dve.wait_ge(s_e, b + C1)
                ts(de[:, HM:2 * HM], de[:, 0:HM], 1.0, None, ALU.add).then_inc(s_e1, 1)
                dve.wait_ge(s_e1, b + C1)
                nc.vector.reciprocal(de[:, 0:HM], de[:, HM:2 * HM]).then_inc(s_r, 1)
                dve.wait_ge(s_r, b + C1)
                tt(h[:, 2 * HM:3 * HM], h[:, 0:HM], de[:, 0:HM], ALU.mult).then_inc(s_a, 1)
                dve.wait_ge(s_a, b + C1)
                tt(h[:, 3 * HM:4 * HM], h[:, 2 * HM:3 * HM], h[:, HM:2 * HM], ALU.mult).then_inc(s_g, 1)
                dve.wait_ge(s_g, b + C1)
                stats(h[:, 3 * HM:4 * HM], 2, b + UNITS, s_gst, s_gvar)
                dve.wait_ge(s_grs, b + C1)
                normalized(h[:, 2 * HM:3 * HM], h[:, 3 * HM:4 * HM], 2).then_inc(s_gn, 1)

            def sh_zlow(b):
                dve.wait_ge(s_zhi, b + C1)
                tt(hl[:, 0, :], ps[:, 6, 0:HM], hh[:, 0, :], ALU.subtract).then_inc(s_zsplit, 1)

            def sh_sum(b):
                dve.wait_ge(s_o, b + C1)
                if not isinstance(b, int) or b > 0:
                    dve.wait_ge(s_out, b * 16)
                tt(acc[:, :], ps[:, 7, 0:D], tvec[:, U_S3:U_S3 + D], ALU.add).then_inc(s_sh, 1)
                dve.wait_ge(s_sh, b + C1)
                tt(fin[:, :], acc[:, :], at(b), ALU.add).then_inc(s_sum, 1)

            def att_c(b, beside):
                n = b + UNITS
                add_bias(n, vc, 0)
                beside(sh_low)
                qk_low(n)
                beside(sh_bias)
                maxima(n)
                beside(sh_gated)
                beside(sh_zlow)
                o_norm(n)
                beside(sh_sum)
                o_low(n)
                x3(n, b)
                sh_y(b)

            def y_c(b):
                y_of(at(b), b + B, b + UNITS)
                y_low(b + B, 2 * KC)

            dve.wait_ge(x_acc, UNITS)
            dve.wait_ge(vc_in, 16)
            y_c(0)
            att_c(0, lambda f: None)
            y_c(1)
            dve.wait_ge(tvec_in, 16)
            att_c(1, lambda f: f(0))
            y_c(2)
            with dve.Fori(1, B - 2) as b:
                att_c(b + 1, lambda f: f(b))
                y_c(b + 2)
            att_c(B - 1, lambda f: f(B - 2))
            for f in (sh_low, sh_bias, sh_gated, sh_zlow, sh_sum):
                f(B - 1)

            links = [0]

            def i_link(ins):
                links[0] += 1
                ins.then_inc(d_idx, 1)
                dve.wait_ge(d_idx, links[0])

            def rows_of(src_b, src_t, fb, ft, tmp, flat, key):
                for src, f, size in ((src_b, fb, B), (src_t, ft, S)):
                    i_link(cp(f, src))
                    i_link(ts(tmp, f, 0.0, float(size), ALU.is_lt, ALU.mult))
                    i_link(tt(f, f, tmp, ALU.add))
                i_link(ts(tmp, fb, 0.0, None, ALU.is_lt))
                i_link(ts(flat, fb, float(B - 1), None, ALU.is_gt))
                i_link(tt(tmp, tmp, flat, ALU.add))
                i_link(ts(flat, ft, 0.0, None, ALU.is_lt))
                i_link(tt(tmp, tmp, flat, ALU.add))
                i_link(ts(flat, ft, float(S - 1), None, ALU.is_gt))
                i_link(tt(tmp, tmp, flat, ALU.add))
                i_link(ts(key, tmp, float(4 * B * S), None, ALU.mult))
                i_link(ts(fb, fb, 0.0, float(B - 1), ALU.max, ALU.min))
                i_link(ts(ft, ft, 0.0, float(S - 1), ALU.max, ALU.min))
                i_link(ts(fb, fb, float(S), None, ALU.mult))
                i_link(tt(flat, fb, ft, ALU.add))
                i_link(tt(key, key, flat, ALU.add))

            dve.wait_ge(idx_in, 16 * 5)
            rows_of(idx_i[:, 0, :], idx_i[:, 1, :], ids[:, 0, :], ids[:, 1, :], ids[:, 2, :], ids[:, 3, :], ids[:, 4, :])
            i_link(cp(gidx[:, :], ids[:, 3, :]))
            nc.vector.memset(dsm[:, 6:7], 0.0).then_inc(d_gidx, 1)
            rows_of(row_i[:, 0, :], row_i[:, 1, :], row_f[:, 0, :], row_f[:, 1, :], h[:, 0:M], h[:, M:2 * M], pT[:, 0:4, :].rearrange("p h q -> p (h q)"))
            for t in range(MT):
                i_link(stt(h[:, 0:M], pT[:, 0:4, :].rearrange("p h q -> p (h q)"), ids[:, 4, t:t + 1], pos, ALU.is_equal,
                           ALU.mult))
                i_link(nc.vector.tensor_reduce(ids[:, 5, t:t + 1], h[:, 0:M], AX.X, ALU.max))
            i_link(tt(ids[:, 6, :], ids[:, 5, :], cst[:, C_M:C_M + MT], ALU.is_gt))
            i_link(ts(ids[:, 7, :], ids[:, 6, :], float(4 * B * S), None, ALU.mult))
            i_link(tt(ids[:, 8, :], ids[:, 7, :], ids[:, 4, :], ALU.add))
            i_link(cp(sidx[:, :], ids[:, 8, :]))
            nc.vector.memset(dsm[:, 6:7], 0.0).then_inc(d_sidx, 1)
            dve.wait_ge(tg_hi, 1)
            tt(tg_l[:, :, :], tg[:, :, :], tg_h[:, :, :], ALU.subtract).then_inc(tg_split, 1)

            CHAIN = 3 + 4 + 2 + 3 + (EM - 1) + 5 + EM + 2
            with dve.Fori(0, MT) as t:
                step = [0]

                def link(ins):
                    step[0] += 1
                    ins.then_inc(d_chain, 1)
                    dve.wait_ge(d_chain, t * CHAIN + step[0])
                dve.wait_ge(d_yhi, t + D1)
                tt(xl[:, :, :], ps[:, 4, 0:D].rearrange("p (c k) -> p c k", k=128), xh[:, :, :],
                   ALU.subtract).then_inc(d_ysplit, 1)
                dve.wait_ge(d_gl, t + D1)
                tt(dg[:, 0, :], ps[:, 5, 0:EM + 1], tvec[:, U_GB:U_GB + EM + 1], ALU.add).then_inc(d_gb, 1)
                dve.wait_ge(d_ge, t + D1)
                link(ts(dg[:, 2, :], dg[:, 1, :], 1.0, None, ALU.add))
                link(nc.vector.reciprocal(dg[:, 3, :], dg[:, 2, :]))
                link(tt(dg[:, 4, 0:EM], dg[:, 3, 1:EM + 1], tvec[:, U_XB:U_XB + EM], ALU.add))
                link(nc.vector.tensor_reduce(dsm[:, 0:1], dg[:, 4, 0:EM], AX.X, ALU.max))
                link(ts(dg[:, 5, 0:EM], dg[:, 4, 0:EM], dsm[:, 0:1], None, ALU.is_equal))
                link(tt(dg[:, 6, 0:EM], dg[:, 5, 0:EM], cst[:, C_RNK8:C_RNK8 + EM], ALU.mult))
                link(nc.vector.tensor_reduce(dsm[:, 1:2], dg[:, 6, 0:EM], AX.X, ALU.max))
                ts(dg[:, 7, 0:EM], dg[:, 6, 0:EM], dsm[:, 1:2], None, ALU.is_equal).then_inc(d_sel, 1)
                dve.wait_ge(d_sel, t + D1)
                link(tt(dg[:, 8, 0:EM], dg[:, 7, 0:EM], dg[:, 3, 1:EM + 1], ALU.mult))
                link(nc.vector.tensor_reduce(dsm[:, 2:3], dg[:, 8, 0:EM], AX.X, ALU.add))
                tt(dsm[:, 3:4], dg[:, 3, 0:1], dsm[:, 2:3], ALU.subtract).then_inc(d_diff, 1)
                dve.wait_ge(d_we, t + D1)
                link(ts(dsm[:, 5:6], dsm[:, 4:5], 1.0, None, ALU.add))
                link(nc.vector.reciprocal(dsm[:, 4:5], dsm[:, 5:6]))
                link(ts(dsm[:, 5:6], dsm[:, 4:5], -1.0, 1.0, ALU.mult, ALU.add))
                dve.wait_ge(d_bias_sb, t + D1)
                dve.wait_ge(d_h, t + D1)
                for e in range(EM):
                    src = bsel[:, 0:2 * HM] if e == 0 else hsel[:, :]
                    ins = stt(hsel[:, :], ps[:, e // 2, 256 * (e % 2):256 * (e % 2) + 256], dg[:, 7, e:e + 1], src,
                              ALU.mult, ALU.add)
                    if e < EM - 1:
                        link(ins)
                ins.then_inc(d_hsel, 1)
                dve.wait_ge(d_e, t + D1)
                link(ts(de[:, HM:2 * HM], de[:, 0:HM], 1.0, None, ALU.add))
                link(nc.vector.reciprocal(de[:, 0:HM], de[:, HM:2 * HM]))
                link(tt(h[:, 0:HM], hsel[:, 0:HM], de[:, 0:HM], ALU.mult))
                link(tt(h[:, HM:2 * HM], h[:, 0:HM], hsel[:, HM:2 * HM], ALU.mult))
                link(nc.vector.bn_stats(st[:, 2, :], h[:, HM:2 * HM]))
                nc.vector.memset(junk[:, 2:3], 0.0)
                nc.vector.bn_aggr(mv[:, 2, :], st[:, 2, :]).then_inc(d_var, 1)
                dve.wait_ge(d_rstd, t + D1)
                normalized(h[:, 2 * HM:3 * HM], h[:, HM:2 * HM], 2).then_inc(d_gn, 1)
                dve.wait_ge(d_zhi, t + D1)
                tt(hl[:, 0, :], ps[:, 6, 0:HM], hh[:, 0, :], ALU.subtract).then_inc(d_zsplit, 1)
                dve.wait_ge(d_o, t + D1)
                for e in range(EM):
                    src = bsel[:, 2 * HM:] if e == 0 else acc[:, :]
                    link(stt(acc[:, :], ps[:, e // 2, 256 * (e % 2):256 * (e % 2) + 256], dg[:, 7, e:e + 1], src,
                             ALU.mult, ALU.add))
                link(ts(acc[:, :], acc[:, :], dsm[:, 5:6], None, ALU.mult))
                link(stt(acc[:, :], comb[:, ds(t * (3 * D) + 2 * D, D)], dsm[:, 4:5], acc[:, :], ALU.mult, ALU.add))
                tt(finD[:, ds(t * D, D)], acc[:, :], comb[:, ds(t * (3 * D), D)], ALU.add).then_inc(d_fin, 1)
                assert step[0] == CHAIN, step[0]

        @block.gpsimd
        def _(pool):
            tt = nc.gpsimd.tensor_tensor

            def rstd(i, n, var, veps, done):
                pool.wait_ge(var, n)
                tt(rs[:, i, :], mv[:, i, 1:2], cst[:, C_EPS:C_EPS + 1], ALU.add).then_inc(veps, 1)
                pool.wait_ge(veps, n)
                tt(rs[:, i, :], rs[:, i, :], halves, ALU.pow).then_inc(done, 1)

            pool.wait_ge(cst_in, 16)
            with pool.Fori(0, B // 2) as i:
                n = [i * 2 + (j + 1) for j in range(2)]
                for j in range(2):
                    rstd(j, n[j], a_var, a_veps, a_rstd)
                pool.wait_ge(w_hi_ready, n[0])
                tt(w_lo[:, ds(i * (2 * WCH), WCH)], stage[:, 0, :], w_hi[:, ds(i * (2 * WCH), WCH)],
                   ALU.subtract).then_inc(w_lo_ready, 1)
                for j in range(2):
                    rstd(2 + j, n[j], a_gvar, a_gveps, a_grstd)
                pool.wait_ge(w_hi_ready, n[1])
                tt(w_lo[:, ds(i * (2 * WCH) + WCH, WCH)], stage[:, 1, :], w_hi[:, ds(i * (2 * WCH) + WCH, WCH)],
                   ALU.subtract).then_inc(w_lo_ready, 1)
            pool.wait_ge(wc_hi_ready, 1)
            tt(wc_lo, wc_raw, wc_hi, ALU.subtract).then_inc(wc_ready, 1)

            def expert(u):
                return pool.value_load(chosen[0:1, ds(u, 1)], min_val=0, max_val=E - 1)

            def at(b):
                return x[:, ds(b * D, D)]

            def y_bias(n, k, base):
                pool.wait_ge(y_ready, k + 1)
                tt(ybo[:, :], y[:, :], vec[:, ds(base + V_OUT, D)], ALU.add).then_inc(ybo_ready, 1)

            def affine1(n, base):
                rstd(1, n + 1, l1_var, l1_veps, l1_rstd)
                pool.wait_ge(l1_xn, n + 1)
                tt(x1[:, :], x1[:, :], vec[:, ds(base + V_G1, D)], ALU.mult).then_inc(l1_g, 1)
                pool.wait_ge(l1_g, n + 1)
                tt(x1[:, :], x1[:, :], vec[:, ds(base + V_B1, D)], ALU.add).then_inc(x1_ready, 1)
                pool.wait_ge(x1_ready, n + 1)
                tt(x1b[:, :], x1[:, :], vec[:, ds(base + V_L2, D)], ALU.add).then_inc(x1b_ready, 1)

            def affine2(n, base):
                rstd(2, n + 1, l2_var, l2_veps, l2_rstd)
                pool.wait_ge(l2_xn, n + 1)
                tt(y2[:, :], y2[:, :], vec[:, ds(base + V_G2, D)], ALU.mult).then_inc(l2_g, 1)
                pool.wait_ge(l2_g, n + 1)
                tt(y2[:, :], y2[:, :], vec[:, ds(base + V_B2, D)], ALU.add).then_inc(y2_ready, 1)

            def both(n, k, f, k_next):
                bn, bf = expert(n) * V_EXP, expert(f) * V_EXP
                pool.wait_ge(res1, n)
                y_bias(n, k, bn)
                if k_next is not None:
                    rstd(0, k_next + 1, y_var, y_veps, y_rstd)
                affine2(f, bf)
                affine1(n, bn)

            pool.wait_ge(g_ready, 1)
            rstd(0, 1, y_var, y_veps, y_rstd)
            b0 = expert(0) * V_EXP
            y_bias(0, 0, b0)
            affine1(0, b0)
            with pool.Fori(0, B - 1) as b:
                both(b * 2 + 1, b, b * 2, b + 1)
                both(b * 2 + 2, b + 1, b * 2 + 1, None)
            both(UNITS - 1, B - 1, UNITS - 2, None)
            affine2(UNITS - 1, expert(UNITS - 1) * V_EXP)

            def tw(i):
                for j in range(2):
                    pool.wait_ge(tw_hi, i * 2 + (j + 1))
                    tt(w_lo[:, ds(i * (2 * TCH) + j * TCH, TCH)], tstage[:, j, :],
                       w_hi[:, ds(i * (2 * TCH) + j * TCH, TCH)], ALU.subtract).then_inc(tw_lo, 1)

            def x_bias(b):
                pool.wait_ge(res1, b + UNITS)
                pool.wait_ge(y_ready, b + (B + 1))
                tt(ybo[:, :], at(b), vc[:, V_OUT:V_OUT + D], ALU.add).then_inc(ybo_ready, 1)

            def sh_rstd(b):
                rstd(1, b + C1, s_var, s_veps, s_rstd)

            def sh_affine(b):
                rstd(2, b + C1, s_gvar, s_gveps, s_grs)
                pool.wait_ge(s_gn, b + C1)
                tt(h[:, 512:512 + HM], h[:, 2 * HM:3 * HM], tvec[:, U_SG:U_SG + HM], ALU.mult).then_inc(s_gg, 1)
                pool.wait_ge(s_gg, b + C1)
                tt(h[:, 512:512 + HM], h[:, 512:512 + HM], tvec[:, U_SB:U_SB + HM], ALU.add).then_inc(s_z, 1)

            with pool.Fori(0, B // 2) as i:
                tw(i)
            pool.wait_ge(vc_in, 16)
            rstd(0, B + 1, y_var, y_veps, y_rstd)
            x_bias(0)
            sh_rstd(0)
            rstd(0, B + 2, y_var, y_veps, y_rstd)
            pool.wait_ge(tvec_in, 16)
            with pool.Fori(0, B - 2) as b:
                x_bias(b + 1)
                sh_affine(b)
                sh_rstd(b + 1)
                rstd(0, b + (B + 3), y_var, y_veps, y_rstd)
            x_bias(B - 1)
            sh_affine(B - 2)
            sh_rstd(B - 1)
            sh_affine(B - 1)

            pool.wait_ge(s_comb, 16 * 3 * B)
            pool.wait_ge(d_gidx, 1)
            for t in range(MT):
                nc.gpsimd.indirect_dma_start(out=comb[:, t * 3 * D:(t + 1) * 3 * D], out_offset=None, in_=comb_d[:, :],
                                             in_offset=bass.IndirectOffsetOnAxis(ap=gidx[:, t:t + 1], axis=0)
                                             ).then_inc(d_gather, 16)
            with pool.Fori(0, MT) as t:
                rstd(2, t + D1, d_var, d_veps, d_rstd)
                pool.wait_ge(d_gn, t + D1)
                tt(h[:, 512:512 + HM], h[:, 2 * HM:3 * HM], tvec[:, U_EG:U_EG + HM], ALU.mult).then_inc(d_gg, 1)
                pool.wait_ge(d_gg, t + D1)
                tt(h[:, 512:512 + HM], h[:, 512:512 + HM], tvec[:, U_EB:U_EB + HM], ALU.add).then_inc(d_z, 1)
            pool.wait_ge(d_sidx, 1)
            pool.wait_ge(s_out, 16 * B)
            for t in range(MT):
                pool.wait_ge(d_fin, t + D1)
                nc.gpsimd.indirect_dma_start(out=out[:, :],
                                             out_offset=bass.IndirectOffsetOnAxis(ap=sidx[:, t:t + 1], axis=0),
                                             in_=finD[:, t * D:(t + 1) * D], in_offset=None,
                                             bounds_check=B * S - 1, oob_is_err=False).then_inc(d_out, 16)


def _consts(np):
    p = np.arange(128)
    c = np.zeros((128, C_ALL), np.float32)
    c[:, C_ID:C_ID + 128] = np.eye(128)
    c[:, C_ME] = (p % 32) < 16
    c[:, C_MO] = (p % 32) >= 16
    c[:, C_RNK4:C_RNK4 + E] = [4, 3, 2, 1]
    c[:, C_ID4:C_ID4 + E] = [0, 1, 2, 3]
    c[:, C_RNK8:C_RNK8 + EM] = [8, 7, 6, 5, 4, 3, 2, 1]
    c[:, C_M:C_M + MT] = p[:, None] + 128 * np.arange(MT)[None, :]
    c[:, C_HALF] = -0.5
    c[:, C_EPS] = EPS
    k = np.zeros((128, K_ALL), np.float32)
    for s in range(4):
        k[:, K_SEL + 128 * s:K_SEL + 128 * (s + 1)] = ((p % 16) == 4 * (p // 32) + s)[:, None]
    k[:, K_CS:K_CS + 128] = np.where(p[None, :] > p[:, None], -1e30, 0)
    k[:, K_CT:K_CT + 128] = np.where(p[:, None] > p[None, :], -1e30, 0)
    for e in range(E):
        k[[e, 32 + e], K_ROW + 128 * e:K_ROW + 128 * (e + 1)] = 1
    return c, k, np.arange(M, dtype=np.float32)[None, :]


def _chunks(np, w):
    n = w.shape[0] // 128
    return np.concatenate([w[128 * c:128 * (c + 1)] for c in range(n)], axis=1)


def kernel(**inputs):
    import numpy as np
    import concourse.bacc as bacc
    from concourse.bass_utils import run_bass_kernel_spmd

    a = {k: np.asarray(v) for k, v in inputs.items()}
    f0 = {k[7:]: v for k, v in a.items() if k.startswith("L0_ffn_")}
    at = {k[9:]: v for k, v in a.items() if k.startswith("L1_xattn_")}
    f1 = {k[7:]: v for k, v in a.items() if k.startswith("L1_ffn_")}
    tokens = lambda t: np.ascontiguousarray(t.transpose(1, 0, 2).reshape(S, B * D))
    cat = np.concatenate
    w = cat([cat([_chunks(np, f0["in_proj_w"][e].T), _chunks(np, f0["out_proj_w"][e].T),
                  _chunks(np, f0["lin1_w"][e].T), _chunks(np, f0["lin2_w"][e].T)], axis=1) for e in range(E)], axis=1)
    wc = cat([_chunks(np, cat([at["Wq"], at["Wk"], at["Wv"]]).T), _chunks(np, at["Wo"].T)], axis=1)
    vec = cat([cat([f0["in_proj_b"][e], f0["out_proj_b"][e], f0["lin2_b"][e], f0["ln1_w"][e], f0["ln1_b"][e],
                    f0["ln2_w"][e], f0["ln2_b"][e]]) for e in range(E)])[None, :]
    vc = cat([at["bq"], at["bk"], at["bv"], at["bo"]])[None, :]
    e12 = cat([cat([f1["ew1"][e], f1["ew2"][e]]).T for e in range(EM)], axis=1)
    tw = cat([_chunks(np, cat([f1["sw1"], f1["sw2"]]).T), _chunks(np, f1["sw3"].T), _chunks(np, e12),
              cat([f1["ew3"][e].T for e in range(EM)], axis=1)], axis=1)
    tvec = cat([f1["sb1"], f1["sb2"], f1["sb3"], f1["s_ln_g"], f1["s_ln_b"], f1["sel_ln_g"], f1["sel_ln_b"],
                f1["sg_b"], f1["eg_b"], f1["exp_bias"]])[None, :]
    tg = cat([f1["sg_w"], f1["eg_w"]]).T.reshape(KC, 128, EM + 1).transpose(1, 0, 2)
    tb = cat([f1["eb1"], f1["eb2"], f1["eb3"]], axis=1)
    cst, kst, pos = _consts(np)
    arrays = {
        "x": tokens(a["x"]), "ctx": tokens(a["ctx_1024"]), "mask": a["mask_Bx1xS2_ik1"].reshape(1, B * S),
        "w": w, "wc": wc, "vec": vec, "vc": vc, "b1": f0["lin1_b"],
        "gw": f0["gate_w"].T.reshape(KC, 128, E).transpose(1, 0, 2), "gb": f0["gate_b"][None, :],
        "tw": tw, "tvec": tvec, "tg": tg, "tb": tb,
        "ib": f1["index_b"].reshape(MT, 128).T, "it": f1["index_t"].reshape(MT, 128).T,
        "ibr": f1["index_b"][None, :], "itr": f1["index_t"][None, :], "cst": cst, "kst": kst, "pos": pos,
    }
    arrays = {f"in_{k}": np.ascontiguousarray(v) for k, v in arrays.items()}
    nc = bacc.Bacc("TRN2", target_bir_lowering=False, num_devices=1)
    args = [nc.dram_tensor(k, v.shape, mybir.dt.from_np(v.dtype), kind="ExternalInput").ap() for k, v in arrays.items()]
    out = nc.dram_tensor("out", (B * S, D), mybir.dt.float32, kind="ExternalOutput").ap()
    comb = nc.dram_tensor("comb", (B * S, 3 * D), mybir.dt.float32, kind="Internal").ap()
    encoder_kernel(nc, *args, out, comb)
    r = run_bass_kernel_spmd(nc, [arrays], core_ids=[0])
    return np.asarray(r.results[0]["out"]).reshape(B, S, D)
```

```python
import concourse.bass as bass
from concourse import mybir
from contextlib import ExitStack

B, S, D = 16, 128, 256
KC = D // 128
H, HD = 16, 16
E, TOPK = 4, 2
DFF = 1024
FC = DFF // 128
EM, HM, M = 8, 128, 512
MT = M // 128
UNITS = B * TOPK
EPS = 1e-5
NEG = -1e10
SCALE_A = 0.25
KEEP = 1.0 / (1.0 - 0.1 / (256 * 512))
SCALE_H = HD ** -0.5

W_QKV, W_OUT, W_L1, W_L2 = 0, KC * 3 * D, KC * 4 * D, KC * 4 * D + KC * DFF
W_EXP = W_L2 + FC * D
W_ALL = E * W_EXP
WCH = W_ALL // B
W_CAUS = KC * 4 * D
T_S12, T_S3 = 0, KC * 2 * HM
T_E12 = T_S3 + D
T_E3 = T_E12 + KC * EM * 2 * HM
T_ALL = T_E3 + EM * D
TCH = T_ALL // B
V_QKV, V_OUT, V_L2, V_G1, V_B1, V_G2, V_B2 = 0, 768, 1024, 1280, 1536, 1792, 2048
V_EXP = 2304
V_ALL = E * V_EXP
U_S12, U_S3, U_SG, U_SB, U_EG, U_EB, U_GB, U_XB = 0, 256, 512, 640, 768, 896, 1024, 1033
U_ALL = U_XB + EM
R_STAGE, R_TVEC, R_COMB = 0, 2 * TCH + 160, 2304
R_ROWI = R_COMB + MT * 3 * D
R_ROWF = R_ROWI + 2 * M
R_FIN = R_ROWF + 2 * M
R_POS = R_FIN + MT * D
C_ID, C_ME, C_MO, C_RNK4, C_ID4, C_RNK8, C_M, C_HALF, C_EPS = 0, 128, 129, 130, 134, 138, 146, 150, 151
C_ALL = 152
K_SEL, K_CS, K_CT, K_ROW = 0, 512, 640, 768
K_ALL = K_ROW + E * 128


def encoder_kernel(nc, x_d, ctx_d, mask_d, w_d, wc_d, vec_d, vc_d, b1_d, gw_d, gb_d, tw_d, tvec_d, tg_d, tb_d,
                   ib_d, it_d, ibr_d, itr_d, cst_d, kst_d, pos_d, out, comb_d):
    f32, bf16, i32, u32 = mybir.dt.float32, mybir.dt.bfloat16, mybir.dt.int32, mybir.dt.uint32
    ALU = mybir.AluOpType
    ACT = mybir.ActivationFunctionType
    AX = mybir.AxisListType
    ds = bass.ds

    stack = ExitStack()
    with stack:
        def sb(name, shape, dt=f32):
            return stack.enter_context(nc.sbuf_tensor(name, shape, dt))

        ps = stack.enter_context(nc.psum_tensor("ps", [128, 8, 512], f32))

        x = sb("x", [128, B * D])
        w_hi = sb("w_hi", [128, W_ALL], bf16)
        w_lo = sb("w_lo", [128, W_ALL], bf16)
        vec = sb("vec", [128, V_ALL])
        b1hl = sb("b1hl", [64, DFF], bf16)
        cst = sb("cst", [128, C_ALL])
        identb = sb("identb", [128, 128], bf16)
        kst = sb("kst", [128, K_ALL], bf16)
        gate_b = sb("gate_b", [128, E])
        ones = sb("ones", [128, 128])
        gmean = sb("gmean", [128, KC, B])
        gw = sb("gw", [128, KC, E])
        gate_w = sb("gate_w", [128, UNITS])
        chosen = sb("chosen", [128, UNITS], i32)

        y = sb("y", [128, D])
        ycT_hi = sb("ycT_hi", [128, 2 * KC, 128], bf16)
        ycT_lo = sb("ycT_lo", [128, 2 * KC, 128], bf16)
        qk = sb("qk", [128, 2 * D])
        v = sb("v", [128, H, 32])
        qh = sb("qh", [128, KC, 128], bf16)
        ql = sb("ql", [128, KC, 128], bf16)
        khm = sb("khm", [128, KC, 2, 128], bf16)
        klm = sb("klm", [128, KC, 2, 128], bf16)
        mx = sb("mx", [128, H])
        mtile = sb("mtile", [128, 4, 2, H], bf16)
        mT = sb("mT", [128, 128], bf16)
        pT = sb("pT", [128, H, 128])
        o_rs = sb("o_rs", [128, H])
        o = sb("o", [128, D])
        ooh = sb("ooh", [128, KC, 128], bf16)
        ool = sb("ool", [128, KC, 128], bf16)
        ybo = sb("ybo", [128, 2, D])
        t1 = sb("t1", [128, D])
        ctxb = sb("ctxb", [128, 2, D])
        oT = ctxb[:, :, :].rearrange("p j (a q) -> p (j a) q", q=128)
        ctxc = sb("ctxc", [128, D])
        x1 = sb("x1", [128, D])
        x1b = sb("x1b", [128, D])
        xh = sb("xh", [128, KC, 128], bf16)
        xl = sb("xl", [128, KC, 128], bf16)
        h = sb("h", [128, DFF])
        hh = sb("hh", [128, FC, 128], bf16)
        hl = sb("hl", [128, FC, 128], bf16)
        t2 = sb("t2", [128, D])
        y2 = sb("y2", [128, D])
        st = sb("st", [128, 4, 6])
        mv = sb("mv", [128, 4, 2])
        rs = sb("rs", [128, 4, 1])
        junk = sb("junk", [128, 3])
        mask_i = pT[:, :, :].rearrange("p h q -> p (h q)").bitcast(i32)
        stage = sb("stage", [128, 2, WCH])
        kraw = vec[:, 0:K_ALL]
        gl = h[:, 0:12 * B * E].rearrange("p (k j) -> p k j", j=B * E)
        gprod = h[:, 768:768 + KC * B * E].rearrange("p (c b e) -> p c b e", b=B, e=E)
        gs = h[:, 896:896 + 8 * B].rearrange("p (k b) -> p k b", b=B)
        wc_raw = pT[:, :, :].rearrange("p h q -> p (h q)")
        stage_b = stage[:, :, :].rearrange("p a w -> p (a w)").bitcast(bf16)
        wc_hi, wc_lo = stage_b[:, 0:W_CAUS], stage_b[:, W_CAUS:2 * W_CAUS]
        vc = stage[:, :, :].rearrange("p a w -> p (a w)")[:, W_CAUS:W_CAUS + 4 * D]
        tstage = vec[:, R_STAGE:R_STAGE + 2 * TCH].rearrange("p (a w) -> p a w", a=2)
        tvec = vec[:, R_TVEC:R_TVEC + U_ALL]
        acc, fin = x1b, x1
        comb = vec[:, R_COMB:R_COMB + MT * 3 * D]
        row_i = vec[:, R_ROWI:R_ROWI + 2 * M].rearrange("p (a m) -> p a m", a=2).bitcast(i32)
        row_f = vec[:, R_ROWF:R_ROWF + 2 * M].rearrange("p (a m) -> p a m", a=2)
        finD = vec[:, R_FIN:R_FIN + MT * D]
        pos = vec[:, R_POS:R_POS + M]
        idx_i = sb("idx_i", [128, 2, MT], i32)

        def sem(name):
            return stack.enter_context(nc.semaphore(name))

        (x_in0, x_in1, ctx_in00, ctx_in01, ctx_in10, ctx_in11, cst_in, kst_in, mask_in, w_in0, w_in1, vec_in, b1_in, gw_in, wc_in, vc_in,
         tvec_in) = (sem(n) for n in (
             "x_in0", "x_in1", "ctx_in00", "ctx_in01", "ctx_in10", "ctx_in11", "cst_in", "kst_in", "mask_in", "w_in0", "w_in1", "vec_in", "b1_in",
             "gw_in", "wc_in", "vc_in", "tvec_in"))
        ctx_in = ((ctx_in00, ctx_in01), (ctx_in10, ctx_in11))
        cst_ready, ones_ready, vones_ready, b1_zero, b1_hi, b1_ready, w_hi_ready, w_lo_ready, wc_hi_ready, wc_ready = (
            sem(n) for n in ("cst_ready", "ones_ready", "vones_ready", "b1_zero", "b1_hi", "b1_ready", "w_hi_ready",
                             "w_lo_ready", "wc_hi_ready", "wc_ready"))
        (a_stats, a_var, a_veps, a_rstd, a_q, a_T, a_hi, a_split, a_s, a_m01, a_neg, a_sm, a_sn, a_max, a_bias,
         a_p, a_pT, a_pTs, a_pv, a_rsum, a_keep, a_x, a_gstats, a_gvar, a_gveps, a_grstd, a_g, a_gm, a_gmean) = (
            sem("a_" + n) for n in ("stats", "var", "veps", "rstd", "q", "T", "hi", "split", "s", "m01", "neg", "sm",
                                    "sn", "max", "bias", "p", "pT", "pTs", "pv", "rsum", "keep", "x", "gstats", "gvar",
                                    "gveps", "grstd", "g", "gm", "gmean"))
        g_prod, g_log, g_fill, g_dve, g_exp, g_ready = (
            sem("g_" + n) for n in ("prod", "log", "fill", "dve", "exp", "ready"))
        (y_stats, y_var, y_veps, y_rstd, y_ready, yT_psum, yT_hi, yT_ready) = (
            sem("y_" + n) for n in ("stats", "var", "veps", "rstd", "ready", "T_psum", "T_hi", "T_ready"))
        (qk_psum, v_psum, qk_sb, v_sb, qkT_psum, qkT_hi, qk_split, s_psum, m_max, m_hi, m_split, mT_psum, mT_sb, st_psum,
         pT_a, pT_b, oT_psum, oT_sb, o_row, o_rsum, o_sb, oo_psum, oo_hi, oo_split, proj_psum, ybo_ready) = (
            sem(n) for n in ("qk_psum", "v_psum", "qk_sb", "v_sb", "qkT_psum", "qkT_hi", "qk_split", "s_psum", "m_max", "m_hi",
                             "m_split", "mT_psum", "mT_sb", "st_psum", "pT_a", "pT_b", "oT_psum", "oT_sb", "o_row",
                             "o_rsum", "o_sb", "oo_psum", "oo_hi", "oo_split", "proj_psum", "ybo_ready"))
        (res1, l1_stats, l1_var, l1_veps, l1_rstd, l1_xn, l1_g, x1_ready, x1b_ready) = (
            sem(n) for n in ("res1", "l1_stats", "l1_var", "l1_veps", "l1_rstd", "l1_xn", "l1_g", "x1_ready",
                             "x1b_ready"))
        (x1T_psum, x1T_hi, x1T_split, h_a, h_b, h_sb_a, h_sb_b, hT_a, hT_b, hh_a, hh_b, hl_a, hl_b, ff_psum,
         res2, l2_stats, l2_var, l2_veps, l2_rstd, l2_xn, l2_g, y2_ready, x_acc) = (
            sem(n) for n in ("x1T_psum", "x1T_hi", "x1T_split", "h_a", "h_b", "h_sb_a", "h_sb_b", "hT_a", "hT_b",
                             "hh_a", "hh_b", "hl_a", "hl_b", "ff_psum", "res2", "l2_stats", "l2_var", "l2_veps",
                             "l2_rstd", "l2_xn", "l2_g", "y2_ready", "x_acc"))
        c_ctx, tw_in0, tw_in1, tw_hi, tw_lo, s_comb, s_shared, s_out = (
            sem("c_" + n) for n in ("ctx", "tw_in0", "tw_in1", "tw_hi", "tw_lo", "comb", "shared", "out"))
        s_stats, s_var, s_veps, s_rstd, s_y, s_yT, s_yhi, s_ysplit, s_h, s_hb, s_e, s_e1, s_r, s_a = (
            l1_stats, l1_var, l1_veps, l1_rstd, l1_xn, x1T_psum, x1T_hi, x1T_split, h_a, h_sb_a, h_b, h_sb_b, l1_g, hT_a)
        s_g, s_gst, s_gvar, s_gveps, s_grs, s_gn, s_gg, s_z, s_zT, s_zhi, s_zsplit, s_o, s_sh, s_sum = (
            hT_b, l2_stats, l2_var, l2_veps, l2_rstd, l2_xn, l2_g, y2_ready, hh_b, hh_a, hl_a, ff_psum, res2, x1_ready)
        tg_in, tb_in, idx_in, tg_hi, tg_split, d_gidx, d_sidx, d_idx, d_gather, d_chain, d_out = (
            sem("d_" + n) for n in ("tg_in", "tb_in", "idx_in", "tg_hi", "tg_split", "gidx", "sidx", "idx", "gather",
                                    "chain", "out"))
        d_yT, d_yhi, d_ysplit, d_gl, d_gb, d_ge, d_sel, d_diff, d_we, d_oT, d_oTs, d_bias, d_bias_sb, d_h = (
            a_T, a_hi, a_split, a_s, a_bias, a_p, a_max, a_keep, a_pTs, a_pT, a_m01, a_pv, a_neg, a_gm)
        d_hsel, d_e, d_var, d_veps, d_rstd, d_gn, d_gg, d_z, d_zT, d_zhi, d_zsplit, d_o, d_fin = (
            a_x, a_rsum, a_var, a_veps, a_rstd, a_q, a_g, a_sm, a_sn, a_gstats, a_gvar, a_grstd, a_gmean)
        d_y = a_gveps
        C1, D1 = UNITS + 1, B + 1

        tg = sb("tg", [128, KC, EM + 1])
        tg_h = sb("tg_h", [128, KC, EM + 1], bf16)
        tg_l = sb("tg_l", [128, KC, EM + 1], bf16)
        tb = v[0:EM, :, :].rearrange("p h k -> p (h k)")
        ids = sb("ids", [128, 10, MT])
        gidx = sb("gidx", [128, MT], i32)
        sidx = sb("sidx", [128, MT], i32)
        dg = sb("dg", [128, 10, EM + 1])
        dsm = sb("dsm", [128, 8])
        ohT = ooh[0:EM, :, :].rearrange("p c k -> p (c k)").bitcast(f32)
        bsel = qk
        hsel = o
        de = y2

        ident = cst[:, C_ID:C_ID + 128]
        mask_eo = [cst[:, C_ME:C_ME + 1], cst[:, C_MO:C_MO + 1]]
        att = ps[:, 0:4, :].rearrange("p g (s k) -> p g s k", k=128)

        selb = kst[:, K_SEL:K_SEL + 512].rearrange("p (s k) -> p s k", k=128)
        causb = kst[:, K_CS:K_CS + 256].rearrange("p (s k) -> p s k", k=128)
        halves = cst[:, C_HALF:C_HALF + 1]

        def head(g, c, s):
            return 8 * c + 2 * g + s

        b1f = [v[0:E, :, :].rearrange("p h k -> p (h k)"), qk[0:E, :]]
        ya, ta, tb2, tg2 = (y, y2), (t1, o), (t2, ybo[:, 0, :]), (x1, x1b)
        ctx_a = ((ctxb[:, 0, :], ctxb[:, 1, :]), (ctxc[:, :], ybo[:, 1, :]))
        PAIRS = B // 2
        yca_hi, yca_lo = (ycT_hi, hh), (ycT_lo, hl)

        block = stack.enter_context(nc.Block())

        @block.sync
        def _(sp):
            sp.dma_start(x[:, 0:2 * D], x_d[:, 0:2 * D]).then_inc(x_in0, 16)
            sp.dma_start(cst[:, :], cst_d).then_inc(cst_in, 16)
            sp.dma_start(ctx_a[0][0], ctx_d[:, 0:D]).then_inc(ctx_in[0][0], 16)
            sp.dma_start(ctx_a[0][1], ctx_d[:, D:2 * D]).then_inc(ctx_in[0][1], 16)
            sp.dma_start(kraw, kst_d).then_inc(kst_in, 16)
            sp.dma_start(mask_i, mask_d.broadcast_to([128, B * S])).then_inc(mask_in, 16)
            sp.dma_start(stage[:, 0, :], w_d[:, 0:WCH]).then_inc(w_in0, 16)
            sp.dma_start(stage[:, 1, :], w_d[:, WCH:2 * WCH]).then_inc(w_in1, 16)
            sp.dma_start(x[:, 2 * D:], x_d[:, 2 * D:]).then_inc(x_in1, 16)
            sp.dma_start(ctx_a[1][0], ctx_d[:, 2 * D:3 * D]).then_inc(ctx_in[1][0], 16)
            sp.dma_start(ctx_a[1][1], ctx_d[:, 3 * D:4 * D]).then_inc(ctx_in[1][1], 16)
            sp.dma_start(gw[:, :, :], gw_d).then_inc(gw_in, 16)
            sp.dma_start(gate_b[:, :], gb_d.broadcast_to([128, E])).then_inc(gw_in, 16)
            for half in range(2):
                sp.dma_start(b1f[half], b1_d[:, 512 * half:512 * half + 512]).then_inc(b1_in, 16)
            sp.wait_ge(cst_ready, 1)
            for e in range(E):
                sp.dma_start(vec[:, e * V_EXP:(e + 1) * V_EXP],
                             vec_d[:, e * V_EXP:(e + 1) * V_EXP].broadcast_to([128, V_EXP])).then_inc(vec_in, 16)
            def next_of_pair(i, parity, with_ctx):
                for j in range(2):
                    sp.wait_ge(w_lo_ready, i * 2 + (j + 1))
                    sp.dma_start(stage[:, j, :], w_d[:, ds(i * (2 * WCH) + (2 + j) * WCH, WCH)]).then_inc(
                        w_in1 if j else w_in0, 16)
                    if with_ctx:
                        sp.wait_ge(a_x, i * 2 + (j + 1))
                        sp.dma_start(ctx_a[parity][j], ctx_d[:, ds(i * (2 * D) + (4 + j) * D, D)]).then_inc(
                            ctx_in[parity][j], 16)
            with sp.Fori(0, PAIRS // 2 - 1) as p:
                next_of_pair(p * 2, 0, True)
                next_of_pair(p * 2 + 1, 1, True)
            next_of_pair(PAIRS - 2, 0, False)
            sp.wait_ge(a_neg, B)
            sp.dma_start(wc_raw, wc_d).then_inc(wc_in, 16)
            sp.wait_ge(w_lo_ready, B)
            sp.dma_start(vc, vc_d.broadcast_to([128, 4 * D])).then_inc(vc_in, 16)
            sp.wait_ge(a_x, B)
            sp.dma_start(ctxc[:, :], ctx_d[:, 0:D]).then_inc(c_ctx, 16)
            sp.wait_ge(yT_psum, B + 1)
            sp.dma_start(ctxc[:, :], ctx_d[:, D:2 * D]).then_inc(c_ctx, 16)
            sp.wait_ge(yT_psum, B + 2)
            sp.dma_start(ctxc[:, :], ctx_d[:, 2 * D:3 * D]).then_inc(c_ctx, 16)
            sp.wait_ge(y2_ready, UNITS)
            sp.dma_start(tstage[:, 0, :], tw_d[:, 0:TCH]).then_inc(tw_in0, 16)
            sp.dma_start(tstage[:, 1, :], tw_d[:, TCH:2 * TCH]).then_inc(tw_in1, 16)
            sp.dma_start(tvec, tvec_d.broadcast_to([128, U_ALL])).then_inc(tvec_in, 16)
            sp.dma_start(tg[:, :, :], tg_d).then_inc(tg_in, 16)
            sp.dma_start(pos, pos_d.broadcast_to([128, M])).then_inc(idx_in, 16)
            sp.dma_start(idx_i[:, 0, :], ib_d).then_inc(idx_in, 16)
            sp.dma_start(idx_i[:, 1, :], it_d).then_inc(idx_in, 16)
            sp.dma_start(row_i[:, 0, :], ibr_d.broadcast_to([128, M])).then_inc(idx_in, 16)
            sp.dma_start(row_i[:, 1, :], itr_d.broadcast_to([128, M])).then_inc(idx_in, 16)

            def next_weights(c, j):
                sp.wait_ge(tw_lo, c - 1)
                sp.dma_start(tstage[:, j, :], tw_d[:, ds(c * TCH, TCH)]).then_inc(tw_in1 if j else tw_in0, 16)

            def next_context(b):
                sp.wait_ge(yT_psum, b + B)
                sp.dma_start(ctxc[:, :], ctx_d[:, ds(b * D, D)]).then_inc(c_ctx, 16)

            def put_tokens(b):
                sp.wait_ge(s_y, b + C1)
                sp.dma_start(comb_d[ds(b * S, S), 0:D], x[:, ds(b * D, D)]).then_inc(s_comb, 16)
                sp.dma_start(comb_d[ds(b * S, S), D:2 * D], t1[:, :]).then_inc(s_comb, 16)

            def put_shared(b):
                sp.wait_ge(s_sum, b + C1)
                sp.dma_start(comb_d[ds(b * S, S), 2 * D:3 * D], acc[:, :]).then_inc(s_shared, 16)
                sp.dma_start(out[ds(b * S, S), :], fin[:, :]).then_inc(s_out, 16)

            next_context(3)
            put_tokens(0)
            next_weights(2, 0)
            next_weights(3, 1)
            next_context(4)
            put_tokens(1)
            with sp.Fori(1, B // 2 - 2) as j:
                for i in range(2):
                    b = j * 2 + i
                    put_shared(j * 2 + (i - 2) if i != 0 else (j - 1) * 2)
                    next_weights(j * 2 + (i + 2), i)
                    next_context(j * 2 + (i + 3))
                    put_tokens(b)
            for b in range(B - 4, B + 2):
                put_shared(b - 2)
                if b + 2 < B:
                    next_weights(b + 2, b % 2)
                if b + 3 < B:
                    next_context(b + 3)
                if b < B:
                    put_tokens(b)
            sp.wait_ge(oT_psum, UNITS + B)
            sp.dma_start(tb, tb_d).then_inc(tb_in, 16)
            sp.wait_ge(s_comb, 16 * 2 * B)
            sp.wait_ge(s_shared, 16 * B)
            sp.wait_ge(s_out, 16 * B)
            sp.wait_ge(d_out, 16 * MT)

        @block.tensor
        def _(pe):
            mm = nc.tensor.matmul

            def transposed(src, bank, c0, n):
                for j in range(n):
                    last = nc.tensor.transpose(ps[:, bank, c0 + 128 * j:c0 + 128 * (j + 1)], src(j), ident)
                return last

            def split_products(dst, lhs_hi, lhs_lo, rhs_hi, rhs_lo, chunks, first=True, final=True):
                for j in range(chunks):
                    mm(dst, lhs_hi(j), rhs_hi(j), start=(first and j == 0), stop=False)
                    mm(dst, lhs_lo(j), rhs_hi(j), start=False, stop=False)
                    last = mm(dst, lhs_hi(j), rhs_lo(j), start=False, stop=(final and j == chunks - 1))
                return last

            pe.wait_ge(cst_ready, 1)
            pe.wait_ge(ones_ready, 1)

            def gate_means(i):
                for j in range(2):
                    pe.wait_ge(a_g, i * 2 + (j + 1))
                    for c in range(KC):
                        last = mm(ps[:, 4 * j + 3, c:c + 1], tg2[j][:, 128 * c:128 * c + 128], ones[:, 0:1],
                                  start=True, stop=True)
                    last.then_inc(a_gm, 1)

            def pair(i, parity, gate, turn):
                n = [i * 2 + (j + 1) for j in range(2)]
                ctx = ctx_a[parity]
                for j in range(2):
                    pe.wait_ge(a_q, n[j])
                    pe.wait_ge(ctx_in[parity][j], turn * 16)
                    transposed(lambda c: ya[j][:, 128 * c:128 * c + 128], 4 * j, 0, KC)
                    transposed(lambda c: ctx[j][:, 128 * c:128 * c + 128], 4 * j, 256, KC).then_inc(a_T, 1)
                for j in range(2):
                    pe.wait_ge(a_split, n[j])
                    split_products(ps[:, 4 * j + 1, 0:128], lambda c: yca_hi[j][:, c, :], lambda c: yca_lo[j][:, c, :],
                                   lambda c: yca_hi[j][:, KC + c, :], lambda c: yca_lo[j][:, KC + c, :],
                                   KC).then_inc(a_s, 1)
                if gate is not None:
                    gate_means(gate)
                for j in range(2):
                    pe.wait_ge(a_p, n[j])
                    transposed(lambda c: ta[j][:, 0:128], 4 * j + 2, 0, 1).then_inc(a_pT, 1)
                for j in range(2):
                    pe.wait_ge(a_pTs, n[j])
                    if gate is not None:
                        pe.wait_ge(a_gmean, gate * 2 + (j + 1))
                    mm(ps[:, 4 * j + 3, 0:D], h[:, 512 + 128 * j:640 + 128 * j], ctx[j],
                       start=True, stop=True).then_inc(a_pv, 1)

            pair(0, 0, None, 1)
            with pe.Fori(0, PAIRS // 2 - 1) as p:
                pair(p * 2 + 1, 1, p * 2, p + 1)
                pair(p * 2 + 2, 0, p * 2 + 1, p + 2)
            pair(PAIRS - 1, 1, PAIRS - 2, PAIRS // 2)
            gate_means(PAIRS - 1)
            pe.wait_ge(g_prod, 1)
            for c in range(KC):
                last = mm(ps[:, 5, 0:B * E], ones[:, :], gprod[:, c, :, :].rearrange("p b e -> p (b e)"),
                          start=(c == 0), stop=(c == KC - 1))
            last.then_inc(g_log, 1)

            def prep(k, with_ctx, bank=4):
                pe.wait_ge(y_ready, k + 1)
                last = transposed(lambda c: y[:, 128 * c:128 * c + 128], bank, 0, KC)
                if with_ctx:
                    pe.wait_ge(c_ctx, (k - (B - 1)) * 16)
                    last = transposed(lambda c: ctxc[:, 128 * c:128 * c + 128], bank, 256, KC)
                last.then_inc(yT_psum, 1)

            def w_of(base, wh, wl, off, stride, width):
                return (lambda c: wh[:, ds(base + off + c * stride, width)],
                        lambda c: wl[:, ds(base + off + c * stride, width)])

            def yT(src):
                return (lambda c: ycT_hi[:, src + c, :]), (lambda c: ycT_lo[:, src + c, :])

            PROJ_QKV, PROJ_CAUSAL = 12, 18

            def projection(n, k, base, i):
                if i == 0:
                    pe.wait_ge(yT_ready, k + 1)
                j, part = i // 3, i % 3
                if base is None:
                    kind, c = j // KC, j % KC
                    src = c if kind == 0 else KC + c
                    dst = ps[:, 5, 0:D] if kind == 2 else ps[:, 4, D * kind:D * kind + D]
                    off, width, wh, wl = W_QKV + kind * D + c * 3 * D, D, wc_hi, wc_lo
                else:
                    kind, c = (0 if j < KC else 2), j % KC
                    src = c
                    dst = ps[:, 5, 0:D] if kind == 2 else ps[:, 4, :]
                    off, width, wh, wl = base + (W_QKV + kind * D + c * 3 * D), (D if kind == 2 else 2 * D), w_hi, w_lo
                if kind == 2 and c == 0 and part == 0 and (not isinstance(n, int) or n > 1):
                    pe.wait_ge(res1, n - 1)
                lhs = (ycT_hi, ycT_lo, ycT_hi)[part][:, src, :]
                rhs = (wh, wh, wl)[part][:, ds(off, width)]
                ins = mm(dst, lhs, rhs, start=(c == 0 and part == 0), stop=(c == KC - 1 and part == 2))
                if c == KC - 1 and part == 2 and kind != 0:
                    ins.then_inc(v_psum if kind == 2 else qk_psum, 1)
                elif c == KC - 1 and part == 2 and base is not None:
                    ins.then_inc(qk_psum, 1)

            def qk_transposes(n):
                pe.wait_ge(qk_sb, n + 1)
                transposed(lambda c: qk[:, 128 * c:128 * c + 128], 4, 0, 2 * KC).then_inc(qkT_psum, 1)

            def scores(n, causal):
                pe.wait_ge(qkT_hi, n + 1)
                if causal:
                    for g in range(4):
                        mm(ps[:, g, :], identb[:, :], causb[:, 0:1, :].broadcast_to([128, 4, 128]),
                           start=True, stop=False)
                for c in range(KC):
                    for g in range(4):
                        r = slice(32 * g, 32 * g + 32)
                        last = mm(att[:, g, 2 * c:2 * c + 2, :], qh[r, c, :], khm[r, c, :, :],
                                  start=not causal, stop=(not causal or c == KC - 1))
                last.then_inc(s_psum, 1)

            def shift_transpose(n):
                pe.wait_ge(m_split, n + 1)
                nc.tensor.transpose(ps[:, 4, 0:64].bitcast(bf16),
                                    mtile[:, :, :, :].rearrange("p r a h -> p (r a h)"), identb[:, :]).then_inc(mT_psum, 1)

            def scores_T(n, causal, beside=lambda slot: None):
                pe.wait_ge(qk_split, n + 1)
                pe.wait_ge(mT_sb, n + 1)
                if causal:
                    for g in range(4):
                        mm(ps[:, g, :], identb[:, :], causb[:, 1:2, :].broadcast_to([128, 4, 128]),
                           start=True, stop=False)
                for c in range(KC):
                    for s in range(2):
                        terms = ((khm, qh), (khm, ql), (klm, qh), (None, None))
                        for k, (kt, qt) in enumerate(terms):
                            for g in range(4):
                                r = slice(32 * g, 32 * g + 32)
                                lhs = selb[r, 2 * c + s, :] if kt is None else kt[r, c, s, :]
                                rhs = mT[r, :] if qt is None else qt[r, c, :]
                                stop = k == 3 and (not causal or (c == KC - 1 and s == 1))
                                last = mm(att[:, g, 2 * c + s, :], lhs, rhs, start=(not causal and k == 0), stop=stop)
                            if 4 * (2 * c + s) + k == 15:
                                last.then_inc(st_psum, 1)
                            beside(4 * (2 * c + s) + k)

            def values(n, bank):
                pe.wait_ge(v_sb, n + 1)
                for g in range(4):
                    if g == 0:
                        pe.wait_ge(pT_a, n + 1)
                    if g == 2:
                        pe.wait_ge(pT_b, n + 1)
                    for c in range(KC):
                        for s in range(2):
                            hd = head(g, c, s)
                            a, j = hd // 4, hd % 4
                            last = mm(ps[32 * j:32 * j + 32, bank, 128 * a:128 * a + 128], v[:, hd, :],
                                      pT[:, 4 * g + 2 * c + s, :], start=True, stop=True)
                last.then_inc(oT_psum, 1)

            def o_rows(n, bank):
                pe.wait_ge(oT_sb, n + 1)
                transposed(lambda a: oT[:, a, :], bank, 0, 4).then_inc(o_row, 1)

            def o_transposes(n, m):
                pe.wait_ge(o_sb, n + 1)
                if m is not None:
                    pe.wait_ge(v_sb, m + 1)
                transposed(lambda c: o[:, 128 * c:128 * c + 128], 5, 256, KC).then_inc(oo_psum, 1)

            def out_proj(n, base):
                pe.wait_ge(oo_split, n + 1)
                w = w_of(0, wc_hi, wc_lo, W_OUT, D, D) if base is None else w_of(base, w_hi, w_lo, W_OUT, D, D)
                split_products(ps[:, 5, 0:D], lambda c: ooh[:, c, :], lambda c: ool[:, c, :], *w,
                               KC).then_inc(proj_psum, 1)

            def x1_transposes(n):
                pe.wait_ge(x1_ready, n + 1)
                transposed(lambda c: x1[:, 128 * c:128 * c + 128], 6, 0, KC).then_inc(x1T_psum, 1)

            def hidden(n, half, base, e):
                if half == 0:
                    pe.wait_ge(x1T_hi, n + 1)
                    if not isinstance(n, int) or n > 0:
                        pe.wait_ge(res2, n)
                dst = ps[:, 7 - half, :]

                def w(t, c):
                    return t[:, ds(base + (W_L1 + 512 * half) + c * DFF, 512)]
                mm(dst, kst[0:64, ds(e * 128 + K_ROW, 128)], b1hl[:, 512 * half:512 * half + 512],
                   start=True, stop=False)
                for c in range(KC):
                    mm(dst, xh[:, c, :], w(w_hi, c), start=False, stop=False)
                    mm(dst, xh[:, c, :], w(w_lo, c), start=False, stop=False)
                if half == 0:
                    pe.wait_ge(x1T_split, n + 1)
                for c in range(KC):
                    last = mm(dst, xl[:, c, :], w(w_hi, c), start=False, stop=(c == KC - 1))
                last.then_inc(h_b if half else h_a, 1)

            def hidden_T(n, half):
                pe.wait_ge(h_sb_b if half else h_sb_a, n + 1)
                transposed(lambda j: h[:, 512 * half + 128 * j:512 * half + 128 * j + 128], 7 - half, 0,
                           4).then_inc(hT_b if half else hT_a, 1)

            def second(n, j0, j1, base):
                if j0 == 0:
                    pe.wait_ge(hl_a, n + 1)
                if j0 == 4:
                    pe.wait_ge(hl_b, n + 1)
                last = split_products(ps[:, 7, 0:D], lambda j: hh[:, j0 + j, :], lambda j: hl[:, j0 + j, :],
                                      lambda j: w_hi[:, ds(base + (W_L2 + (j0 + j) * D), D)],
                                      lambda j: w_lo[:, ds(base + (W_L2 + (j0 + j) * D), D)],
                                      j1 - j0, first=(j0 == 0), final=(j1 == FC))
                if j1 == FC:
                    last.then_inc(ff_psum, 1)

            def expert(u):
                return pe.value_load(chosen[0:1, ds(u, 1)], min_val=0, max_val=E - 1)

            def weights_of(u):
                e = expert(u)
                return e * W_EXP, e

            def block(n, m, k, f, w, next_k, next_ctx):
                wm = []

                def beside(slot):
                    if slot == 3:
                        wm.append(w(m))
                    if slot == 8 and f is not None:
                        w(f)
                    if slot == 12:
                        w(n)
                    if 4 <= slot < 16:
                        projection(m, k, wm[0] and wm[0][0], slot - 4) if slot - 4 < (12 if wm[0] is None else 9) else None
                scores_T(n, n is UNITS, beside)
                bm = wm[0] and wm[0][0]
                if f is not None:
                    wf = w(f)
                    x1_transposes(f)
                n_proj = PROJ_CAUSAL if bm is None else PROJ_QKV
                for i in range(9 if bm is not None else 12, n_proj):
                    projection(m, k, bm, i)
                if f is not None:
                    hidden(f, 0, *wf)
                bn = w(n) and w(n)[0]
                values(n, 0)
                qk_transposes(m)
                if f is not None:
                    hidden(f, 1, *wf)
                o_rows(n, 1)
                if f is not None:
                    hidden_T(f, 0)
                    hidden_T(f, 1)
                if next_k is not None:
                    pe.wait_ge(qk_split, m + 1)
                    prep(next_k, next_ctx)
                o_transposes(n, m)
                scores(m, bm is None)
                if f is not None:
                    second(f, 0, 4, wf[0])
                out_proj(n, bn)
                if f is not None:
                    second(f, 4, FC, wf[0])
                if next_k is not None:
                    pe.wait_ge(yT_ready, next_k + 1)
                shift_transpose(m)

            pe.wait_ge(g_ready, 1)
            pe.wait_ge(w_lo_ready, B)
            pe.wait_ge(w_hi_ready, B)
            pe.wait_ge(b1_ready, 2)
            pe.wait_ge(vones_ready, 2)

            def places(us):
                known = {}

                def w(u):
                    for i, x in enumerate(us):
                        if x is u:
                            if i not in known:
                                known[i] = weights_of(u)
                            return known[i]
                    return None
                return w

            prep(0, False)
            u = [0, 1, 2]
            w = places(u)
            for i in range(PROJ_QKV):
                projection(0, 0, w(0)[0], i)
            qk_transposes(0)
            scores(0, False)
            shift_transpose(0)
            block(0, 1, 0, None, w, 1, False)
            block(1, 2, 1, 0, w, None, False)
            with pe.Fori(1, B - 1) as b:
                u = [(b - 1) * 2 + 1, b * 2, b * 2 + 1, b * 2 + 2]
                w = places(u)
                block(u[1], u[2], b, u[0], w, b + 1, False)
                block(u[2], u[3], b + 1, u[1], w, None, False)
            u = [UNITS - 3, UNITS - 2, UNITS - 1]
            w = places(u)
            block(u[1], u[2], B - 1, u[0], w, B, True)
            pe.wait_ge(wc_ready, 1)
            block(u[2], UNITS, B, u[1], w, B + 1, True)
            block(UNITS, UNITS + 1, B + 1, u[2], w, B + 2, True)

            def sh_transposes(f):
                pe.wait_ge(s_y, f + C1)
                transposed(lambda c: t1[:, 128 * c:128 * c + 128], 7, 0, KC).then_inc(s_yT, 1)

            def sh_hidden(f):
                pe.wait_ge(s_ysplit, f + C1)
                split_products(ps[:, 7, 256:256 + 2 * HM], lambda c: xh[:, c, :], lambda c: xl[:, c, :],
                               *w_of(0, w_hi, w_lo, T_S12, 2 * HM, 2 * HM), KC).then_inc(s_h, 1)

            def sh_z(g):
                pe.wait_ge(s_z, g + C1)
                transposed(lambda c: h[:, 512:512 + HM], 6, 256, 1).then_inc(s_zT, 1)

            def sh_out(g):
                pe.wait_ge(s_zsplit, g + C1)
                split_products(ps[:, 6, 0:D], lambda c: hh[:, 0, :], lambda c: hl[:, 0, :],
                               *w_of(0, w_hi, w_lo, T_S3, D, D), 1).then_inc(s_o, 1)

            def block_c(b, parts, first_weights=False):
                n = b + UNITS
                def beside(slot):
                    if "next" in parts and slot < 12:
                        projection(n + 1, b + (B + 1), None, slot)
                if "att" in parts:
                    scores_T(n, True, beside)
                if "sh1" in parts:
                    sh_transposes(b - 1)
                if "next" in parts:
                    for i in range(12, PROJ_CAUSAL):
                        projection(n + 1, b + (B + 1), None, i)
                if "att" in parts:
                    if "sh2" in parts and not (isinstance(b, int) and b == 2):
                        pe.wait_ge(s_sh, b + (C1 - 3))
                    values(n, 6)
                if "next" in parts:
                    qk_transposes(n + 1)
                if "sh1" in parts:
                    if first_weights:
                        pe.wait_ge(tw_lo, 2)
                        pe.wait_ge(tw_hi, 2)
                    sh_hidden(b - 1)
                if "att" in parts:
                    o_rows(n, 6)
                if "next" in parts:
                    scores(n + 1, True)
                if "prep" in parts:
                    pe.wait_ge(qk_split, n + 2)
                    prep(b + (B + 2), True, 4)
                if "att" in parts:
                    o_transposes(n, n + 1 if "next" in parts else None)
                if "sh2" in parts:
                    sh_z(b - 2)
                if "att" in parts:
                    out_proj(n, None)
                if "sh2" in parts:
                    sh_out(b - 2)
                if "next" in parts:
                    if "prep" in parts:
                        pe.wait_ge(yT_ready, b + (B + 3))
                    shift_transpose(n + 1)

            block_c(1, ("att", "next", "prep", "sh1"), True)
            with pe.Fori(2, B - 2) as b:
                block_c(b, ("att", "next", "prep", "sh1", "sh2"))
            block_c(B - 2, ("att", "next", "sh1", "sh2"))
            block_c(B - 1, ("att", "sh1", "sh2"))
            block_c(B, ("sh1", "sh2"))
            block_c(B + 1, ("sh2",))
            pe.wait_ge(tw_lo, B)
            pe.wait_ge(tw_hi, B)

            pe.wait_ge(tg_split, 1)
            pe.wait_ge(tb_in, 16)
            with pe.Fori(0, MT) as t:
                pe.wait_ge(d_y, t + D1)
                transposed(lambda c: y[:, 128 * c:128 * c + 128], 4, 0, KC).then_inc(d_yT, 1)
                pe.wait_ge(d_ysplit, t + D1)
                split_products(ps[:, 5, 0:EM + 1], lambda c: xh[:, c, :], lambda c: xl[:, c, :],
                               lambda c: tg_h[:, c, :], lambda c: tg_l[:, c, :], KC).then_inc(d_gl, 1)
                for q in range(4):
                    last = split_products(ps[:, q, :], lambda c: xh[:, c, :], lambda c: xl[:, c, :],
                                          lambda c: w_hi[:, T_E12 + c * 2048 + 512 * q:T_E12 + c * 2048 + 512 * q + 512],
                                          lambda c: w_lo[:, T_E12 + c * 2048 + 512 * q:T_E12 + c * 2048 + 512 * q + 512], KC)
                last.then_inc(d_h, 1)
                pe.wait_ge(d_sel, t + D1)
                nc.tensor.transpose(ps[0:EM, 6, 0:128], dg[:, 7, 0:EM], ident).then_inc(d_oT, 1)
                pe.wait_ge(d_oTs, t + D1)
                mm(ps[:, 7, :], ohT, tb, start=True, stop=True).then_inc(d_bias, 1)
                pe.wait_ge(d_z, t + D1)
                transposed(lambda c: h[:, 512:512 + HM], 6, 0, 1).then_inc(d_zT, 1)
                pe.wait_ge(d_zsplit, t + D1)
                for q in range(4):
                    last = split_products(ps[:, q, :], lambda c: hh[:, 0, :], lambda c: hl[:, 0, :],
                                          lambda c: w_hi[:, T_E3 + 512 * q:T_E3 + 512 * q + 512],
                                          lambda c: w_lo[:, T_E3 + 512 * q:T_E3 + 512 * q + 512], 1)
                last.then_inc(d_o, 1)

        @block.scalar
        def _(act):
            A = nc.scalar.activation

            def copy(dst, src):
                return nc.scalar.copy(dst, src)

            act.wait_ge(cst_in, 16)
            copy(identb[:, :], ident)
            act.wait_ge(kst_in, 16)
            copy(kst[:, :], kraw).then_inc(cst_ready, 1)
            act.wait_ge(b1_zero, 1)
            act.wait_ge(b1_in, 32)
            copy(b1hl[0:E, 0:512], b1f[0])
            copy(b1hl[0:E, 512:1024], b1f[1]).then_inc(b1_hi, 1)
            with act.Fori(0, B // 2) as i:
                n = [i * 2 + (j + 1) for j in range(2)]
                for j in range(2):
                    act.wait_ge(a_T, n[j])
                    copy(yca_hi[j][:, 0:4, :], ps[:, 4 * j, :].rearrange("p (c k) -> p c k", k=128)).then_inc(a_hi, 1)
                act.wait_ge(w_in0, i * 16 + 16)
                copy(w_hi[:, ds(i * (2 * WCH), WCH)], stage[:, 0, :]).then_inc(w_hi_ready, 1)
                for j in range(2):
                    act.wait_ge(a_bias, n[j])
                    A(ta[j][:, 0:128], ta[j][:, 128:256], ACT.Exp, bias=mx[:, 8 * j + 1:8 * j + 2], scale=SCALE_A,
                      accum_out=mx[:, 8 * j + 2:8 * j + 3]).then_inc(a_p, 1)
                for j in range(2):
                    act.wait_ge(a_pT, n[j])
                    copy(h[:, 512 + 128 * j:640 + 128 * j], ps[:, 4 * j + 2, 0:128]).then_inc(a_pTs, 1)
                act.wait_ge(w_in1, i * 16 + 16)
                copy(w_hi[:, ds(i * (2 * WCH) + WCH, WCH)], stage[:, 1, :]).then_inc(w_hi_ready, 1)
            act.wait_ge(wc_in, 16)
            act.wait_ge(w_lo_ready, B)
            copy(wc_hi, wc_raw).then_inc(wc_hi_ready, 1)
            act.wait_ge(g_dve, 2)
            A(gl[:, 2, :], gl[:, 1, :], ACT.Exp).then_inc(g_exp, 1)

            def prep(k, n, bank=4):
                act.wait_ge(yT_psum, k + 1)
                copy(ycT_hi[:, 0:n, :], ps[:, bank, 0:128 * n].rearrange("p (c k) -> p c k", k=128)).then_inc(yT_hi, 1)

            def qk_hi(n):
                act.wait_ge(qkT_psum, n + 1)
                copy(qh[:, :, :], ps[:, 4, 0:D].rearrange("p (c k) -> p c k", k=128))
                kk = ps[:, 4, D:2 * D].rearrange("p (c k) -> p c k", k=128)
                for s in range(2):
                    last = A(khm[:, :, s, :], kk, ACT.Copy, scale=mask_eo[s])
                last.then_inc(qkT_hi, 1)

            def shift(n):
                act.wait_ge(mT_psum, n + 1)
                copy(mT[:, :], ps[:, 4, 0:64].bitcast(bf16)).then_inc(mT_sb, 1)

            def exps(n, between):
                act.wait_ge(st_psum, n + 1)
                for a, done in ((0, pT_a), (1, pT_b)):
                    if a:
                        between()
                    A(pT[:, 8 * a:8 * a + 8, :].rearrange("p h q -> p (h q)"),
                      ps[:, 2 * a:2 * a + 2, :].rearrange("p g k -> p (g k)"), ACT.Exp, scale=SCALE_H).then_inc(done, 1)

            def o_evict(n, bank=0):
                act.wait_ge(oT_psum, n + 1)
                copy(oT[:, :, :], ps[:, bank, :].rearrange("p (a q) -> p a q", q=128)).then_inc(oT_sb, 1)

            def oo(n):
                act.wait_ge(oo_psum, n + 1)
                copy(ooh[:, :, :], ps[:, 5, D:2 * D].rearrange("p (c k) -> p c k", k=128)).then_inc(oo_hi, 1)

            def x1_hi(n):
                act.wait_ge(x1T_psum, n + 1)
                copy(xh[:, :, :], ps[:, 6, 0:D].rearrange("p (c k) -> p c k", k=128)).then_inc(x1T_hi, 1)

            def relu(n, half):
                act.wait_ge(h_b if half else h_a, n + 1)
                A(h[:, 512 * half:512 * half + 512], ps[:, 7 - half, :], ACT.Relu).then_inc(h_sb_b if half else h_sb_a, 1)

            def h_hi(n, half):
                act.wait_ge(hT_b if half else hT_a, n + 1)
                copy(hh[:, 4 * half:4 * half + 4, :], ps[:, 7 - half, :].rearrange("p (c k) -> p c k", k=128)).then_inc(
                    hh_b if half else hh_a, 1)

            def block(n, m, f, next_k, tiles=KC):
                exps(n, lambda: x1_hi(f) if f is not None else None)
                if f is not None:
                    relu(f, 0)
                o_evict(n)
                if m is not None:
                    qk_hi(m)
                if f is not None:
                    relu(f, 1)
                    h_hi(f, 0)
                if next_k is not None:
                    prep(next_k, tiles)
                oo(n)
                if f is not None:
                    h_hi(f, 1)
                if m is not None:
                    shift(m)

            prep(0, KC)
            qk_hi(0)
            shift(0)
            block(0, 1, None, 1)
            block(1, 2, 0, None)
            with act.Fori(1, B - 1) as b:
                block(b * 2, b * 2 + 1, (b - 1) * 2 + 1, b + 1)
                block(b * 2 + 1, b * 2 + 2, b * 2, None)
            block(UNITS - 2, UNITS - 1, UNITS - 3, B, 2 * KC)
            block(UNITS - 1, UNITS, UNITS - 2, B + 1, 2 * KC)

            block(UNITS, UNITS + 1, UNITS - 1, B + 2, 2 * KC)

            def tw(c, turn, j):
                act.wait_ge(tw_in1 if j else tw_in0, turn * 16)
                copy(w_hi[:, ds(c * TCH, TCH)], tstage[:, j, :]).then_inc(tw_hi, 1)

            def sh_y(f):
                act.wait_ge(s_yT, f + C1)
                copy(xh[:, :, :], ps[:, 7, 0:D].rearrange("p (c k) -> p c k", k=128)).then_inc(s_yhi, 1)

            def sh_e(f):
                act.wait_ge(s_hb, f + C1)
                A(de[:, 0:HM], h[:, 0:HM], ACT.Exp, scale=-1.0).then_inc(s_e, 1)

            def sh_zhi(g):
                act.wait_ge(s_zT, g + C1)
                copy(hh[:, 0, :], ps[:, 6, 256:256 + HM]).then_inc(s_zhi, 1)

            def block_c(b, parts, weights):
                n = b + UNITS
                first = (lambda: sh_y(b - 1)) if "sh1" in parts else (lambda: None)
                if "att" in parts:
                    exps(n, first)
                else:
                    first()
                for w in weights:
                    tw(*w)
                if "att" in parts:
                    o_evict(n, 6)
                if "next" in parts:
                    qk_hi(n + 1)
                if "sh1" in parts:
                    sh_e(b - 1)
                if "prep" in parts:
                    prep(b + (B + 2), 2 * KC, 4)
                if "att" in parts:
                    oo(n)
                if "sh2" in parts:
                    sh_zhi(b - 2)
                if "next" in parts:
                    shift(n + 1)

            block_c(1, ("att", "next", "prep", "sh1"), [(0, 1, 0), (1, 1, 1)])
            with act.Fori(1, B // 2 - 1) as i:
                for j in range(2):
                    block_c(i * 2 + j, ("att", "next", "prep", "sh1", "sh2"), [(i * 2 + j, i + 1, j)])
            block_c(B - 2, ("att", "next", "sh1", "sh2"), [(B - 2, B // 2, 0)])
            block_c(B - 1, ("att", "sh1", "sh2"), [(B - 1, B // 2, 1)])
            block_c(B, ("sh1", "sh2"), [])
            block_c(B + 1, ("sh2",), [])

            act.wait_ge(tg_in, 16)
            copy(tg_h[:, :, :], tg[:, :, :]).then_inc(tg_hi, 1)
            act.wait_ge(d_gather, 16 * MT)
            with act.Fori(0, MT) as t:
                copy(y[:, :], comb[:, ds(t * (3 * D) + D, D)]).then_inc(d_y, 1)
                act.wait_ge(d_yT, t + D1)
                copy(xh[:, :, :], ps[:, 4, 0:D].rearrange("p (c k) -> p c k", k=128)).then_inc(d_yhi, 1)
                act.wait_ge(d_gb, t + D1)
                A(dg[:, 1, :], dg[:, 0, :], ACT.Exp, scale=-1.0).then_inc(d_ge, 1)
                act.wait_ge(d_oT, t + D1)
                copy(ohT, ps[0:EM, 6, 0:128]).then_inc(d_oTs, 1)
                act.wait_ge(d_bias, t + D1)
                copy(bsel[:, :], ps[:, 7, :]).then_inc(d_bias_sb, 1)
                act.wait_ge(d_diff, t + D1)
                A(dsm[:, 4:5], dsm[:, 3:4], ACT.Exp, scale=-1.0).then_inc(d_we, 1)
                act.wait_ge(d_hsel, t + D1)
                A(de[:, 0:HM], hsel[:, 0:HM], ACT.Exp, scale=-1.0).then_inc(d_e, 1)
                act.wait_ge(d_zT, t + D1)
                copy(hh[:, 0, :], ps[:, 6, 0:128]).then_inc(d_zhi, 1)

        @block.vector
        def _(dve):
            tt, ts, stt, cp = (nc.vector.tensor_tensor, nc.vector.tensor_scalar, nc.vector.scalar_tensor_tensor,
                               nc.vector.tensor_copy)

            def stats(src, i, n, done_stats, done_var):
                nc.vector.memset(junk[:, 0:1], 0.0)
                nc.vector.bn_stats(st[:, i, :], src).then_inc(done_stats, 1)
                dve.wait_ge(done_stats, n + 1)
                nc.vector.memset(junk[:, 1:2], 0.0)
                nc.vector.bn_aggr(mv[:, i, :], st[:, i, :]).then_inc(done_var, 1)

            def normalized(dst, src, i):
                return ts(dst, src, mv[:, i, 0:1], rs[:, i, :], ALU.subtract, ALU.mult)

            nc.vector.memset(ones[:, :], 1.0).then_inc(ones_ready, 1)
            nc.vector.memset(b1hl[:, :], 0.0).then_inc(b1_zero, 1)
            dve.wait_ge(b1_hi, 1)
            for half in range(2):
                tt(b1hl[32:32 + E, 512 * half:512 * half + 512], b1f[half], b1hl[0:E, 512 * half:512 * half + 512],
                   ALU.subtract).then_inc(b1_ready, 1)
            dve.wait_ge(b1_ready, 2)
            nc.vector.memset(v[:, :, :], 0.0).then_inc(vones_ready, 1)
            dve.wait_ge(vones_ready, 1)
            nc.vector.memset(v[:, :, HD:HD + 1], 1.0).then_inc(vones_ready, 1)

            dve.wait_ge(mask_in, 16)
            dve.wait_ge(x_in0, 16)

            def tokens_of(i):
                return [x[:, ds(i * (2 * D) + j * D, D)] for j in range(2)]

            def pair_stats(i):
                for j in range(2):
                    stats(tokens_of(i)[j], j, i * 2 + j, a_stats, a_var)

            def pair_tokens(i):
                for j in range(2):
                    dve.wait_ge(a_rstd, i * 2 + (j + 1))
                    normalized(ya[j][:, :], tokens_of(i)[j], j).then_inc(a_q, 1)
                for j in range(2):
                    m01, neg = h[:, 256 * j:256 * j + S], h[:, 256 * j + S:256 * j + 2 * S]
                    mi = mask_i[:, ds(i * (2 * S) + j * S, S)]
                    ts(m01, mi, 0.0, None, ALU.not_equal).then_inc(a_m01, 1)
                    dve.wait_ge(a_m01, i * 2 + (j + 1))
                    ts(neg, m01, 1.0, -NEG / SCALE_A, ALU.subtract, ALU.mult).then_inc(a_neg, 1)

            def gate_tokens(i):
                for j in range(2):
                    dve.wait_ge(a_grstd, i * 2 + (j + 1))
                    normalized(tg2[j][:, :], tokens_of(i)[j], 2 + j).then_inc(a_g, 1)

            def gate_means(i):
                for j in range(2):
                    dve.wait_ge(a_gm, i * 2 + (j + 1))
                    ts(gmean[:, :, ds(i * 2 + j, 1)], ps[:, 4 * j + 3, 0:KC].rearrange("p (c o) -> p c o", o=1), 1.0 / S,
                       None, ALU.mult).then_inc(a_gmean, 1)

            def pair(i, gate, following):
                n = [i * 2 + (j + 1) for j in range(2)]
                xb = tokens_of(i)
                for j in range(2):
                    dve.wait_ge(a_hi, n[j])
                    tt(yca_lo[j][:, 0:4, :], ps[:, 4 * j, :].rearrange("p (c k) -> p c k", k=128),
                       yca_hi[j][:, 0:4, :], ALU.subtract).then_inc(a_split, 1)
                if gate is not None:
                    gate_tokens(gate)
                for j in range(2):
                    dve.wait_ge(a_s, n[j])
                    dve.wait_ge(a_neg, n[j])
                    tt(tb2[j][:, 0:S], ps[:, 4 * j + 1, 0:S], h[:, 256 * j:256 * j + S], ALU.mult).then_inc(a_sm, 1)
                for j in range(2):
                    dve.wait_ge(a_sm, n[j])
                    tt(ta[j][:, 128:256], tb2[j][:, 0:S], h[:, 256 * j + S:256 * j + 2 * S], ALU.add).then_inc(a_sn, 1)
                for j in range(2):
                    dve.wait_ge(a_sn, n[j])
                    nc.vector.tensor_reduce(mx[:, 8 * j:8 * j + 1], ta[j][:, 128:256], AX.X, ALU.max).then_inc(a_max, 1)
                for j in range(2):
                    dve.wait_ge(a_max, n[j])
                    ts(mx[:, 8 * j + 1:8 * j + 2], mx[:, 8 * j:8 * j + 1], -SCALE_A, None, ALU.mult).then_inc(a_bias, 1)
                if following is not None:
                    pair_stats(following)
                if gate is not None:
                    gate_means(gate)
                for j in range(2):
                    dve.wait_ge(a_p, n[j])
                    nc.vector.reciprocal(mx[:, 8 * j + 3:8 * j + 4], mx[:, 8 * j + 2:8 * j + 3]).then_inc(a_rsum, 1)
                for j in range(2):
                    dve.wait_ge(a_rsum, n[j])
                    ts(mx[:, 8 * j + 4:8 * j + 5], mx[:, 8 * j + 3:8 * j + 4], KEEP, None, ALU.mult).then_inc(a_keep, 1)
                if following is not None:
                    pair_tokens(following)
                for j in range(2):
                    dve.wait_ge(a_keep, n[j])
                    dve.wait_ge(a_pv, n[j])
                    stt(xb[j], ps[:, 4 * j + 3, 0:D], mx[:, 8 * j + 4:8 * j + 5], xb[j], ALU.mult, ALU.add).then_inc(a_x, 1)
                for j in range(2):
                    dve.wait_ge(a_x, n[j])
                    stats(xb[j], 2 + j, i * 2 + j, a_gstats, a_gvar)

            pair_stats(0)
            pair_tokens(0)
            dve.wait_ge(x_in1, 16)
            pair(0, None, 1)
            with dve.Fori(1, PAIRS - 1) as i:
                pair(i, i - 1, i + 1)
            pair(PAIRS - 1, PAIRS - 2, None)
            gate_tokens(PAIRS - 1)
            gate_means(PAIRS - 1)

            count = [0]

            def g_link(ins):
                count[0] += 1
                ins.then_inc(g_dve, 1)
                dve.wait_ge(g_dve, count[0])
            dve.wait_ge(gw_in, 32)
            dve.wait_ge(a_gmean, B)
            for c in range(KC):
                last = tt(gprod[:, c, :, :], gmean[:, c, :].rearrange("p (b o) -> p b o", o=1).broadcast_to([128, B, E]),
                          gw[:, c:c + 1, :].broadcast_to([128, B, E]), ALU.mult)
            last.then_inc(g_prod, 1)
            dve.wait_ge(g_log, 1)

            def be(k):
                return gl[:, k, :].rearrange("p (b e) -> p b e", e=E)

            def per_b(k):
                return gs[:, k, :].rearrange("p (b o) -> p b o", o=1).broadcast_to([128, B, E])

            def const_e(c0):
                return cst[:, c0:c0 + E].rearrange("p (o e) -> p o e", o=1).broadcast_to([128, B, E])
            gb = gate_b[:, :].rearrange("p (o e) -> p o e", o=1).broadcast_to([128, B, E])
            nc.vector.tensor_tensor(be(0), ps[:, 5, 0:B * E].rearrange("p (b e) -> p b e", e=E), gb, ALU.add).then_inc(g_fill, 1)
            dve.wait_ge(g_fill, 1)
            g_link(nc.vector.tensor_reduce(gs[:, 0, :], be(0), AX.X, ALU.max))
            g_link(tt(be(1), be(0), per_b(0), ALU.subtract))
            g_link(tt(be(3), be(0), per_b(0), ALU.is_equal))
            g_link(tt(be(4), be(3), const_e(C_RNK4), ALU.mult))
            g_link(nc.vector.tensor_reduce(gs[:, 1, :], be(4), AX.X, ALU.max))
            g_link(tt(be(5), be(4), per_b(1), ALU.is_equal))
            g_link(ts(be(6), be(5), -3.0e38, None, ALU.mult))
            g_link(ts(be(7), be(5), -1.0, 1.0, ALU.mult, ALU.add))
            g_link(tt(be(8), be(0), be(7), ALU.mult))
            g_link(tt(be(8), be(8), be(6), ALU.add))
            g_link(nc.vector.tensor_reduce(gs[:, 2, :], be(8), AX.X, ALU.max))
            g_link(tt(be(3), be(8), per_b(2), ALU.is_equal))
            g_link(tt(be(4), be(3), const_e(C_RNK4), ALU.mult))
            g_link(nc.vector.tensor_reduce(gs[:, 3, :], be(4), AX.X, ALU.max))
            g_link(tt(be(9), be(4), per_b(3), ALU.is_equal))
            dve.wait_ge(g_exp, 1)
            g_link(nc.vector.tensor_reduce(gs[:, 4, :], be(2), AX.X, ALU.add))
            g_link(nc.vector.reciprocal(gs[:, 5, :], gs[:, 4, :]))
            g_link(tt(be(10), be(2), per_b(5), ALU.mult))
            slots = gate_w[:, :].rearrange("p (b s) -> p b s", s=TOPK)
            picks = chosen[:, :].rearrange("p (b s) -> p b s", s=TOPK)
            for s, k in ((0, 5), (1, 9)):
                g_link(tt(be(11), be(10), be(k), ALU.mult))
                g_link(nc.vector.tensor_reduce(slots[:, :, s], be(11), AX.X, ALU.add))
                g_link(tt(be(11), be(k), const_e(C_ID4), ALU.mult))
                g_link(nc.vector.tensor_reduce(gs[:, 6 + s, :], be(11), AX.X, ALU.add))
                g_link(cp(picks[:, :, s], gs[:, 6 + s, :]))
            dve.wait_ge(vec_in, 16 * E)
            nc.vector.memset(dsm[:, 7:8], 0.0).then_inc(g_ready, 1)

            def y_stats_of(xb, k):
                stats(xb, 0, k, y_stats, y_var)

            def y_of(xb, k, uses=None):
                dve.wait_ge(y_rstd, k + 1)
                if uses is not None:
                    dve.wait_ge(ybo_ready, uses)
                normalized(y[:, :], xb, 0).then_inc(y_ready, 1)

            def y_low(k, n, bank=4):
                dve.wait_ge(yT_hi, k + 1)
                tt(ycT_lo[:, 0:n, :], ps[:, bank, 0:128 * n].rearrange("p (c k) -> p c k", k=128), ycT_hi[:, 0:n, :],
                   ALU.subtract).then_inc(yT_ready, 1)

            def bias_qk(n, t, base):
                dve.wait_ge(qk_psum, n + 1)
                tt(qk[:, :], ps[:, 4, :], t[:, ds(base + V_QKV, 2 * D)], ALU.add).then_inc(qk_sb, 1)

            def bias_v(n, t, base):
                dve.wait_ge(v_psum, n + 1)
                if not isinstance(n, int) or n > 0:
                    dve.wait_ge(oT_psum, n)
                tt(v[:, :, 0:HD], ps[:, 5, 0:D].rearrange("p (h d) -> p h d", d=HD),
                   t[:, ds(base + (V_QKV + 2 * D), D)].rearrange("p (h d) -> p h d", d=HD), ALU.add).then_inc(v_sb, 1)

            def qk_low(n):
                dve.wait_ge(qkT_hi, n + 1)
                tt(ql[:, :, :], ps[:, 4, 0:D].rearrange("p (c k) -> p c k", k=128), qh[:, :, :], ALU.subtract)
                kk = ps[:, 4, D:2 * D].rearrange("p (c k) -> p c k", k=128)
                for s in range(2):
                    last = stt(klm[:, :, s, :], kk, mask_eo[s], khm[:, :, s, :], ALU.mult, ALU.subtract)
                last.then_inc(qk_split, 1)

            def maxima(n):
                dve.wait_ge(s_psum, n + 1)
                nc.vector.tensor_reduce(mx[:, :], att.rearrange("p g s k -> p (g s) k"), AX.X, ALU.max,
                                        negate=True).then_inc(m_max, 1)
                dve.wait_ge(m_max, n + 1)
                many = mx[:, :].rearrange("p (o h) -> p o h", o=1).broadcast_to([128, 4, H])
                cp(mtile[:, :, 0, :], many).then_inc(m_hi, 1)
                dve.wait_ge(m_hi, n + 1)
                tt(mtile[:, :, 1, :], many, mtile[:, :, 0, :], ALU.subtract).then_inc(m_split, 1)

            def o_norm(n, bank=1):
                dve.wait_ge(o_row, n + 1)
                rows = ps[:, bank, :].rearrange("p (h k) -> p h k", k=32)
                nc.vector.reciprocal(o_rs[:, :].rearrange("p (h o) -> p h o", o=1), rows[:, :, HD:HD + 1]).then_inc(o_rsum, 1)
                dve.wait_ge(o_rsum, n + 1)
                tt(o[:, :].rearrange("p (h d) -> p h d", d=HD), rows[:, :, 0:HD],
                   o_rs[:, :].rearrange("p (h o) -> p h o", o=1).broadcast_to([128, H, HD]), ALU.mult).then_inc(o_sb, 1)

            def o_low(n):
                dve.wait_ge(oo_hi, n + 1)
                tt(ool[:, :, :], ps[:, 5, D:2 * D].rearrange("p (c k) -> p c k", k=128), ooh[:, :, :],
                   ALU.subtract).then_inc(oo_split, 1)

            def sum1(n, slot):
                dve.wait_ge(proj_psum, n + 1)
                dve.wait_ge(ybo_ready, n + 1)
                tt(t1[:, :], ps[:, 5, 0:D], ybo[:, slot, :], ALU.add).then_inc(res1, 1)
                dve.wait_ge(res1, n + 1)
                stats(t1[:, :], 1, n, l1_stats, l1_var)

            def norm1(n):
                dve.wait_ge(l1_rstd, n + 1)
                if not isinstance(n, int) or n > 0:
                    dve.wait_ge(x1b_ready, n)
                normalized(x1[:, :], t1[:, :], 1).then_inc(l1_xn, 1)

            def x1_low(n):
                dve.wait_ge(x1T_hi, n + 1)
                tt(xl[:, :, :], ps[:, 6, 0:D].rearrange("p (c k) -> p c k", k=128), xh[:, :, :],
                   ALU.subtract).then_inc(x1T_split, 1)

            def h_low(n, half):
                dve.wait_ge(hh_b if half else hh_a, n + 1)
                tt(hl[:, 4 * half:4 * half + 4, :], ps[:, 7 - half, :].rearrange("p (c k) -> p c k", k=128),
                   hh[:, 4 * half:4 * half + 4, :], ALU.subtract).then_inc(hl_b if half else hl_a, 1)

            def sum2(n):
                dve.wait_ge(ff_psum, n + 1)
                dve.wait_ge(x1b_ready, n + 1)
                tt(t2[:, :], ps[:, 7, 0:D], x1b[:, :], ALU.add).then_inc(res2, 1)
                dve.wait_ge(res2, n + 1)
                stats(t2[:, :], 2, n, l2_stats, l2_var)

            def norm2(n):
                dve.wait_ge(l2_rstd, n + 1)
                normalized(y2[:, :], t2[:, :], 2).then_inc(l2_xn, 1)

            def add_expert(n, xb):
                dve.wait_ge(y2_ready, n + 1)
                stt(xb, y2[:, :], gate_w[:, ds(n, 1)], xb, ALU.mult, ALU.add).then_inc(x_acc, 1)

            def expert(u):
                return dve.value_load(chosen[0:1, ds(u, 1)], min_val=0, max_val=E - 1)

            def at(b):
                return x[:, ds(b * D, D)]

            def block(n, slot, m, f, add, next_k, next_x, causal_m=False):
                vm = (vc, 0) if causal_m else (vec, expert(m) * V_EXP)
                if next_k is not None:
                    y_stats_of(next_x, next_k)
                bias_qk(m, *vm)
                if f is not None:
                    x1_low(f)
                if add is not None:
                    add_expert(*add)
                if next_k is not None:
                    y_of(next_x, next_k, UNITS if isinstance(next_k, int) and next_k >= B else next_k * 2)
                if m is not None:
                    bias_v(m, *vm)
                    qk_low(m)
                o_norm(n)
                if f is not None:
                    h_low(f, 0)
                o_low(n)
                if f is not None:
                    h_low(f, 1)
                if next_k is not None:
                    y_low(next_k, KC if not isinstance(next_k, int) or next_k < B else 2 * KC)
                if m is not None:
                    maxima(m)
                if slot is None:
                    x3(n, n - UNITS)
                else:
                    sum1(n, slot)
                    norm1(n)
                if f is not None:
                    sum2(f)
                    norm2(f)

            def x3(n, b):
                dve.wait_ge(proj_psum, n + 1)
                dve.wait_ge(ybo_ready, n + 1)
                tt(at(b), ps[:, 5, 0:D], ybo[:, 0, :], ALU.add).then_inc(res1, 1)
                dve.wait_ge(res1, n + 1)
                stats(at(b), 1, n, s_stats, s_var)

            def sh_y(b):
                dve.wait_ge(s_rstd, b + C1)
                if not isinstance(b, int) or b > 0:
                    dve.wait_ge(s_comb, b * 32)
                normalized(t1[:, :], at(b), 1).then_inc(s_y, 1)

            def sh_low(f):
                dve.wait_ge(s_yhi, f + C1)
                tt(xl[:, :, :], ps[:, 7, 0:D].rearrange("p (c k) -> p c k", k=128), xh[:, :, :],
                   ALU.subtract).then_inc(s_ysplit, 1)

            def sh_bias(f):
                dve.wait_ge(s_h, f + C1)
                tt(h[:, 0:2 * HM], ps[:, 7, 256:256 + 2 * HM], tvec[:, U_S12:U_S12 + 2 * HM], ALU.add).then_inc(s_hb, 1)

            def sh_gated(f):
                dve.wait_ge(s_e, f + C1)
                ts(de[:, HM:2 * HM], de[:, 0:HM], 1.0, None, ALU.add).then_inc(s_e1, 1)
                dve.wait_ge(s_e1, f + C1)
                nc.vector.reciprocal(de[:, 0:HM], de[:, HM:2 * HM]).then_inc(s_r, 1)
                dve.wait_ge(s_r, f + C1)
                tt(h[:, 2 * HM:3 * HM], h[:, 0:HM], de[:, 0:HM], ALU.mult).then_inc(s_a, 1)
                dve.wait_ge(s_a, f + C1)
                tt(h[:, 3 * HM:4 * HM], h[:, 2 * HM:3 * HM], h[:, HM:2 * HM], ALU.mult).then_inc(s_g, 1)
                dve.wait_ge(s_g, f + C1)
                stats(h[:, 3 * HM:4 * HM], 2, f + UNITS, s_gst, s_gvar)

            def sh_gnorm(f):
                dve.wait_ge(s_grs, f + C1)
                normalized(h[:, 2 * HM:3 * HM], h[:, 3 * HM:4 * HM], 2).then_inc(s_gn, 1)

            def sh_zlow(g):
                dve.wait_ge(s_zhi, g + C1)
                tt(hl[:, 0, :], ps[:, 6, 256:256 + HM], hh[:, 0, :], ALU.subtract).then_inc(s_zsplit, 1)

            def sh_sum(g):
                dve.wait_ge(s_o, g + C1)
                if not isinstance(g, int) or g > 0:
                    dve.wait_ge(s_out, g * 16)
                    dve.wait_ge(s_shared, g * 16)
                tt(acc[:, :], ps[:, 6, 0:D], tvec[:, U_S3:U_S3 + D], ALU.add).then_inc(s_sh, 1)

            def block_c(b, parts):
                n = b + UNITS
                if "prep" in parts:
                    y_stats_of(at(b + 2), b + (B + 2))
                if "next" in parts:
                    bias_qk(n + 1, vc, 0)
                if "sh1" in parts:
                    sh_low(b - 1)
                if "next" in parts:
                    bias_v(n + 1, vc, 0)
                if "prep" in parts:
                    y_of(at(b + 2), b + (B + 2))
                if "next" in parts:
                    qk_low(n + 1)
                if "att" in parts:
                    o_norm(n, 6)
                if "sh1" in parts:
                    sh_bias(b - 1)
                if "prep" in parts:
                    y_low(b + (B + 2), 2 * KC, 4)
                if "att" in parts:
                    o_low(n)
                if "next" in parts:
                    maxima(n + 1)
                if "sh2" in parts:
                    sh_zlow(b - 2)
                if "att" in parts:
                    x3(n, b)
                if "sh1" in parts:
                    sh_gated(b - 1)
                if "sh2" in parts:
                    sh_sum(b - 2)
                if "att" in parts:
                    sh_y(b)
                if "sh1" in parts:
                    sh_gnorm(b - 1)

            y_stats_of(at(0), 0)
            y_of(at(0), 0)
            y_low(0, KC)
            e0 = expert(0) * V_EXP
            bias_qk(0, vec, e0)
            bias_v(0, vec, e0)
            qk_low(0)
            maxima(0)
            block(0, 0, 1, None, None, 1, at(1))
            block(1, 1, 2, 0, None, None, None)
            with dve.Fori(1, B - 1) as b:
                block(b * 2, 0, b * 2 + 1, (b - 1) * 2 + 1, ((b - 1) * 2, at(b - 1)), b + 1, at(b + 1))
                block(b * 2 + 1, 1, b * 2 + 2, b * 2, ((b - 1) * 2 + 1, at(b - 1)), None, None)
            dve.wait_ge(vc_in, 16)
            block(UNITS - 2, 0, UNITS - 1, UNITS - 3, (UNITS - 4, at(B - 2)), B, at(0))
            block(UNITS - 1, 1, UNITS, UNITS - 2, (UNITS - 3, at(B - 2)), B + 1, at(1), causal_m=True)
            block(UNITS, None, UNITS + 1, UNITS - 1, (UNITS - 2, at(B - 1)), B + 2, at(2), causal_m=True)
            sh_y(0)
            add_expert(UNITS - 1, at(B - 1))
            dve.wait_ge(tvec_in, 16)
            block_c(1, ("att", "next", "prep", "sh1"))
            with dve.Fori(2, B - 2) as b:
                block_c(b, ("att", "next", "prep", "sh1", "sh2"))
            block_c(B - 2, ("att", "next", "sh1", "sh2"))
            block_c(B - 1, ("att", "sh1", "sh2"))
            block_c(B, ("sh1", "sh2"))
            block_c(B + 1, ("sh2",))

            links = [0]

            def i_link(ins):
                links[0] += 1
                ins.then_inc(d_idx, 1)
                dve.wait_ge(d_idx, links[0])

            def rows_of(src_b, src_t, fb, ft, tmp, flat, key):
                for src, f, size in ((src_b, fb, B), (src_t, ft, S)):
                    i_link(cp(f, src))
                    i_link(ts(tmp, f, 0.0, float(size), ALU.is_lt, ALU.mult))
                    i_link(tt(f, f, tmp, ALU.add))
                i_link(ts(tmp, fb, 0.0, None, ALU.is_lt))
                i_link(ts(flat, fb, float(B - 1), None, ALU.is_gt))
                i_link(tt(tmp, tmp, flat, ALU.add))
                i_link(ts(flat, ft, 0.0, None, ALU.is_lt))
                i_link(tt(tmp, tmp, flat, ALU.add))
                i_link(ts(flat, ft, float(S - 1), None, ALU.is_gt))
                i_link(tt(tmp, tmp, flat, ALU.add))
                i_link(ts(key, tmp, float(4 * B * S), None, ALU.mult))
                i_link(ts(fb, fb, 0.0, float(B - 1), ALU.max, ALU.min))
                i_link(ts(ft, ft, 0.0, float(S - 1), ALU.max, ALU.min))
                i_link(ts(fb, fb, float(S), None, ALU.mult))
                i_link(tt(flat, fb, ft, ALU.add))
                i_link(tt(key, key, flat, ALU.add))

            dve.wait_ge(idx_in, 16 * 5)
            rows_of(idx_i[:, 0, :], idx_i[:, 1, :], ids[:, 0, :], ids[:, 1, :], ids[:, 2, :], ids[:, 3, :], ids[:, 4, :])
            i_link(cp(gidx[:, :], ids[:, 3, :]))
            nc.vector.memset(dsm[:, 6:7], 0.0).then_inc(d_gidx, 1)
            rows_of(row_i[:, 0, :], row_i[:, 1, :], row_f[:, 0, :], row_f[:, 1, :], h[:, 0:M], h[:, M:2 * M], pT[:, 0:4, :].rearrange("p h q -> p (h q)"))
            for t in range(MT):
                i_link(stt(h[:, 0:M], pT[:, 0:4, :].rearrange("p h q -> p (h q)"), ids[:, 4, t:t + 1], pos, ALU.is_equal,
                           ALU.mult))
                i_link(nc.vector.tensor_reduce(ids[:, 5, t:t + 1], h[:, 0:M], AX.X, ALU.max))
            i_link(tt(ids[:, 6, :], ids[:, 5, :], cst[:, C_M:C_M + MT], ALU.is_gt))
            i_link(ts(ids[:, 7, :], ids[:, 6, :], float(4 * B * S), None, ALU.mult))
            i_link(tt(ids[:, 8, :], ids[:, 7, :], ids[:, 4, :], ALU.add))
            i_link(cp(sidx[:, :], ids[:, 8, :]))
            nc.vector.memset(dsm[:, 6:7], 0.0).then_inc(d_sidx, 1)
            dve.wait_ge(tg_hi, 1)
            tt(tg_l[:, :, :], tg[:, :, :], tg_h[:, :, :], ALU.subtract).then_inc(tg_split, 1)

            CHAIN = 3 + 4 + 2 + 3 + (EM - 1) + 5 + EM + 2
            with dve.Fori(0, MT) as t:
                step = [0]

                def link(ins):
                    step[0] += 1
                    ins.then_inc(d_chain, 1)
                    dve.wait_ge(d_chain, t * CHAIN + step[0])
                dve.wait_ge(d_yhi, t + D1)
                tt(xl[:, :, :], ps[:, 4, 0:D].rearrange("p (c k) -> p c k", k=128), xh[:, :, :],
                   ALU.subtract).then_inc(d_ysplit, 1)
                dve.wait_ge(d_gl, t + D1)
                tt(dg[:, 0, :], ps[:, 5, 0:EM + 1], tvec[:, U_GB:U_GB + EM + 1], ALU.add).then_inc(d_gb, 1)
                dve.wait_ge(d_ge, t + D1)
                link(ts(dg[:, 2, :], dg[:, 1, :], 1.0, None, ALU.add))
                link(nc.vector.reciprocal(dg[:, 3, :], dg[:, 2, :]))
                link(tt(dg[:, 4, 0:EM], dg[:, 3, 1:EM + 1], tvec[:, U_XB:U_XB + EM], ALU.add))
                link(nc.vector.tensor_reduce(dsm[:, 0:1], dg[:, 4, 0:EM], AX.X, ALU.max))
                link(ts(dg[:, 5, 0:EM], dg[:, 4, 0:EM], dsm[:, 0:1], None, ALU.is_equal))
                link(tt(dg[:, 6, 0:EM], dg[:, 5, 0:EM], cst[:, C_RNK8:C_RNK8 + EM], ALU.mult))
                link(nc.vector.tensor_reduce(dsm[:, 1:2], dg[:, 6, 0:EM], AX.X, ALU.max))
                ts(dg[:, 7, 0:EM], dg[:, 6, 0:EM], dsm[:, 1:2], None, ALU.is_equal).then_inc(d_sel, 1)
                dve.wait_ge(d_sel, t + D1)
                link(tt(dg[:, 8, 0:EM], dg[:, 7, 0:EM], dg[:, 3, 1:EM + 1], ALU.mult))
                link(nc.vector.tensor_reduce(dsm[:, 2:3], dg[:, 8, 0:EM], AX.X, ALU.add))
                tt(dsm[:, 3:4], dg[:, 3, 0:1], dsm[:, 2:3], ALU.subtract).then_inc(d_diff, 1)
                dve.wait_ge(d_we, t + D1)
                link(ts(dsm[:, 5:6], dsm[:, 4:5], 1.0, None, ALU.add))
                link(nc.vector.reciprocal(dsm[:, 4:5], dsm[:, 5:6]))
                link(ts(dsm[:, 5:6], dsm[:, 4:5], -1.0, 1.0, ALU.mult, ALU.add))
                dve.wait_ge(d_bias_sb, t + D1)
                dve.wait_ge(d_h, t + D1)
                for e in range(EM):
                    src = bsel[:, 0:2 * HM] if e == 0 else hsel[:, :]
                    ins = stt(hsel[:, :], ps[:, e // 2, 256 * (e % 2):256 * (e % 2) + 256], dg[:, 7, e:e + 1], src,
                              ALU.mult, ALU.add)
                    if e < EM - 1:
                        link(ins)
                ins.then_inc(d_hsel, 1)
                dve.wait_ge(d_e, t + D1)
                link(ts(de[:, HM:2 * HM], de[:, 0:HM], 1.0, None, ALU.add))
                link(nc.vector.reciprocal(de[:, 0:HM], de[:, HM:2 * HM]))
                link(tt(h[:, 0:HM], hsel[:, 0:HM], de[:, 0:HM], ALU.mult))
                link(tt(h[:, HM:2 * HM], h[:, 0:HM], hsel[:, HM:2 * HM], ALU.mult))
                link(nc.vector.bn_stats(st[:, 2, :], h[:, HM:2 * HM]))
                nc.vector.memset(junk[:, 2:3], 0.0)
                nc.vector.bn_aggr(mv[:, 2, :], st[:, 2, :]).then_inc(d_var, 1)
                dve.wait_ge(d_rstd, t + D1)
                normalized(h[:, 2 * HM:3 * HM], h[:, HM:2 * HM], 2).then_inc(d_gn, 1)
                dve.wait_ge(d_zhi, t + D1)
                tt(hl[:, 0, :], ps[:, 6, 0:HM], hh[:, 0, :], ALU.subtract).then_inc(d_zsplit, 1)
                dve.wait_ge(d_o, t + D1)
                for e in range(EM):
                    src = bsel[:, 2 * HM:] if e == 0 else acc[:, :]
                    link(stt(acc[:, :], ps[:, e // 2, 256 * (e % 2):256 * (e % 2) + 256], dg[:, 7, e:e + 1], src,
                             ALU.mult, ALU.add))
                link(ts(acc[:, :], acc[:, :], dsm[:, 5:6], None, ALU.mult))
                link(stt(acc[:, :], comb[:, ds(t * (3 * D) + 2 * D, D)], dsm[:, 4:5], acc[:, :], ALU.mult, ALU.add))
                tt(finD[:, ds(t * D, D)], acc[:, :], comb[:, ds(t * (3 * D), D)], ALU.add).then_inc(d_fin, 1)
                assert step[0] == CHAIN, step[0]

        @block.gpsimd
        def _(pool):
            tt = nc.gpsimd.tensor_tensor

            def rstd(i, n, var, veps, done):
                pool.wait_ge(var, n)
                tt(rs[:, i, :], mv[:, i, 1:2], cst[:, C_EPS:C_EPS + 1], ALU.add).then_inc(veps, 1)
                pool.wait_ge(veps, n)
                tt(rs[:, i, :], rs[:, i, :], halves, ALU.pow).then_inc(done, 1)

            pool.wait_ge(cst_in, 16)

            def pair_roots(i):
                for j in range(2):
                    rstd(j, i * 2 + (j + 1), a_var, a_veps, a_rstd)

            def gate_roots(i):
                for j in range(2):
                    rstd(2 + j, i * 2 + (j + 1), a_gvar, a_gveps, a_grstd)

            def weights_low(i, j):
                pool.wait_ge(w_hi_ready, i * 2 + (j + 1))
                tt(w_lo[:, ds(i * (2 * WCH) + j * WCH, WCH)], stage[:, j, :], w_hi[:, ds(i * (2 * WCH) + j * WCH, WCH)],
                   ALU.subtract).then_inc(w_lo_ready, 1)

            pair_roots(0)
            weights_low(0, 0)
            pair_roots(1)
            weights_low(0, 1)
            with pool.Fori(1, PAIRS - 1) as i:
                gate_roots(i - 1)
                weights_low(i, 0)
                pair_roots(i + 1)
                weights_low(i, 1)
            gate_roots(PAIRS - 2)
            weights_low(PAIRS - 1, 0)
            weights_low(PAIRS - 1, 1)
            gate_roots(PAIRS - 1)
            pool.wait_ge(wc_hi_ready, 1)
            tt(wc_lo, wc_raw, wc_hi, ALU.subtract).then_inc(wc_ready, 1)

            def expert(u):
                return pool.value_load(chosen[0:1, ds(u, 1)], min_val=0, max_val=E - 1)

            def at(b):
                return x[:, ds(b * D, D)]

            def y_bias(u, k, slot, base):
                if not isinstance(u, int) or u > 0:
                    pool.wait_ge(res1, (k - 1) * 2 + (slot + 1) if not isinstance(k, int) else 2 * k + slot - 1)
                pool.wait_ge(y_ready, k + 1)
                tt(ybo[:, slot, :], y[:, :], vec[:, ds(base + V_OUT, D)], ALU.add).then_inc(ybo_ready, 1)

            def affine1(n, base):
                rstd(1, n + 1, l1_var, l1_veps, l1_rstd)
                pool.wait_ge(l1_xn, n + 1)
                tt(x1[:, :], x1[:, :], vec[:, ds(base + V_G1, D)], ALU.mult).then_inc(l1_g, 1)
                pool.wait_ge(l1_g, n + 1)
                tt(x1[:, :], x1[:, :], vec[:, ds(base + V_B1, D)], ALU.add).then_inc(x1_ready, 1)

            def x1_bias(n, base):
                pool.wait_ge(x1_ready, n + 1)
                tt(x1b[:, :], x1[:, :], vec[:, ds(base + V_L2, D)], ALU.add).then_inc(x1b_ready, 1)

            def affine2(n, base):
                pool.wait_ge(l2_xn, n + 1)
                tt(y2[:, :], y2[:, :], vec[:, ds(base + V_G2, D)], ALU.mult).then_inc(l2_g, 1)
                pool.wait_ge(l2_g, n + 1)
                tt(y2[:, :], y2[:, :], vec[:, ds(base + V_B2, D)], ALU.add).then_inc(y2_ready, 1)

            def y_root(k):
                rstd(0, k + 1, y_var, y_veps, y_rstd)

            def block(n, f, bn, bf, next_k):
                if next_k is not None:
                    y_root(next_k)
                affine1(n, bn)
                if f is not None:
                    rstd(2, f + 1, l2_var, l2_veps, l2_rstd)
                x1_bias(n, bn)
                if f is not None:
                    affine2(f, bf)

            pool.wait_ge(g_ready, 1)
            y_root(0)
            bs = [expert(u) * V_EXP for u in range(2)]
            y_bias(0, 0, 0, bs[0])
            y_bias(0, 0, 1, bs[1])
            block(0, None, bs[0], None, 1)
            block(1, 0, bs[1], bs[0], None)
            with pool.Fori(1, B - 1) as b:
                u = [(b - 1) * 2 + 1, b * 2, b * 2 + 1]
                bs = [expert(i) * V_EXP for i in u]
                y_root(b + 1)
                y_bias(u[1], b, 0, bs[1])
                y_bias(u[2], b, 1, bs[2])
                block(u[1], u[0], bs[1], bs[0], None)
                block(u[2], u[1], bs[2], bs[1], None)
            u = [UNITS - 3, UNITS - 2, UNITS - 1]
            bs = [expert(i) * V_EXP for i in u]
            y_bias(u[1], B - 1, 0, bs[1])
            y_bias(u[2], B - 1, 1, bs[2])
            block(u[1], u[0], bs[1], bs[0], B)
            block(u[2], u[1], bs[2], bs[1], B + 1)

            def x_bias(b):
                pool.wait_ge(res1, b + UNITS)
                tt(ybo[:, 0, :], at(b), vc[:, V_OUT:V_OUT + D], ALU.add).then_inc(ybo_ready, 1)

            pool.wait_ge(vc_in, 16)
            x_bias(0)
            y_root(B + 2)
            rstd(1, C1, s_var, s_veps, s_rstd)
            rstd(2, UNITS, l2_var, l2_veps, l2_rstd)
            affine2(UNITS - 1, bs[2])

            def tw(c, j):
                pool.wait_ge(tw_hi, c + 1)
                tt(w_lo[:, ds(c * TCH, TCH)], tstage[:, j, :], w_hi[:, ds(c * TCH, TCH)], ALU.subtract).then_inc(tw_lo, 1)

            def sh_affine(f):
                pool.wait_ge(s_gn, f + C1)
                tt(h[:, 512:512 + HM], h[:, 2 * HM:3 * HM], tvec[:, U_SG:U_SG + HM], ALU.mult).then_inc(s_gg, 1)
                pool.wait_ge(s_gg, f + C1)
                tt(h[:, 512:512 + HM], h[:, 512:512 + HM], tvec[:, U_SB:U_SB + HM], ALU.add).then_inc(s_z, 1)

            def sh_sum(g):
                pool.wait_ge(s_sh, g + C1)
                if not isinstance(g, int) or g > 0:
                    pool.wait_ge(s_out, g * 16)
                tt(fin[:, :], acc[:, :], at(g), ALU.add).then_inc(s_sum, 1)

            def block_c(b, parts, weights):
                if "prep" in parts:
                    y_root(b + (B + 2))
                if "att" in parts:
                    x_bias(b)
                for w in weights:
                    tw(*w)
                if "sh1" in parts:
                    rstd(2, b + (C1 - 1), s_gvar, s_gveps, s_grs)
                if "att" in parts:
                    rstd(1, b + C1, s_var, s_veps, s_rstd)
                if "sh1" in parts:
                    sh_affine(b - 1)
                if "sh2" in parts:
                    sh_sum(b - 2)

            pool.wait_ge(tvec_in, 16)
            block_c(1, ("att", "next", "prep", "sh1"), [(0, 0), (1, 1)])
            with pool.Fori(1, B // 2 - 1) as i:
                for j in range(2):
                    block_c(i * 2 + j, ("att", "next", "prep", "sh1", "sh2"), [(i * 2 + j, j)])
            block_c(B - 2, ("att", "next", "sh1", "sh2"), [(B - 2, 0)])
            block_c(B - 1, ("att", "sh1", "sh2"), [(B - 1, 1)])
            block_c(B, ("sh1", "sh2"), [])
            block_c(B + 1, ("sh2",), [])

            pool.wait_ge(s_comb, 16 * 2 * B)
            pool.wait_ge(s_shared, 16 * B)
            pool.wait_ge(d_gidx, 1)
            for t in range(MT):
                nc.gpsimd.indirect_dma_start(out=comb[:, t * 3 * D:(t + 1) * 3 * D], out_offset=None, in_=comb_d[:, :],
                                             in_offset=bass.IndirectOffsetOnAxis(ap=gidx[:, t:t + 1], axis=0)
                                             ).then_inc(d_gather, 16)
            with pool.Fori(0, MT) as t:
                rstd(2, t + D1, d_var, d_veps, d_rstd)
                pool.wait_ge(d_gn, t + D1)
                tt(h[:, 512:512 + HM], h[:, 2 * HM:3 * HM], tvec[:, U_EG:U_EG + HM], ALU.mult).then_inc(d_gg, 1)
                pool.wait_ge(d_gg, t + D1)
                tt(h[:, 512:512 + HM], h[:, 512:512 + HM], tvec[:, U_EB:U_EB + HM], ALU.add).then_inc(d_z, 1)
            pool.wait_ge(d_sidx, 1)
            pool.wait_ge(s_out, 16 * B)
            for t in range(MT):
                pool.wait_ge(d_fin, t + D1)
                nc.gpsimd.indirect_dma_start(out=out[:, :],
                                             out_offset=bass.IndirectOffsetOnAxis(ap=sidx[:, t:t + 1], axis=0),
                                             in_=finD[:, t * D:(t + 1) * D], in_offset=None,
                                             bounds_check=B * S - 1, oob_is_err=False).then_inc(d_out, 16)


def _consts(np):
    p = np.arange(128)
    c = np.zeros((128, C_ALL), np.float32)
    c[:, C_ID:C_ID + 128] = np.eye(128)
    c[:, C_ME] = (p % 32) < 16
    c[:, C_MO] = (p % 32) >= 16
    c[:, C_RNK4:C_RNK4 + E] = [4, 3, 2, 1]
    c[:, C_ID4:C_ID4 + E] = [0, 1, 2, 3]
    c[:, C_RNK8:C_RNK8 + EM] = [8, 7, 6, 5, 4, 3, 2, 1]
    c[:, C_M:C_M + MT] = p[:, None] + 128 * np.arange(MT)[None, :]
    c[:, C_HALF] = -0.5
    c[:, C_EPS] = EPS
    k = np.zeros((128, K_ALL), np.float32)
    for s in range(4):
        k[:, K_SEL + 128 * s:K_SEL + 128 * (s + 1)] = ((p % 16) == 4 * (p // 32) + s)[:, None]
    k[:, K_CS:K_CS + 128] = np.where(p[None, :] > p[:, None], -1e30, 0)
    k[:, K_CT:K_CT + 128] = np.where(p[:, None] > p[None, :], -1e30, 0)
    for e in range(E):
        k[[e, 32 + e], K_ROW + 128 * e:K_ROW + 128 * (e + 1)] = 1
    return c, k, np.arange(M, dtype=np.float32)[None, :]


def _chunks(np, w):
    n = w.shape[0] // 128
    return np.concatenate([w[128 * c:128 * (c + 1)] for c in range(n)], axis=1)


def kernel(**inputs):
    import numpy as np
    import concourse.bacc as bacc
    from concourse.bass_utils import run_bass_kernel_spmd

    a = {k: np.asarray(v) for k, v in inputs.items()}
    f0 = {k[7:]: v for k, v in a.items() if k.startswith("L0_ffn_")}
    at = {k[9:]: v for k, v in a.items() if k.startswith("L1_xattn_")}
    f1 = {k[7:]: v for k, v in a.items() if k.startswith("L1_ffn_")}
    tokens = lambda t: np.ascontiguousarray(t.transpose(1, 0, 2).reshape(S, B * D))
    cat = np.concatenate
    w = cat([cat([_chunks(np, f0["in_proj_w"][e].T), _chunks(np, f0["out_proj_w"][e].T),
                  _chunks(np, f0["lin1_w"][e].T), _chunks(np, f0["lin2_w"][e].T)], axis=1) for e in range(E)], axis=1)
    wc = cat([_chunks(np, cat([at["Wq"], at["Wk"], at["Wv"]]).T), _chunks(np, at["Wo"].T)], axis=1)
    vec = cat([cat([f0["in_proj_b"][e], f0["out_proj_b"][e], f0["lin2_b"][e], f0["ln1_w"][e], f0["ln1_b"][e],
                    f0["ln2_w"][e], f0["ln2_b"][e]]) for e in range(E)])[None, :]
    vc = cat([at["bq"], at["bk"], at["bv"], at["bo"]])[None, :]
    e12 = cat([cat([f1["ew1"][e], f1["ew2"][e]]).T for e in range(EM)], axis=1)
    tw = cat([_chunks(np, cat([f1["sw1"], f1["sw2"]]).T), _chunks(np, f1["sw3"].T), _chunks(np, e12),
              cat([f1["ew3"][e].T for e in range(EM)], axis=1)], axis=1)
    tvec = cat([f1["sb1"], f1["sb2"], f1["sb3"], f1["s_ln_g"], f1["s_ln_b"], f1["sel_ln_g"], f1["sel_ln_b"],
                f1["sg_b"], f1["eg_b"], f1["exp_bias"]])[None, :]
    tg = cat([f1["sg_w"], f1["eg_w"]]).T.reshape(KC, 128, EM + 1).transpose(1, 0, 2)
    tb = cat([f1["eb1"], f1["eb2"], f1["eb3"]], axis=1)
    cst, kst, pos = _consts(np)
    arrays = {
        "x": tokens(a["x"]), "ctx": tokens(a["ctx_1024"]), "mask": a["mask_Bx1xS2_ik1"].reshape(1, B * S),
        "w": w, "wc": wc, "vec": vec, "vc": vc, "b1": f0["lin1_b"],
        "gw": f0["gate_w"].T.reshape(KC, 128, E).transpose(1, 0, 2), "gb": f0["gate_b"][None, :],
        "tw": tw, "tvec": tvec, "tg": tg, "tb": tb,
        "ib": f1["index_b"].reshape(MT, 128).T, "it": f1["index_t"].reshape(MT, 128).T,
        "ibr": f1["index_b"][None, :], "itr": f1["index_t"][None, :], "cst": cst, "kst": kst, "pos": pos,
    }
    arrays = {f"in_{k}": np.ascontiguousarray(v) for k, v in arrays.items()}
    nc = bacc.Bacc("TRN2", target_bir_lowering=False, num_devices=1)
    args = [nc.dram_tensor(k, v.shape, mybir.dt.from_np(v.dtype), kind="ExternalInput").ap() for k, v in arrays.items()]
    out = nc.dram_tensor("out", (B * S, D), mybir.dt.float32, kind="ExternalOutput").ap()
    comb = nc.dram_tensor("comb", (B * S, 3 * D), mybir.dt.float32, kind="Internal").ap()
    encoder_kernel(nc, *args, out, comb)
    r = run_bass_kernel_spmd(nc, [arrays], core_ids=[0])
    return np.asarray(r.results[0]["out"]).reshape(B, S, D)
```

```python
import concourse.bass as bass
from concourse import mybir
from contextlib import ExitStack

B, S, D = 16, 128, 256
KC = D // 128
H, HD = 16, 16
E, TOPK = 4, 2
DFF = 1024
FC = DFF // 128
EM, HM, M = 8, 128, 512
MT = M // 128
UNITS = B * TOPK
EPS = 1e-5
NEG = -1e10
SCALE_A = 0.25
KEEP = 1.0 / (1.0 - 0.1 / (256 * 512))
SCALE_H = HD ** -0.5

W_QKV, W_OUT, W_L1, W_L2 = 0, KC * 3 * D, KC * 4 * D, KC * 4 * D + KC * DFF
W_EXP = W_L2 + FC * D
W_ALL = E * W_EXP
WCH = W_ALL // B
W_CAUS = KC * 4 * D
T_S12, T_S3 = 0, KC * 2 * HM
T_E12 = T_S3 + D
T_E3 = T_E12 + KC * EM * 2 * HM
T_ALL = T_E3 + EM * D
TCH = T_ALL // B
V_QKV, V_OUT, V_L2, V_G1, V_B1, V_G2, V_B2 = 0, 768, 1024, 1280, 1536, 1792, 2048
V_EXP = 2304
V_ALL = E * V_EXP
U_S12, U_S3, U_SG, U_SB, U_EG, U_EB, U_GB, U_XB = 0, 256, 512, 640, 768, 896, 1024, 1033
U_ALL = U_XB + EM
R_STAGE, R_TVEC, R_COMB = 0, 2 * TCH + 160, 2304
R_FIN = R_COMB + MT * 3 * D
C_ID, C_ME, C_MO, C_RNK4, C_ID4, C_RNK8, C_M, C_HALF, C_EPS = 0, 128, 129, 130, 134, 138, 146, 150, 151
C_ALL = 152
K_SEL, K_CS, K_CT, K_ROW = 0, 512, 640, 768
K_ALL = K_ROW + E * 128


def encoder_kernel(nc, x_d, ctx_d, mask_d, w_d, wc_d, vec_d, vc_d, b1_d, gw_d, gb_d, tw_d, tvec_d, tg_d, tb_d,
                   ib_d, it_d, ibr_d, itr_d, cst_d, kst_d, pos_d, out, comb_d, shared_d):
    f32, bf16, i32 = mybir.dt.float32, mybir.dt.bfloat16, mybir.dt.int32
    ALU = mybir.AluOpType
    ACT = mybir.ActivationFunctionType
    AX = mybir.AxisListType
    ds = bass.ds

    stack = ExitStack()
    with stack:
        def sb(name, shape, dt=f32):
            return stack.enter_context(nc.sbuf_tensor(name, shape, dt))

        ps = stack.enter_context(nc.psum_tensor("ps", [128, 8, 512], f32))

        x = sb("x", [128, B * D])
        w_hi = sb("w_hi", [128, W_ALL], bf16)
        w_lo = sb("w_lo", [128, W_ALL], bf16)
        vec = sb("vec", [128, V_ALL])
        b1hl = sb("b1hl", [64, DFF], bf16)
        cst = sb("cst", [128, C_ALL])
        identb = sb("identb", [128, 128], bf16)
        kst = sb("kst", [128, K_ALL], bf16)
        gate_b = sb("gate_b", [128, E])
        ones = sb("ones", [128, 128])
        gmean = sb("gmean", [128, KC, B])
        gw = sb("gw", [128, KC, E])
        gate_w = sb("gate_w", [128, UNITS])
        chosen = sb("chosen", [128, UNITS], i32)

        y = sb("y", [128, D])
        ycT_hi = sb("ycT_hi", [128, 2 * KC, 128], bf16)
        ycT_lo = sb("ycT_lo", [128, 2 * KC, 128], bf16)
        qk = sb("qk", [128, 2 * D])
        v = sb("v", [128, H, 32])
        qh = sb("qh", [128, KC, 128], bf16)
        ql = sb("ql", [128, KC, 128], bf16)
        khm = sb("khm", [128, KC, 2, 128], bf16)
        klm = sb("klm", [128, KC, 2, 128], bf16)
        mx = sb("mx", [128, H])
        mtile = sb("mtile", [128, 4, 2, H], bf16)
        mT = sb("mT", [128, 128], bf16)
        pT = sb("pT", [128, H, 128])
        o_rs = sb("o_rs", [128, H])
        o = sb("o", [128, D])
        ooh = sb("ooh", [128, KC, 128], bf16)
        ool = sb("ool", [128, KC, 128], bf16)
        ybo = sb("ybo", [128, 2, D])
        t1 = sb("t1", [128, D])
        ctxb = sb("ctxb", [128, 2, D])
        oT = ctxb[:, :, :].rearrange("p j (a q) -> p (j a) q", q=128)
        ctxc = sb("ctxc", [128, D])
        x1 = sb("x1", [128, D])
        x1b = sb("x1b", [128, D])
        xh = sb("xh", [128, KC, 128], bf16)
        xl = sb("xl", [128, KC, 128], bf16)
        h = sb("h", [128, DFF])
        hh = sb("hh", [128, FC, 128], bf16)
        hl = sb("hl", [128, FC, 128], bf16)
        t2 = sb("t2", [128, D])
        y2 = sb("y2", [128, D])
        st = sb("st", [128, 4, 6])
        mv = sb("mv", [128, 4, 2])
        rs = sb("rs", [128, 4, 1])
        junk = sb("junk", [128, 3])
        mask_i = pT[:, :, :].rearrange("p h q -> p (h q)").bitcast(i32)
        stage = sb("stage", [128, 2, WCH])
        kraw = vec[:, 0:K_ALL]
        gl = h[:, 0:12 * B * E].rearrange("p (k j) -> p k j", j=B * E)
        gprod = h[:, 768:768 + KC * B * E].rearrange("p (c b e) -> p c b e", b=B, e=E)
        gs = h[:, 896:896 + 8 * B].rearrange("p (k b) -> p k b", b=B)
        wc_raw = pT[:, :, :].rearrange("p h q -> p (h q)")
        stage_b = stage[:, :, :].rearrange("p a w -> p (a w)").bitcast(bf16)
        wc_hi, wc_lo = stage_b[:, 0:W_CAUS], stage_b[:, W_CAUS:2 * W_CAUS]
        vc = stage[:, :, :].rearrange("p a w -> p (a w)")[:, W_CAUS:W_CAUS + 4 * D]
        tstage = vec[:, R_STAGE:R_STAGE + 2 * TCH].rearrange("p (a w) -> p a w", a=2)
        tvec = vec[:, R_TVEC:R_TVEC + U_ALL]
        acc, fin = x1b, x1
        comb = vec[:, R_COMB:R_COMB + MT * 3 * D]
        rows = w_lo[:, W_ALL - 16 * M:].bitcast(f32).rearrange("p (k m) -> p k m", m=M)
        row_i, row_f, pos = rows[:, 0:2, :].bitcast(i32), rows[:, 2:4, :], rows[:, 4, :]
        row_tmp, row_flat, row_key = rows[:, 5, :], rows[:, 6, :], rows[:, 7, :]
        finD = vec[:, R_FIN:R_FIN + MT * D]
        idx_i = sb("idx_i", [128, 2, MT], i32)

        def sem(name):
            return stack.enter_context(nc.semaphore(name))

        (x_in0, x_in1, x_in2, ctx_in00, ctx_in01, ctx_in10, ctx_in11, cst_in, kst_in, mask_in, w_in0, w_in1, vec_in, b1_in, gw_in, wc_in, vc_in,
         tvec_in) = (sem(n) for n in (
             "x_in0", "x_in1", "x_in2", "ctx_in00", "ctx_in01", "ctx_in10", "ctx_in11", "cst_in", "kst_in", "mask_in", "w_in0", "w_in1", "vec_in", "b1_in",
             "gw_in", "wc_in", "vc_in", "tvec_in"))
        ctx_in = ((ctx_in00, ctx_in01), (ctx_in10, ctx_in11))
        cst_ready, ones_ready, vones_ready, b1_zero, b1_hi, b1_ready, w_hi_ready, w_lo_ready, wc_hi_ready, wc_ready = (
            sem(n) for n in ("cst_ready", "ones_ready", "vones_ready", "b1_zero", "b1_hi", "b1_ready", "w_hi_ready",
                             "w_lo_ready", "wc_hi_ready", "wc_ready"))
        (a_stats, a_var, a_veps, a_rstd, a_q, a_T, a_hi, a_split, a_s, a_m01, a_neg, a_sm, a_sn, a_max, a_bias,
         a_p, a_pT, a_pTs, a_pv, a_rsum, a_keep, a_x, a_gstats, a_gvar, a_gveps, a_grstd, a_g, a_gm, a_gmean) = (
            sem("a_" + n) for n in ("stats", "var", "veps", "rstd", "q", "T", "hi", "split", "s", "m01", "neg", "sm",
                                    "sn", "max", "bias", "p", "pT", "pTs", "pv", "rsum", "keep", "x", "gstats", "gvar",
                                    "gveps", "grstd", "g", "gm", "gmean"))
        g_prod, g_log, g_fill, g_dve, g_exp, g_ready = (
            sem("g_" + n) for n in ("prod", "log", "fill", "dve", "exp", "ready"))
        (y_stats, y_var, y_veps, y_rstd, y_ready, yT_psum, yT_hi, yT_ready) = (
            sem("y_" + n) for n in ("stats", "var", "veps", "rstd", "ready", "T_psum", "T_hi", "T_ready"))
        (qk_psum, v_psum, qk_sb, v_sb, qkT_psum, qkT_hi, qk_split, s_psum, m_max, m_hi, m_split, mT_psum, mT_sb, st_psum,
         pT_a, pT_b, oT_psum, oT_sb, o_row, o_rsum, o_sb, oo_psum, oo_hi, oo_split, proj_psum, ybo_ready) = (
            sem(n) for n in ("qk_psum", "v_psum", "qk_sb", "v_sb", "qkT_psum", "qkT_hi", "qk_split", "s_psum", "m_max", "m_hi",
                             "m_split", "mT_psum", "mT_sb", "st_psum", "pT_a", "pT_b", "oT_psum", "oT_sb", "o_row",
                             "o_rsum", "o_sb", "oo_psum", "oo_hi", "oo_split", "proj_psum", "ybo_ready"))
        (res1, l1_stats, l1_var, l1_veps, l1_rstd, l1_xn, l1_g, x1_ready, x1b_ready) = (
            sem(n) for n in ("res1", "l1_stats", "l1_var", "l1_veps", "l1_rstd", "l1_xn", "l1_g", "x1_ready",
                             "x1b_ready"))
        (x1T_psum, x1T_hi, x1T_split, h_a, h_b, h_sb_a, h_sb_b, hT_a, hT_b, hh_a, hh_b, hl_a, hl_b, ff_psum,
         res2, l2_stats, l2_var, l2_veps, l2_rstd, l2_xn, l2_g, y2_ready, x_acc) = (
            sem(n) for n in ("x1T_psum", "x1T_hi", "x1T_split", "h_a", "h_b", "h_sb_a", "h_sb_b", "hT_a", "hT_b",
                             "hh_a", "hh_b", "hl_a", "hl_b", "ff_psum", "res2", "l2_stats", "l2_var", "l2_veps",
                             "l2_rstd", "l2_xn", "l2_g", "y2_ready", "x_acc"))
        c_ctx, tw_in0, tw_in1, tw_hi, tw_lo, s_comb, s_shared, s_out = (
            sem("c_" + n) for n in ("ctx", "tw_in0", "tw_in1", "tw_hi", "tw_lo", "comb", "shared", "out"))
        s_stats, s_var, s_veps, s_rstd, s_y, s_yT, s_yhi, s_ysplit, s_h, s_hb, s_e, s_e1, s_r, s_a = (
            l1_stats, l1_var, l1_veps, l1_rstd, l1_xn, x1T_psum, x1T_hi, x1T_split, h_a, h_sb_a, h_b, h_sb_b, l1_g, hT_a)
        s_g, s_gst, s_gvar, s_gveps, s_grs, s_gn, s_gg, s_z, s_zT, s_zhi, s_zsplit, s_o, s_sh, s_sum = (
            hT_b, l2_stats, l2_var, l2_veps, l2_rstd, l2_xn, l2_g, y2_ready, hh_b, hh_a, hl_a, ff_psum, res2, x1_ready)
        tg_in, tb_in, idx_in, row_in, tg_hi, tg_split, d_gidx, d_sidx, d_idx, d_gather, d_gshared, d_chain, d_out = (
            sem("d_" + n) for n in ("tg_in", "tb_in", "idx_in", "row_in", "tg_hi", "tg_split", "gidx", "sidx", "idx", "gather", "gshared",
                                    "chain", "out"))
        d_xT, d_xhi, d_xsplit, d_gl, d_gb, d_ge, d_sel, d_diff, d_we, d_oT, d_oTs = (
            a_T, a_hi, a_split, a_s, a_bias, a_p, a_max, a_keep, a_pTs, a_pT, a_m01)
        d_bc, d_ohb, d_xm, d_h, d_e, d_var, d_veps, d_rstd, d_gn, d_gg, d_z, d_zT, d_zhi, d_zsplit, d_zm, d_o, d_fin = (
            a_pv, a_neg, a_gm, a_x, a_rsum, a_var, a_veps, a_rstd, a_q, a_g, a_sm, a_sn, a_gstats, a_gvar, a_grstd,
            a_gmean, a_gveps)
        C1, D1 = UNITS + 1, B + 1

        tg = sb("tg", [128, KC, EM + 1])
        tg_h = sb("tg_h", [128, KC, EM + 1], bf16)
        tg_l = sb("tg_l", [128, KC, EM + 1], bf16)
        tb = v[0:EM, :, :].rearrange("p h k -> p (h k)")
        ids = sb("ids", [128, 10, MT])
        gidx = sb("gidx", [128, MT], i32)
        sidx = sb("sidx", [128, MT], i32)
        dg = stage[:, 0, 0:9 * MT * (EM + 1)].rearrange("p (k t e) -> p k t e", k=9, t=MT)
        dsm = sb("dsm", [128, 8, MT])
        de = y2
        ohT = h[0:EM, 512:512 + M]
        ohTb = o[0:EM, :].bitcast(bf16)
        free = T_ALL
        ohb = w_hi[:, free:free + MT * EM * 128].rearrange("p (t e k) -> p t e k", t=MT, k=128)
        free += MT * EM * 128
        xm = w_hi[:, free:free + 2 * EM * 2 * KC * 128].rearrange("p (a e c k) -> p a e c k", a=2, e=EM, k=128)
        free += 2 * EM * 2 * KC * 128
        zm = w_hi[:, free:free + 2 * EM * 2 * 128].rearrange("p (a e c k) -> p a e c k", a=2, e=EM, k=128)
        xT = w_lo[:, T_ALL:T_ALL + MT * 2 * KC * 128].rearrange("p (t c k) -> p t c k", t=MT, k=128)
        zT = w_lo[:, T_ALL + 2048:T_ALL + 2560].rearrange("p (a c k) -> p a c k", a=2, k=128)

        ident = cst[:, C_ID:C_ID + 128]
        mask_eo = [cst[:, C_ME:C_ME + 1], cst[:, C_MO:C_MO + 1]]
        att = ps[:, 0:4, :].rearrange("p g (s k) -> p g s k", k=128)

        selb = kst[:, K_SEL:K_SEL + 512].rearrange("p (s k) -> p s k", k=128)
        causb = kst[:, K_CS:K_CS + 256].rearrange("p (s k) -> p s k", k=128)
        halves = cst[:, C_HALF:C_HALF + 1]

        def head(g, c, s):
            return 8 * c + 2 * g + s

        b1f = [v[0:E, :, :].rearrange("p h k -> p (h k)"), qk[0:E, :]]
        ya, ta, tb2, tg2 = (y, y2), (t1, o), (t2, ybo[:, 0, :]), (x1, x1b)
        ctx_a = ((ctxb[:, 0, :], ctxb[:, 1, :]), (ctxc[:, :], ybo[:, 1, :]))
        PAIRS = B // 2
        yca_hi, yca_lo = (ycT_hi, hh), (ycT_lo, hl)

        block = stack.enter_context(nc.Block())

        @block.sync
        def _(sp):
            sp.dma_start(x[:, 0:2 * D], x_d[:, 0:2 * D]).then_inc(x_in0, 16)
            sp.dma_start(cst[:, :], cst_d).then_inc(cst_in, 16)
            sp.dma_start(ctx_a[0][0], ctx_d[:, 0:D]).then_inc(ctx_in[0][0], 16)
            sp.dma_start(ctx_a[0][1], ctx_d[:, D:2 * D]).then_inc(ctx_in[0][1], 16)
            sp.dma_start(stage[:, 0, :], w_d[:, 0:WCH]).then_inc(w_in0, 16)
            sp.dma_start(mask_i, mask_d.broadcast_to([128, B * S])).then_inc(mask_in, 16)
            sp.dma_start(stage[:, 1, :], w_d[:, WCH:2 * WCH]).then_inc(w_in1, 16)
            sp.dma_start(x[:, 2 * D:4 * D], x_d[:, 2 * D:4 * D]).then_inc(x_in1, 16)
            sp.dma_start(ctx_a[1][0], ctx_d[:, 2 * D:3 * D]).then_inc(ctx_in[1][0], 16)
            sp.dma_start(ctx_a[1][1], ctx_d[:, 3 * D:4 * D]).then_inc(ctx_in[1][1], 16)
            sp.dma_start(kraw, kst_d).then_inc(kst_in, 16)
            sp.dma_start(x[:, 4 * D:], x_d[:, 4 * D:]).then_inc(x_in2, 16)
            sp.dma_start(idx_i[:, 0, :], ib_d).then_inc(idx_in, 16)
            sp.dma_start(idx_i[:, 1, :], it_d).then_inc(idx_in, 16)
            sp.dma_start(gw[:, :, :], gw_d).then_inc(gw_in, 16)
            sp.dma_start(gate_b[:, :], gb_d.broadcast_to([128, E])).then_inc(gw_in, 16)
            for half in range(2):
                sp.dma_start(b1f[half], b1_d[:, 512 * half:512 * half + 512]).then_inc(b1_in, 16)
            sp.wait_ge(cst_ready, 1)

            def bias_rows(e):
                sp.dma_start(vec[:, ds(e * V_EXP, V_EXP)],
                             vec_d[:, ds(e * V_EXP, V_EXP)].broadcast_to([128, V_EXP])).then_inc(vec_in, 16)

            def next_of_pair(i, parity, with_ctx):
                for j in range(2):
                    sp.wait_ge(w_lo_ready, i * 2 + (j + 1))
                    sp.dma_start(stage[:, j, :], w_d[:, ds(i * (2 * WCH) + (2 + j) * WCH, WCH)]).then_inc(
                        w_in1 if j else w_in0, 16)
                    if with_ctx:
                        sp.wait_ge(a_x, i * 2 + (j + 1))
                        sp.dma_start(ctx_a[parity][j], ctx_d[:, ds(i * (2 * D) + (4 + j) * D, D)]).then_inc(
                            ctx_in[parity][j], 16)
            assert E == PAIRS // 2
            with sp.Fori(0, PAIRS // 2 - 1) as p:
                bias_rows(p)
                next_of_pair(p * 2, 0, True)
                next_of_pair(p * 2 + 1, 1, True)
            bias_rows(E - 1)
            next_of_pair(PAIRS - 2, 0, False)
            sp.wait_ge(a_neg, B)
            sp.dma_start(wc_raw, wc_d).then_inc(wc_in, 16)
            sp.wait_ge(w_lo_ready, B)
            sp.dma_start(vc, vc_d.broadcast_to([128, 4 * D])).then_inc(vc_in, 16)
            sp.wait_ge(a_x, B)
            sp.dma_start(ctxc[:, :], ctx_d[:, 0:D]).then_inc(c_ctx, 16)
            sp.wait_ge(yT_psum, B + 1)
            sp.dma_start(ctxc[:, :], ctx_d[:, D:2 * D]).then_inc(c_ctx, 16)
            sp.wait_ge(yT_psum, B + 2)
            sp.dma_start(ctxc[:, :], ctx_d[:, 2 * D:3 * D]).then_inc(c_ctx, 16)
            sp.wait_ge(y2_ready, UNITS)
            sp.dma_start(tstage[:, 0, :], tw_d[:, 0:TCH]).then_inc(tw_in0, 16)
            sp.dma_start(tstage[:, 1, :], tw_d[:, TCH:2 * TCH]).then_inc(tw_in1, 16)
            sp.dma_start(tvec, tvec_d.broadcast_to([128, U_ALL])).then_inc(tvec_in, 16)
            sp.dma_start(tg[:, :, :], tg_d).then_inc(tg_in, 16)
            sp.dma_start(row_i[:, 0, :], ibr_d.broadcast_to([128, M])).then_inc(row_in, 16)
            sp.dma_start(row_i[:, 1, :], itr_d.broadcast_to([128, M])).then_inc(row_in, 16)
            sp.dma_start(pos, pos_d.broadcast_to([128, M])).then_inc(row_in, 16)

            def next_weights(c, j):
                sp.wait_ge(tw_lo, c - 1)
                sp.dma_start(tstage[:, j, :], tw_d[:, ds(c * TCH, TCH)]).then_inc(tw_in1 if j else tw_in0, 16)

            def next_context(b):
                sp.wait_ge(yT_psum, b + B)
                sp.dma_start(ctxc[:, :], ctx_d[:, ds(b * D, D)]).then_inc(c_ctx, 16)

            def put_tokens(b):
                sp.wait_ge(s_y, b + C1)
                sp.dma_start(comb_d[ds(b * S, S), 0:D], x[:, ds(b * D, D)]).then_inc(s_comb, 16)
                sp.dma_start(comb_d[ds(b * S, S), D:2 * D], t1[:, :]).then_inc(s_comb, 16)

            def put_shared(b):
                sp.wait_ge(s_sum, b + C1)
                sp.dma_start(shared_d[ds(b * S, S), :], acc[:, :]).then_inc(s_shared, 16)
                sp.dma_start(out[ds(b * S, S), :], fin[:, :]).then_inc(s_out, 16)

            next_context(3)
            put_tokens(0)
            next_weights(2, 0)
            next_weights(3, 1)
            next_context(4)
            put_tokens(1)
            with sp.Fori(1, B // 2 - 2) as j:
                for i in range(2):
                    b = j * 2 + i
                    put_shared(j * 2 + (i - 2) if i != 0 else (j - 1) * 2)
                    next_weights(j * 2 + (i + 2), i)
                    next_context(j * 2 + (i + 3))
                    put_tokens(b)
            for b in range(B - 4, B + 2):
                put_shared(b - 2)
                if b + 2 < B:
                    next_weights(b + 2, b % 2)
                if b + 3 < B:
                    next_context(b + 3)
                if b < B:
                    put_tokens(b)
            sp.wait_ge(oT_psum, UNITS + B)
            sp.dma_start(tb, tb_d).then_inc(tb_in, 16)
            sp.wait_ge(s_comb, 16 * 2 * B)
            sp.wait_ge(s_shared, 16 * (B + 1))
            sp.wait_ge(s_out, 16 * (B + 1))
            sp.wait_ge(d_out, 16 * MT)

        @block.tensor
        def _(pe):
            mm = nc.tensor.matmul

            def transposed(src, bank, c0, n):
                for j in range(n):
                    last = nc.tensor.transpose(ps[:, bank, c0 + 128 * j:c0 + 128 * (j + 1)], src(j), ident)
                return last

            def split_products(dst, lhs_hi, lhs_lo, rhs_hi, rhs_lo, chunks, first=True, final=True):
                for j in range(chunks):
                    mm(dst, lhs_hi(j), rhs_hi(j), start=(first and j == 0), stop=False)
                    mm(dst, lhs_lo(j), rhs_hi(j), start=False, stop=False)
                    last = mm(dst, lhs_hi(j), rhs_lo(j), start=False, stop=(final and j == chunks - 1))
                return last

            pe.wait_ge(cst_in, 16)
            pe.wait_ge(ones_ready, 1)

            def gate_means(i):
                for j in range(2):
                    pe.wait_ge(a_g, i * 2 + (j + 1))
                    for c in range(KC):
                        last = mm(ps[:, 4 * j + 3, c:c + 1], tg2[j][:, 128 * c:128 * c + 128], ones[:, 0:1],
                                  start=True, stop=True)
                    last.then_inc(a_gm, 1)

            def pair(i, parity, gate, turn):
                n = [i * 2 + (j + 1) for j in range(2)]
                ctx = ctx_a[parity]
                for j in range(2):
                    pe.wait_ge(a_q, n[j])
                    pe.wait_ge(ctx_in[parity][j], turn * 16)
                    transposed(lambda c: ya[j][:, 128 * c:128 * c + 128], 4 * j, 0, KC)
                    transposed(lambda c: ctx[j][:, 128 * c:128 * c + 128], 4 * j, 256, KC).then_inc(a_T, 1)
                for j in range(2):
                    pe.wait_ge(a_split, n[j])
                    split_products(ps[:, 4 * j + 1, 0:128], lambda c: yca_hi[j][:, c, :], lambda c: yca_lo[j][:, c, :],
                                   lambda c: yca_hi[j][:, KC + c, :], lambda c: yca_lo[j][:, KC + c, :],
                                   KC).then_inc(a_s, 1)
                if gate is not None:
                    gate_means(gate)
                for j in range(2):
                    pe.wait_ge(a_p, n[j])
                    transposed(lambda c: ta[j][:, 0:128], 4 * j + 2, 0, 1).then_inc(a_pT, 1)
                for j in range(2):
                    pe.wait_ge(a_pTs, n[j])
                    if gate is not None:
                        pe.wait_ge(a_gmean, gate * 2 + (j + 1))
                    mm(ps[:, 4 * j + 3, 0:D], h[:, 512 + 128 * j:640 + 128 * j], ctx[j],
                       start=True, stop=True).then_inc(a_pv, 1)

            pair(0, 0, None, 1)
            with pe.Fori(0, PAIRS // 2 - 1) as p:
                pair(p * 2 + 1, 1, p * 2, p + 1)
                pair(p * 2 + 2, 0, p * 2 + 1, p + 2)
            pair(PAIRS - 1, 1, PAIRS - 2, PAIRS // 2)
            gate_means(PAIRS - 1)
            pe.wait_ge(g_prod, 1)
            for c in range(KC):
                last = mm(ps[:, 5, 0:B * E], ones[:, :], gprod[:, c, :, :].rearrange("p b e -> p (b e)"),
                          start=(c == 0), stop=(c == KC - 1))
            last.then_inc(g_log, 1)

            def dense(bank, count):
                for _ in range(count):
                    mm(ps[:, bank, :], identb[:, :], kst[:, 0:512], start=True, stop=True)

            def prep(k, with_ctx, bank=4):
                pe.wait_ge(y_ready, k + 1)
                last = transposed(lambda c: y[:, 128 * c:128 * c + 128], bank, 0, KC)
                if with_ctx:
                    pe.wait_ge(c_ctx, (k - (B - 1)) * 16)
                    last = transposed(lambda c: ctxc[:, 128 * c:128 * c + 128], bank, 256, KC)
                last.then_inc(yT_psum, 1)

            def w_of(base, wh, wl, off, stride, width):
                return (lambda c: wh[:, ds(base + off + c * stride, width)],
                        lambda c: wl[:, ds(base + off + c * stride, width)])

            PROJ_QKV, PROJ_CAUSAL = 12, 18

            def projection(n, k, base, i):
                if i == 0:
                    pe.wait_ge(yT_ready, k + 1)
                j, part = i // 3, i % 3
                if base is None:
                    kind, c = j // KC, j % KC
                    src = c if kind == 0 else KC + c
                    dst = ps[:, 5, 0:D] if kind == 2 else ps[:, 4, D * kind:D * kind + D]
                    off, width, wh, wl = W_QKV + kind * D + c * 3 * D, D, wc_hi, wc_lo
                else:
                    kind, c = (0 if j < KC else 2), j % KC
                    src = c
                    dst = ps[:, 5, 0:D] if kind == 2 else ps[:, 4, :]
                    off, width, wh, wl = base + (W_QKV + kind * D + c * 3 * D), (D if kind == 2 else 2 * D), w_hi, w_lo
                if kind == 2 and c == 0 and part == 0 and (not isinstance(n, int) or n > 1):
                    pe.wait_ge(res1, n - 1)
                lhs = (ycT_hi, ycT_lo, ycT_hi)[part][:, src, :]
                rhs = (wh, wh, wl)[part][:, ds(off, width)]
                ins = mm(dst, lhs, rhs, start=(c == 0 and part == 0), stop=(c == KC - 1 and part == 2))
                if c == KC - 1 and part == 2 and kind != 0:
                    ins.then_inc(v_psum if kind == 2 else qk_psum, 1)
                elif c == KC - 1 and part == 2 and base is not None:
                    ins.then_inc(qk_psum, 1)

            def qk_transposes(n):
                pe.wait_ge(qk_sb, n + 1)
                transposed(lambda c: qk[:, 128 * c:128 * c + 128], 4, 0, 2 * KC).then_inc(qkT_psum, 1)

            def scores(n, causal):
                pe.wait_ge(qkT_hi, n + 1)
                if causal:
                    for g in range(4):
                        mm(ps[:, g, :], identb[:, :], causb[:, 0:1, :].broadcast_to([128, 4, 128]),
                           start=True, stop=False)
                for c in range(KC):
                    for g in range(4):
                        r = slice(32 * g, 32 * g + 32)
                        last = mm(att[:, g, 2 * c:2 * c + 2, :], qh[r, c, :], khm[r, c, :, :],
                                  start=not causal, stop=(not causal or c == KC - 1))
                last.then_inc(s_psum, 1)

            def shift_transpose(n):
                pe.wait_ge(m_split, n + 1)
                nc.tensor.transpose(ps[:, 4, 0:64].bitcast(bf16),
                                    mtile[:, :, :, :].rearrange("p r a h -> p (r a h)"), identb[:, :]).then_inc(mT_psum, 1)

            def scores_T(n, causal, beside=lambda slot: None):
                pe.wait_ge(qk_split, n + 1)
                pe.wait_ge(mT_sb, n + 1)
                if causal:
                    for g in range(4):
                        mm(ps[:, g, :], identb[:, :], causb[:, 1:2, :].broadcast_to([128, 4, 128]),
                           start=True, stop=False)
                for c in range(KC):
                    for s in range(2):
                        terms = ((khm, qh), (khm, ql), (klm, qh), (None, None))
                        for k, (kt, qt) in enumerate(terms):
                            for g in range(4):
                                r = slice(32 * g, 32 * g + 32)
                                lhs = selb[r, 2 * c + s, :] if kt is None else kt[r, c, s, :]
                                rhs = mT[r, :] if qt is None else qt[r, c, :]
                                stop = k == 3 and (not causal or (c == KC - 1 and s == 1))
                                last = mm(att[:, g, 2 * c + s, :], lhs, rhs, start=(not causal and k == 0), stop=stop)
                            if 4 * (2 * c + s) + k == 15:
                                last.then_inc(st_psum, 1)
                            beside(4 * (2 * c + s) + k)

            def values(n, bank):
                pe.wait_ge(v_sb, n + 1)
                for g in range(4):
                    if g == 0:
                        pe.wait_ge(pT_a, n + 1)
                    if g == 2:
                        pe.wait_ge(pT_b, n + 1)
                    for c in range(KC):
                        for s in range(2):
                            hd = head(g, c, s)
                            a, j = hd // 4, hd % 4
                            last = mm(ps[32 * j:32 * j + 32, bank, 128 * a:128 * a + 128], v[:, hd, :],
                                      pT[:, 4 * g + 2 * c + s, :], start=True, stop=True)
                last.then_inc(oT_psum, 1)

            def o_rows(n, bank):
                pe.wait_ge(oT_sb, n + 1)
                transposed(lambda a: oT[:, a, :], bank, 0, 4).then_inc(o_row, 1)

            def o_transposes(n, m):
                pe.wait_ge(o_sb, n + 1)
                if m is not None:
                    pe.wait_ge(v_sb, m + 1)
                transposed(lambda c: o[:, 128 * c:128 * c + 128], 5, 256, KC).then_inc(oo_psum, 1)

            def out_proj(n, base):
                pe.wait_ge(oo_split, n + 1)
                w = w_of(0, wc_hi, wc_lo, W_OUT, D, D) if base is None else w_of(base, w_hi, w_lo, W_OUT, D, D)
                split_products(ps[:, 5, 0:D], lambda c: ooh[:, c, :], lambda c: ool[:, c, :], *w,
                               KC).then_inc(proj_psum, 1)

            def x1_transposes(n):
                pe.wait_ge(x1_ready, n + 1)
                transposed(lambda c: x1[:, 128 * c:128 * c + 128], 6, 0, KC).then_inc(x1T_psum, 1)

            def hidden(n, half, base, e):
                if half == 0:
                    pe.wait_ge(x1T_hi, n + 1)
                    if not isinstance(n, int) or n > 0:
                        pe.wait_ge(res2, n)
                dst = ps[:, 7 - half, :]

                def w(t, c):
                    return t[:, ds(base + (W_L1 + 512 * half) + c * DFF, 512)]
                mm(dst, kst[0:64, ds(e * 128 + K_ROW, 128)], b1hl[:, 512 * half:512 * half + 512],
                   start=True, stop=False)
                for c in range(KC):
                    mm(dst, xh[:, c, :], w(w_hi, c), start=False, stop=False)
                    mm(dst, xh[:, c, :], w(w_lo, c), start=False, stop=False)
                if half == 0:
                    pe.wait_ge(x1T_split, n + 1)
                for c in range(KC):
                    last = mm(dst, xl[:, c, :], w(w_hi, c), start=False, stop=(c == KC - 1))
                last.then_inc(h_b if half else h_a, 1)

            def hidden_T(n, half):
                pe.wait_ge(h_sb_b if half else h_sb_a, n + 1)
                transposed(lambda j: h[:, 512 * half + 128 * j:512 * half + 128 * j + 128], 7 - half, 0,
                           4).then_inc(hT_b if half else hT_a, 1)

            def second(n, j0, j1, base):
                if j0 == 0:
                    pe.wait_ge(hl_a, n + 1)
                if j0 == 4:
                    pe.wait_ge(hl_b, n + 1)
                last = split_products(ps[:, 7, 0:D], lambda j: hh[:, j0 + j, :], lambda j: hl[:, j0 + j, :],
                                      lambda j: w_hi[:, ds(base + (W_L2 + (j0 + j) * D), D)],
                                      lambda j: w_lo[:, ds(base + (W_L2 + (j0 + j) * D), D)],
                                      j1 - j0, first=(j0 == 0), final=(j1 == FC))
                if j1 == FC:
                    last.then_inc(ff_psum, 1)

            def expert(u):
                return pe.value_load(chosen[0:1, ds(u, 1)], min_val=0, max_val=E - 1)

            def weights_of(u):
                e = expert(u)
                return e * W_EXP, e

            def places(u):
                known = {}

                def place(j):
                    if j not in known:
                        known[j] = weights_of(u[j])
                    return known[j]
                return place

            def block(u, j, k, place, next_k, causal_n=False, causal_m=False):
                n, m = u[j], u[j + 1]
                f = u[j - 1] if j > 0 else None

                def m_base():
                    return None if causal_m else place(j + 1)[0]

                def beside(slot):
                    if slot == 8 and f is not None:
                        place(j - 1)
                    if slot == 12 and not causal_n:
                        place(j)
                    if 2 <= slot < 14:
                        projection(m, k, m_base(), slot - 2)
                    if slot == 1:
                        m_base()
                    if slot == 14 and f is not None:
                        x1_transposes(f)
                scores_T(n, causal_n, beside)
                if causal_m:
                    for i in range(12, PROJ_CAUSAL):
                        projection(m, k, None, i)
                if f is not None:
                    hidden(f, 0, *place(j - 1))
                qk_transposes(m)
                values(n, 0)
                if f is not None:
                    hidden(f, 1, *place(j - 1))
                o_rows(n, 1)
                if f is not None:
                    hidden_T(f, 0)
                    hidden_T(f, 1)
                if next_k is not None:
                    pe.wait_ge(qk_split, m + 1)
                    prep(next_k, isinstance(next_k, int) and next_k >= B)
                o_transposes(n, m)
                scores(m, causal_m)
                if f is not None:
                    second(f, 0, 4, place(j - 1)[0])
                out_proj(n, None if causal_n else place(j)[0])
                if f is not None:
                    second(f, 4, FC, place(j - 1)[0])
                if next_k is not None:
                    pe.wait_ge(yT_ready, next_k + 1)
                if f is not None:
                    dense(6, 2)
                shift_transpose(m)
                if f is not None:
                    dense(6, 1)

            pe.wait_ge(g_ready, 1)
            pe.wait_ge(w_lo_ready, B)
            pe.wait_ge(w_hi_ready, B)
            pe.wait_ge(b1_ready, 2)
            pe.wait_ge(vones_ready, 2)
            prep(0, False)
            u = [0, 1, 2]
            place = places(u)
            for i in range(PROJ_QKV):
                projection(0, 0, place(0)[0], i)
            qk_transposes(0)
            scores(0, False)
            shift_transpose(0)
            block(u, 0, 0, place, 1)
            block(u, 1, 1, place, None)
            with pe.Fori(1, B - 1) as b:
                u = [(b - 1) * 2 + 1, b * 2, b * 2 + 1, b * 2 + 2]
                place = places(u)
                block(u, 1, b, place, b + 1)
                block(u, 2, b + 1, place, None)
            u = [UNITS - 3, UNITS - 2, UNITS - 1, UNITS, UNITS + 1]
            place = places(u)
            block(u, 1, B - 1, place, B)
            pe.wait_ge(wc_ready, 1)
            block(u, 2, B, place, B + 1, causal_m=True)
            block(u, 3, B + 1, place, B + 2, causal_n=True, causal_m=True)

            def sh_transposes(f):
                pe.wait_ge(s_y, f + C1)
                transposed(lambda c: t1[:, 128 * c:128 * c + 128], 7, 0, KC).then_inc(s_yT, 1)

            def sh_hidden(f):
                pe.wait_ge(s_ysplit, f + C1)
                split_products(ps[:, 7, 256:256 + 2 * HM], lambda c: xh[:, c, :], lambda c: xl[:, c, :],
                               *w_of(0, w_hi, w_lo, T_S12, 2 * HM, 2 * HM), KC).then_inc(s_h, 1)

            def sh_z(g):
                pe.wait_ge(s_z, g + C1)
                transposed(lambda c: h[:, 512:512 + HM], 6, 256, 1).then_inc(s_zT, 1)

            def sh_out(g):
                pe.wait_ge(s_zsplit, g + C1)
                split_products(ps[:, 6, 0:D], lambda c: hh[:, 0, :], lambda c: hl[:, 0, :],
                               *w_of(0, w_hi, w_lo, T_S3, D, D), 1).then_inc(s_o, 1)

            def block_c(b, parts, first_weights=False):
                n = b + UNITS
                def beside(slot):
                    if slot == 13 and "sh1" in parts:
                        sh_transposes(b - 1)
                    if "next" in parts and slot < 12:
                        projection(n + 1, b + (B + 1), None, slot)
                if "att" in parts:
                    scores_T(n, True, beside)
                if "sh1" in parts and "att" not in parts:
                    sh_transposes(b - 1)
                if "next" in parts:
                    for i in range(12, PROJ_CAUSAL):
                        projection(n + 1, b + (B + 1), None, i)
                if "next" in parts:
                    qk_transposes(n + 1)
                if "att" in parts:
                    if "sh2" in parts and not (isinstance(b, int) and b == 2):
                        pe.wait_ge(s_sh, b + (C1 - 3))
                    values(n, 6)
                if "sh1" in parts:
                    if first_weights:
                        pe.wait_ge(tw_lo, 2)
                        pe.wait_ge(tw_hi, 2)
                    sh_hidden(b - 1)
                if "att" in parts:
                    o_rows(n, 6)
                if "next" in parts:
                    scores(n + 1, True)
                if "prep" in parts:
                    pe.wait_ge(qk_split, n + 2)
                    prep(b + (B + 2), True, 4)
                if "next" in parts and "sh1" in parts:
                    pe.wait_ge(s_hb, b + (C1 - 1))
                    dense(7, 1)
                if "att" in parts:
                    o_transposes(n, n + 1 if "next" in parts else None)
                if "sh2" in parts:
                    sh_z(b - 2)
                if "att" in parts:
                    out_proj(n, None)
                if "sh2" in parts:
                    sh_out(b - 2)
                if "next" in parts:
                    if "prep" in parts:
                        pe.wait_ge(yT_ready, b + (B + 3))
                    if "sh1" in parts:
                        pe.wait_ge(s_hb, b + (C1 - 1))
                    dense(7, 4)
                    shift_transpose(n + 1)
                    dense(7, 2)

            block_c(1, ("att", "next", "prep", "sh1"), True)
            with pe.Fori(2, B - 2) as b:
                block_c(b, ("att", "next", "prep", "sh1", "sh2"))
            block_c(B - 2, ("att", "next", "sh1", "sh2"))
            block_c(B - 1, ("att", "sh1", "sh2"))
            block_c(B, ("sh1", "sh2"))
            block_c(B + 1, ("sh2",))
            pe.wait_ge(tw_lo, B)
            pe.wait_ge(tw_hi, B)

            pe.wait_ge(d_gather, 16 * MT)
            for t in range(MT):
                last = transposed(lambda c: comb[:, t * 3 * D + D + 128 * c:t * 3 * D + D + 128 * c + 128], 4 + t // 2,
                                  256 * (t % 2), KC)
                if t % 2:
                    last.then_inc(d_xT, 1)
            pe.wait_ge(tg_split, 1)
            for t in range(MT):
                pe.wait_ge(d_xsplit, D1 + t // 2)
                last = split_products(ps[:, 3, 16 * t:16 * t + EM + 1], lambda c: xT[:, t, c, :],
                                      lambda c: xT[:, t, KC + c, :], lambda c: tg_h[:, c, :], lambda c: tg_l[:, c, :], KC)
            last.then_inc(d_gl, 1)
            dense(0, 0)
            pe.wait_ge(d_sel, D1)
            for t in range(MT):
                last = nc.tensor.transpose(ps[0:EM, 4, 128 * t:128 * t + 128], dg[:, 7, t, 0:EM], ident)
            last.then_inc(d_oT, 1)
            pe.wait_ge(d_oTs, D1 + 1)
            pe.wait_ge(tb_in, 16)

            def choice(t):
                if t > 0:
                    pe.wait_ge(d_ohb, D1 + t - 1)
                for e in range(EM):
                    last = mm(ps[:, 6 + e // 4, 128 * (e % 4):128 * (e % 4) + 128],
                              identb[0:EM, e:e + 1].broadcast_to([EM, 128]), ohTb[:, 128 * t:128 * t + 128],
                              start=True, stop=True)
                last.then_inc(d_bc, 1)

            def chosen_products(dst, bias, t, masked, chunks, w0, stride):
                mm(dst, ohT[:, 128 * t:128 * t + 128], bias, start=True, stop=False)
                for e in range(EM):
                    for c in range(chunks):
                        w = slice(w0 + c * stride + D * e, w0 + c * stride + D * e + D)
                        mm(dst, masked[:, e, c, :], w_hi[:, w], start=False, stop=False)
                        mm(dst, masked[:, e, chunks + c, :], w_hi[:, w], start=False, stop=False)
                        last = mm(dst, masked[:, e, c, :], w_lo[:, w], start=False, stop=(e == EM - 1 and c == chunks - 1))
                return last

            def chosen_hidden(t):
                pe.wait_ge(d_xm, D1 + t)
                chosen_products(ps[:, t % 2, 0:2 * HM], tb[:, 0:2 * HM], t, xm[:, t % 2], KC, T_E12,
                                EM * 2 * HM).then_inc(d_h, 1)

            def chosen_z(t):
                pe.wait_ge(d_z, D1 + t)
                transposed(lambda c: y[:, 128 * (t % 2):128 * (t % 2) + 128], 4 + t % 2, 0, 1).then_inc(d_zT, 1)

            def chosen_out(t):
                pe.wait_ge(d_zm, D1 + t)
                if t >= 2:
                    pe.wait_ge(d_fin, D1 + t - 2)
                chosen_products(ps[:, 2 + t % 2, 0:D], tb[:, 2 * HM:2 * HM + D], t, zm[:, t % 2], 1, T_E3,
                                0).then_inc(d_o, 1)

            assert MT == 4
            for step, t in ((choice, 0), (choice, 1), (chosen_hidden, 0), (choice, 2), (chosen_hidden, 1), (choice, 3),
                            (chosen_z, 0), (chosen_hidden, 2), (chosen_out, 0), (chosen_z, 1), (chosen_hidden, 3),
                            (chosen_out, 1), (chosen_z, 2), (chosen_out, 2), (chosen_z, 3), (chosen_out, 3)):
                step(t)

        @block.scalar
        def _(act):
            A = nc.scalar.activation

            def copy(dst, src):
                return nc.scalar.copy(dst, src)

            act.wait_ge(cst_in, 16)
            copy(identb[:, :], ident)

            def pair(i):
                n = [i * 2 + (j + 1) for j in range(2)]
                for j in range(2):
                    act.wait_ge(a_T, n[j])
                    copy(yca_hi[j][:, 0:4, :], ps[:, 4 * j, :].rearrange("p (c k) -> p c k", k=128)).then_inc(a_hi, 1)
                act.wait_ge(w_in0, i * 16 + 16)
                copy(w_hi[:, ds(i * (2 * WCH), WCH)], stage[:, 0, :]).then_inc(w_hi_ready, 1)
                for j in range(2):
                    act.wait_ge(a_bias, n[j])
                    A(ta[j][:, 0:128], ta[j][:, 128:256], ACT.Exp, bias=mx[:, 8 * j + 1:8 * j + 2], scale=SCALE_A,
                      accum_out=mx[:, 8 * j + 2:8 * j + 3]).then_inc(a_p, 1)
                for j in range(2):
                    act.wait_ge(a_pT, n[j])
                    copy(h[:, 512 + 128 * j:640 + 128 * j], ps[:, 4 * j + 2, 0:128]).then_inc(a_pTs, 1)
                act.wait_ge(w_in1, i * 16 + 16)
                copy(w_hi[:, ds(i * (2 * WCH) + WCH, WCH)], stage[:, 1, :]).then_inc(w_hi_ready, 1)

            pair(0)
            act.wait_ge(kst_in, 16)
            copy(kst[:, :], kraw).then_inc(cst_ready, 1)
            with act.Fori(1, PAIRS) as i:
                pair(i)
            act.wait_ge(b1_zero, 1)
            act.wait_ge(b1_in, 32)
            copy(b1hl[0:E, 0:512], b1f[0])
            copy(b1hl[0:E, 512:1024], b1f[1]).then_inc(b1_hi, 1)
            act.wait_ge(wc_in, 16)
            act.wait_ge(w_lo_ready, B)
            copy(wc_hi, wc_raw).then_inc(wc_hi_ready, 1)
            act.wait_ge(g_dve, 2)
            A(gl[:, 2, :], gl[:, 1, :], ACT.Exp).then_inc(g_exp, 1)

            def prep(k, n, bank=4):
                act.wait_ge(yT_psum, k + 1)
                copy(ycT_hi[:, 0:n, :], ps[:, bank, 0:128 * n].rearrange("p (c k) -> p c k", k=128)).then_inc(yT_hi, 1)

            def qk_hi(n):
                act.wait_ge(qkT_psum, n + 1)
                copy(qh[:, :, :], ps[:, 4, 0:D].rearrange("p (c k) -> p c k", k=128))
                kk = ps[:, 4, D:2 * D].rearrange("p (c k) -> p c k", k=128)
                for s in range(2):
                    last = A(khm[:, :, s, :], kk, ACT.Copy, scale=mask_eo[s])
                last.then_inc(qkT_hi, 1)

            def shift(n):
                act.wait_ge(mT_psum, n + 1)
                copy(mT[:, :], ps[:, 4, 0:64].bitcast(bf16)).then_inc(mT_sb, 1)

            def exps(n):
                act.wait_ge(st_psum, n + 1)
                for a, done in ((0, pT_a), (1, pT_b)):
                    A(pT[:, 8 * a:8 * a + 8, :].rearrange("p h q -> p (h q)"),
                      ps[:, 2 * a:2 * a + 2, :].rearrange("p g k -> p (g k)"), ACT.Exp, scale=SCALE_H).then_inc(done, 1)

            def o_evict(n, bank=0):
                act.wait_ge(oT_psum, n + 1)
                copy(oT[:, :, :], ps[:, bank, :].rearrange("p (a q) -> p a q", q=128)).then_inc(oT_sb, 1)

            def oo(n):
                act.wait_ge(oo_psum, n + 1)
                copy(ooh[:, :, :], ps[:, 5, D:2 * D].rearrange("p (c k) -> p c k", k=128)).then_inc(oo_hi, 1)

            def x1_hi(n):
                act.wait_ge(x1T_psum, n + 1)
                copy(xh[:, :, :], ps[:, 6, 0:D].rearrange("p (c k) -> p c k", k=128)).then_inc(x1T_hi, 1)

            def relu(n, half):
                act.wait_ge(h_b if half else h_a, n + 1)
                A(h[:, 512 * half:512 * half + 512], ps[:, 7 - half, :], ACT.Relu).then_inc(h_sb_b if half else h_sb_a, 1)

            def h_hi(n, half):
                act.wait_ge(hT_b if half else hT_a, n + 1)
                copy(hh[:, 4 * half:4 * half + 4, :], ps[:, 7 - half, :].rearrange("p (c k) -> p c k", k=128)).then_inc(
                    hh_b if half else hh_a, 1)

            def block(n, m, f, next_k, tiles=KC):
                if f is not None:
                    x1_hi(f)
                exps(n)
                if f is not None:
                    relu(f, 0)
                if m is not None:
                    qk_hi(m)
                o_evict(n)
                if f is not None:
                    relu(f, 1)
                    h_hi(f, 0)
                if next_k is not None:
                    prep(next_k, tiles)
                oo(n)
                if f is not None:
                    h_hi(f, 1)
                if m is not None:
                    shift(m)

            prep(0, KC)
            qk_hi(0)
            shift(0)
            block(0, 1, None, 1)
            block(1, 2, 0, None)
            with act.Fori(1, B - 1) as b:
                block(b * 2, b * 2 + 1, (b - 1) * 2 + 1, b + 1)
                block(b * 2 + 1, b * 2 + 2, b * 2, None)
            block(UNITS - 2, UNITS - 1, UNITS - 3, B, 2 * KC)
            block(UNITS - 1, UNITS, UNITS - 2, B + 1, 2 * KC)

            block(UNITS, UNITS + 1, UNITS - 1, B + 2, 2 * KC)

            def tw(c, turn, j):
                act.wait_ge(tw_in1 if j else tw_in0, turn * 16)
                copy(w_hi[:, ds(c * TCH, TCH)], tstage[:, j, :]).then_inc(tw_hi, 1)

            def sh_y(f):
                act.wait_ge(s_yT, f + C1)
                copy(xh[:, :, :], ps[:, 7, 0:D].rearrange("p (c k) -> p c k", k=128)).then_inc(s_yhi, 1)

            def sh_e(f):
                act.wait_ge(s_hb, f + C1)
                A(de[:, 0:HM], h[:, 0:HM], ACT.Exp, scale=-1.0).then_inc(s_e, 1)

            def sh_zhi(g):
                act.wait_ge(s_zT, g + C1)
                copy(hh[:, 0, :], ps[:, 6, 256:256 + HM]).then_inc(s_zhi, 1)

            def block_c(b, parts, weights):
                n = b + UNITS
                if "sh1" in parts:
                    sh_y(b - 1)
                if "att" in parts:
                    exps(n)
                for w in weights:
                    tw(*w)
                if "next" in parts:
                    qk_hi(n + 1)
                if "att" in parts:
                    o_evict(n, 6)
                if "sh1" in parts:
                    sh_e(b - 1)
                if "prep" in parts:
                    prep(b + (B + 2), 2 * KC, 4)
                if "att" in parts:
                    oo(n)
                if "sh2" in parts:
                    sh_zhi(b - 2)
                if "next" in parts:
                    shift(n + 1)

            block_c(1, ("att", "next", "prep", "sh1"), [(0, 1, 0), (1, 1, 1)])
            with act.Fori(1, B // 2 - 1) as i:
                for j in range(2):
                    block_c(i * 2 + j, ("att", "next", "prep", "sh1", "sh2"), [(i * 2 + j, i + 1, j)])
            block_c(B - 2, ("att", "next", "sh1", "sh2"), [(B - 2, B // 2, 0)])
            block_c(B - 1, ("att", "sh1", "sh2"), [(B - 1, B // 2, 1)])
            block_c(B, ("sh1", "sh2"), [])
            block_c(B + 1, ("sh2",), [])

            act.wait_ge(tg_in, 16)
            copy(tg_h[:, :, :], tg[:, :, :]).then_inc(tg_hi, 1)
            for i in range(2):
                act.wait_ge(d_xT, D1 + i)
                copy(xT[:, 2 * i:2 * i + 2, 0:KC, :],
                     ps[:, 4 + i, :].rearrange("p (t c k) -> p t c k", t=2, k=128)).then_inc(d_xhi, 1)
            act.wait_ge(d_gb, D1)
            A(dg[:, 1, :, :], dg[:, 0, :, :], ACT.Exp, scale=-1.0).then_inc(d_ge, 1)
            act.wait_ge(d_oT, D1)
            copy(ohTb, ps[0:EM, 4, :]).then_inc(d_oTs, 1)
            copy(ohT, ps[0:EM, 4, :]).then_inc(d_oTs, 1)
            act.wait_ge(d_diff, D1)
            A(dsm[:, 4, :], dsm[:, 3, :], ACT.Exp, scale=-1.0).then_inc(d_we, 1)

            def choice(t):
                act.wait_ge(d_bc, D1 + t)
                copy(ohb[:, t, :, :], ps[:, 6:8, :].rearrange("p a (e k) -> p (a e) k", k=128)).then_inc(d_ohb, 1)

            def hidden_exp(t):
                act.wait_ge(d_h, D1 + t)
                copy(qk[:, 256 * (t % 2):256 * (t % 2) + 256], ps[:, t % 2, 0:2 * HM])
                A(de[:, HM * (t % 2):HM * (t % 2) + HM], ps[:, t % 2, 0:HM], ACT.Exp, scale=-1.0).then_inc(d_e, 1)

            def z_hi(t):
                act.wait_ge(d_zT, D1 + t)
                copy(zT[:, t % 2, 0, :], ps[:, 4 + t % 2, 0:HM]).then_inc(d_zhi, 1)

            for step, t in ((choice, 0), (choice, 1), (choice, 2), (hidden_exp, 0), (choice, 3), (hidden_exp, 1),
                            (z_hi, 0), (hidden_exp, 2), (z_hi, 1), (hidden_exp, 3), (z_hi, 2), (z_hi, 3)):
                step(t)

        @block.vector
        def _(dve):
            tt, ts, stt, cp = (nc.vector.tensor_tensor, nc.vector.tensor_scalar, nc.vector.scalar_tensor_tensor,
                               nc.vector.tensor_copy)

            def stats(src, i, n, done_stats, done_var):
                nc.vector.memset(junk[:, 0:1], 0.0)
                nc.vector.bn_stats(st[:, i, :], src).then_inc(done_stats, 1)
                dve.wait_ge(done_stats, n + 1)
                nc.vector.memset(junk[:, 1:2], 0.0)
                nc.vector.bn_aggr(mv[:, i, :], st[:, i, :]).then_inc(done_var, 1)

            def normalized(dst, src, i):
                return ts(dst, src, mv[:, i, 0:1], rs[:, i, :], ALU.subtract, ALU.mult)

            nc.vector.memset(ones[:, :], 1.0).then_inc(ones_ready, 1)
            nc.vector.memset(junk[:, 0:1], 0.0).then_inc(s_shared, 16)
            nc.vector.memset(junk[:, 1:2], 0.0).then_inc(s_out, 16)
            dve.wait_ge(s_shared, 16)
            dve.wait_ge(s_out, 16)
            dve.wait_ge(x_in0, 16)

            def tokens_of(i):
                return [x[:, ds(i * (2 * D) + j * D, D)] for j in range(2)]

            def pair_stats(i):
                for j in range(2):
                    stats(tokens_of(i)[j], j, i * 2 + j, a_stats, a_var)

            def pair_tokens(i):
                for j in range(2):
                    dve.wait_ge(a_rstd, i * 2 + (j + 1))
                    normalized(ya[j][:, :], tokens_of(i)[j], j).then_inc(a_q, 1)
                for j in range(2):
                    m01, neg = h[:, 256 * j:256 * j + S], h[:, 256 * j + S:256 * j + 2 * S]
                    mi = mask_i[:, ds(i * (2 * S) + j * S, S)]
                    ts(m01, mi, 0.0, None, ALU.not_equal).then_inc(a_m01, 1)
                    dve.wait_ge(a_m01, i * 2 + (j + 1))
                    ts(neg, m01, 1.0, -NEG / SCALE_A, ALU.subtract, ALU.mult).then_inc(a_neg, 1)

            def gate_tokens(i):
                for j in range(2):
                    dve.wait_ge(a_grstd, i * 2 + (j + 1))
                    normalized(tg2[j][:, :], tokens_of(i)[j], 2 + j).then_inc(a_g, 1)

            def gate_means(i):
                for j in range(2):
                    dve.wait_ge(a_gm, i * 2 + (j + 1))
                    ts(gmean[:, :, ds(i * 2 + j, 1)], ps[:, 4 * j + 3, 0:KC].rearrange("p (c o) -> p c o", o=1), 1.0 / S,
                       None, ALU.mult).then_inc(a_gmean, 1)

            def pair(i, gate, following):
                n = [i * 2 + (j + 1) for j in range(2)]
                xb = tokens_of(i)
                for j in range(2):
                    dve.wait_ge(a_hi, n[j])
                    tt(yca_lo[j][:, 0:4, :], ps[:, 4 * j, :].rearrange("p (c k) -> p c k", k=128),
                       yca_hi[j][:, 0:4, :], ALU.subtract).then_inc(a_split, 1)
                if gate is not None:
                    gate_tokens(gate)
                for j in range(2):
                    dve.wait_ge(a_s, n[j])
                    dve.wait_ge(a_neg, n[j])
                    tt(tb2[j][:, 0:S], ps[:, 4 * j + 1, 0:S], h[:, 256 * j:256 * j + S], ALU.mult).then_inc(a_sm, 1)
                for j in range(2):
                    dve.wait_ge(a_sm, n[j])
                    tt(ta[j][:, 128:256], tb2[j][:, 0:S], h[:, 256 * j + S:256 * j + 2 * S], ALU.add).then_inc(a_sn, 1)
                for j in range(2):
                    dve.wait_ge(a_sn, n[j])
                    nc.vector.tensor_reduce(mx[:, 8 * j:8 * j + 1], ta[j][:, 128:256], AX.X, ALU.max).then_inc(a_max, 1)
                for j in range(2):
                    dve.wait_ge(a_max, n[j])
                    ts(mx[:, 8 * j + 1:8 * j + 2], mx[:, 8 * j:8 * j + 1], -SCALE_A, None, ALU.mult).then_inc(a_bias, 1)
                if following is not None:
                    pair_stats(following)
                if gate is not None:
                    gate_means(gate)
                for j in range(2):
                    dve.wait_ge(a_p, n[j])
                    nc.vector.reciprocal(mx[:, 8 * j + 3:8 * j + 4], mx[:, 8 * j + 2:8 * j + 3]).then_inc(a_rsum, 1)
                for j in range(2):
                    dve.wait_ge(a_rsum, n[j])
                    ts(mx[:, 8 * j + 4:8 * j + 5], mx[:, 8 * j + 3:8 * j + 4], KEEP, None, ALU.mult).then_inc(a_keep, 1)
                if following is not None:
                    pair_tokens(following)
                for j in range(2):
                    dve.wait_ge(a_keep, n[j])
                    dve.wait_ge(a_pv, n[j])
                    stt(xb[j], ps[:, 4 * j + 3, 0:D], mx[:, 8 * j + 4:8 * j + 5], xb[j], ALU.mult, ALU.add).then_inc(a_x, 1)
                for j in range(2):
                    dve.wait_ge(a_x, n[j])
                    stats(xb[j], 2 + j, i * 2 + j, a_gstats, a_gvar)

            pair_stats(0)
            dve.wait_ge(mask_in, 16)
            pair_tokens(0)
            dve.wait_ge(x_in1, 16)
            pair(0, None, 1)
            dve.wait_ge(x_in2, 16)
            with dve.Fori(1, PAIRS - 1) as i:
                pair(i, i - 1, i + 1)
            pair(PAIRS - 1, PAIRS - 2, None)
            gate_tokens(PAIRS - 1)
            gate_means(PAIRS - 1)

            count = [0]

            def g_link(ins):
                count[0] += 1
                ins.then_inc(g_dve, 1)
                dve.wait_ge(g_dve, count[0])
            dve.wait_ge(gw_in, 32)
            dve.wait_ge(a_gmean, B)
            for c in range(KC):
                last = tt(gprod[:, c, :, :], gmean[:, c, :].rearrange("p (b o) -> p b o", o=1).broadcast_to([128, B, E]),
                          gw[:, c:c + 1, :].broadcast_to([128, B, E]), ALU.mult)
            last.then_inc(g_prod, 1)
            nc.vector.memset(b1hl[:, :], 0.0).then_inc(b1_zero, 1)
            dve.wait_ge(b1_hi, 1)
            for half in range(2):
                tt(b1hl[32:32 + E, 512 * half:512 * half + 512], b1f[half], b1hl[0:E, 512 * half:512 * half + 512],
                   ALU.subtract).then_inc(b1_ready, 1)
            dve.wait_ge(b1_ready, 2)
            nc.vector.memset(v[:, :, :], 0.0).then_inc(vones_ready, 1)
            dve.wait_ge(vones_ready, 1)
            nc.vector.memset(v[:, :, HD:HD + 1], 1.0).then_inc(vones_ready, 1)
            dve.wait_ge(g_log, 1)

            def be(k):
                return gl[:, k, :].rearrange("p (b e) -> p b e", e=E)

            def per_b(k):
                return gs[:, k, :].rearrange("p (b o) -> p b o", o=1).broadcast_to([128, B, E])

            def const_e(c0):
                return cst[:, c0:c0 + E].rearrange("p (o e) -> p o e", o=1).broadcast_to([128, B, E])
            gb = gate_b[:, :].rearrange("p (o e) -> p o e", o=1).broadcast_to([128, B, E])
            nc.vector.tensor_tensor(be(0), ps[:, 5, 0:B * E].rearrange("p (b e) -> p b e", e=E), gb, ALU.add).then_inc(g_fill, 1)
            dve.wait_ge(g_fill, 1)
            g_link(nc.vector.tensor_reduce(gs[:, 0, :], be(0), AX.X, ALU.max))
            g_link(tt(be(1), be(0), per_b(0), ALU.subtract))
            g_link(tt(be(3), be(0), per_b(0), ALU.is_equal))
            g_link(tt(be(4), be(3), const_e(C_RNK4), ALU.mult))
            g_link(nc.vector.tensor_reduce(gs[:, 1, :], be(4), AX.X, ALU.max))
            g_link(tt(be(5), be(4), per_b(1), ALU.is_equal))
            g_link(ts(be(6), be(5), -3.0e38, None, ALU.mult))
            g_link(ts(be(7), be(5), -1.0, 1.0, ALU.mult, ALU.add))
            g_link(tt(be(8), be(0), be(7), ALU.mult))
            g_link(tt(be(8), be(8), be(6), ALU.add))
            g_link(nc.vector.tensor_reduce(gs[:, 2, :], be(8), AX.X, ALU.max))
            g_link(tt(be(3), be(8), per_b(2), ALU.is_equal))
            g_link(tt(be(4), be(3), const_e(C_RNK4), ALU.mult))
            g_link(nc.vector.tensor_reduce(gs[:, 3, :], be(4), AX.X, ALU.max))
            g_link(tt(be(9), be(4), per_b(3), ALU.is_equal))
            dve.wait_ge(g_exp, 1)
            g_link(nc.vector.tensor_reduce(gs[:, 4, :], be(2), AX.X, ALU.add))
            g_link(nc.vector.reciprocal(gs[:, 5, :], gs[:, 4, :]))
            g_link(tt(be(10), be(2), per_b(5), ALU.mult))
            slots = gate_w[:, :].rearrange("p (b s) -> p b s", s=TOPK)
            picks = chosen[:, :].rearrange("p (b s) -> p b s", s=TOPK)
            for s, k in ((0, 5), (1, 9)):
                g_link(tt(be(11), be(10), be(k), ALU.mult))
                g_link(nc.vector.tensor_reduce(slots[:, :, s], be(11), AX.X, ALU.add))
                g_link(tt(be(11), be(k), const_e(C_ID4), ALU.mult))
                g_link(nc.vector.tensor_reduce(gs[:, 6 + s, :], be(11), AX.X, ALU.add))
                g_link(cp(picks[:, :, s], gs[:, 6 + s, :]))
            dve.wait_ge(vec_in, 16 * E)
            nc.vector.memset(dsm[:, 7, 0:1], 0.0).then_inc(g_ready, 1)

            def y_stats_of(xb, k):
                stats(xb, 0, k, y_stats, y_var)

            def y_of(xb, k, uses=None):
                dve.wait_ge(y_rstd, k + 1)
                if uses is not None:
                    dve.wait_ge(ybo_ready, uses)
                normalized(y[:, :], xb, 0).then_inc(y_ready, 1)

            def y_low(k, n, bank=4):
                dve.wait_ge(yT_hi, k + 1)
                tt(ycT_lo[:, 0:n, :], ps[:, bank, 0:128 * n].rearrange("p (c k) -> p c k", k=128), ycT_hi[:, 0:n, :],
                   ALU.subtract).then_inc(yT_ready, 1)

            def bias_qk(n, t, base):
                dve.wait_ge(qk_psum, n + 1)
                tt(qk[:, :], ps[:, 4, :], t[:, ds(base + V_QKV, 2 * D)], ALU.add).then_inc(qk_sb, 1)

            def bias_v(n, t, base):
                dve.wait_ge(v_psum, n + 1)
                if not isinstance(n, int) or n > 0:
                    dve.wait_ge(oT_psum, n)
                tt(v[:, :, 0:HD], ps[:, 5, 0:D].rearrange("p (h d) -> p h d", d=HD),
                   t[:, ds(base + (V_QKV + 2 * D), D)].rearrange("p (h d) -> p h d", d=HD), ALU.add).then_inc(v_sb, 1)

            def qk_low(n):
                dve.wait_ge(qkT_hi, n + 1)
                tt(ql[:, :, :], ps[:, 4, 0:D].rearrange("p (c k) -> p c k", k=128), qh[:, :, :], ALU.subtract)
                kk = ps[:, 4, D:2 * D].rearrange("p (c k) -> p c k", k=128)
                for s in range(2):
                    last = stt(klm[:, :, s, :], kk, mask_eo[s], khm[:, :, s, :], ALU.mult, ALU.subtract)
                last.then_inc(qk_split, 1)

            def maxima(n):
                dve.wait_ge(s_psum, n + 1)
                nc.vector.tensor_reduce(mx[:, :], att.rearrange("p g s k -> p (g s) k"), AX.X, ALU.max,
                                        negate=True).then_inc(m_max, 1)
                dve.wait_ge(m_max, n + 1)
                many = mx[:, :].rearrange("p (o h) -> p o h", o=1).broadcast_to([128, 4, H])
                cp(mtile[:, :, 0, :], many).then_inc(m_hi, 1)
                dve.wait_ge(m_hi, n + 1)
                tt(mtile[:, :, 1, :], many, mtile[:, :, 0, :], ALU.subtract).then_inc(m_split, 1)

            def o_norm(n, bank=1):
                dve.wait_ge(o_row, n + 1)
                rows = ps[:, bank, :].rearrange("p (h k) -> p h k", k=32)
                nc.vector.reciprocal(o_rs[:, :].rearrange("p (h o) -> p h o", o=1), rows[:, :, HD:HD + 1]).then_inc(o_rsum, 1)
                dve.wait_ge(o_rsum, n + 1)
                tt(o[:, :].rearrange("p (h d) -> p h d", d=HD), rows[:, :, 0:HD],
                   o_rs[:, :].rearrange("p (h o) -> p h o", o=1).broadcast_to([128, H, HD]), ALU.mult).then_inc(o_sb, 1)

            def o_low(n):
                dve.wait_ge(oo_hi, n + 1)
                tt(ool[:, :, :], ps[:, 5, D:2 * D].rearrange("p (c k) -> p c k", k=128), ooh[:, :, :],
                   ALU.subtract).then_inc(oo_split, 1)

            def sum1(n, slot):
                dve.wait_ge(proj_psum, n + 1)
                dve.wait_ge(ybo_ready, n + 1)
                tt(t1[:, :], ps[:, 5, 0:D], ybo[:, slot, :], ALU.add).then_inc(res1, 1)
                dve.wait_ge(res1, n + 1)
                stats(t1[:, :], 1, n, l1_stats, l1_var)

            def norm1(n):
                dve.wait_ge(l1_rstd, n + 1)
                if not isinstance(n, int) or n > 0:
                    dve.wait_ge(x1b_ready, n)
                normalized(x1[:, :], t1[:, :], 1).then_inc(l1_xn, 1)

            def x1_low(n):
                dve.wait_ge(x1T_hi, n + 1)
                tt(xl[:, :, :], ps[:, 6, 0:D].rearrange("p (c k) -> p c k", k=128), xh[:, :, :],
                   ALU.subtract).then_inc(x1T_split, 1)

            def h_low(n, half):
                dve.wait_ge(hh_b if half else hh_a, n + 1)
                tt(hl[:, 4 * half:4 * half + 4, :], ps[:, 7 - half, :].rearrange("p (c k) -> p c k", k=128),
                   hh[:, 4 * half:4 * half + 4, :], ALU.subtract).then_inc(hl_b if half else hl_a, 1)

            def sum2(n):
                dve.wait_ge(ff_psum, n + 1)
                dve.wait_ge(x1b_ready, n + 1)
                tt(t2[:, :], ps[:, 7, 0:D], x1b[:, :], ALU.add).then_inc(res2, 1)
                dve.wait_ge(res2, n + 1)
                stats(t2[:, :], 2, n, l2_stats, l2_var)

            def norm2(n):
                dve.wait_ge(l2_rstd, n + 1)
                normalized(y2[:, :], t2[:, :], 2).then_inc(l2_xn, 1)

            def add_expert(n, xb):
                dve.wait_ge(y2_ready, n + 1)
                stt(xb, y2[:, :], gate_w[:, ds(n, 1)], xb, ALU.mult, ALU.add).then_inc(x_acc, 1)

            def expert(u):
                return dve.value_load(chosen[0:1, ds(u, 1)], min_val=0, max_val=E - 1)

            def at(b):
                return x[:, ds(b * D, D)]

            def block(n, slot, m, f, add, next_k, next_x, causal_m=False):
                vm = (vc, 0) if causal_m else (vec, expert(m) * V_EXP)
                if next_k is not None:
                    y_stats_of(next_x, next_k)
                bias_qk(m, *vm)
                if f is not None:
                    x1_low(f)
                if add is not None:
                    add_expert(*add)
                if next_k is not None:
                    y_of(next_x, next_k, UNITS if isinstance(next_k, int) and next_k >= B else next_k * 2)
                bias_v(m, *vm)
                qk_low(m)
                o_norm(n)
                if f is not None:
                    h_low(f, 0)
                o_low(n)
                if f is not None:
                    h_low(f, 1)
                if next_k is not None:
                    y_low(next_k, KC if not isinstance(next_k, int) or next_k < B else 2 * KC)
                maxima(m)
                if slot is None:
                    x3(n, n - UNITS)
                else:
                    sum1(n, slot)
                    norm1(n)
                if f is not None:
                    sum2(f)
                    norm2(f)

            def x3(n, b):
                dve.wait_ge(proj_psum, n + 1)
                dve.wait_ge(ybo_ready, n + 1)
                tt(at(b), ps[:, 5, 0:D], ybo[:, 0, :], ALU.add).then_inc(res1, 1)
                dve.wait_ge(res1, n + 1)
                stats(at(b), 1, n, s_stats, s_var)

            def sh_y(b):
                dve.wait_ge(s_rstd, b + C1)
                if not isinstance(b, int) or b > 0:
                    dve.wait_ge(s_comb, b * 32)
                normalized(t1[:, :], at(b), 1).then_inc(s_y, 1)

            def sh_low(f):
                dve.wait_ge(s_yhi, f + C1)
                tt(xl[:, :, :], ps[:, 7, 0:D].rearrange("p (c k) -> p c k", k=128), xh[:, :, :],
                   ALU.subtract).then_inc(s_ysplit, 1)

            def sh_bias(f):
                dve.wait_ge(s_h, f + C1)
                tt(h[:, 0:2 * HM], ps[:, 7, 256:256 + 2 * HM], tvec[:, U_S12:U_S12 + 2 * HM], ALU.add).then_inc(s_hb, 1)

            def sh_gated(f):
                dve.wait_ge(s_e, f + C1)
                ts(de[:, HM:2 * HM], de[:, 0:HM], 1.0, None, ALU.add).then_inc(s_e1, 1)
                dve.wait_ge(s_e1, f + C1)
                nc.vector.reciprocal(de[:, 0:HM], de[:, HM:2 * HM]).then_inc(s_r, 1)
                dve.wait_ge(s_r, f + C1)
                tt(h[:, 2 * HM:3 * HM], h[:, 0:HM], de[:, 0:HM], ALU.mult).then_inc(s_a, 1)
                dve.wait_ge(s_a, f + C1)
                tt(h[:, 3 * HM:4 * HM], h[:, 2 * HM:3 * HM], h[:, HM:2 * HM], ALU.mult).then_inc(s_g, 1)
                dve.wait_ge(s_g, f + C1)
                stats(h[:, 3 * HM:4 * HM], 2, f + UNITS, s_gst, s_gvar)

            def sh_gnorm(f):
                dve.wait_ge(s_grs, f + C1)
                normalized(h[:, 2 * HM:3 * HM], h[:, 3 * HM:4 * HM], 2).then_inc(s_gn, 1)

            def sh_zlow(g):
                dve.wait_ge(s_zhi, g + C1)
                tt(hl[:, 0, :], ps[:, 6, 256:256 + HM], hh[:, 0, :], ALU.subtract).then_inc(s_zsplit, 1)

            def sh_sum(g):
                dve.wait_ge(s_o, g + C1)
                dve.wait_ge(s_shared, g * 16 + 16)
                tt(acc[:, :], ps[:, 6, 0:D], tvec[:, U_S3:U_S3 + D], ALU.add).then_inc(s_sh, 1)

            def block_c(b, parts):
                n = b + UNITS
                if "prep" in parts:
                    y_stats_of(at(b + 2), b + (B + 2))
                if "next" in parts:
                    bias_qk(n + 1, vc, 0)
                if "sh1" in parts:
                    sh_low(b - 1)
                if "next" in parts:
                    bias_v(n + 1, vc, 0)
                if "prep" in parts:
                    y_of(at(b + 2), b + (B + 2))
                if "next" in parts:
                    qk_low(n + 1)
                if "att" in parts:
                    o_norm(n, 6)
                if "sh1" in parts:
                    sh_bias(b - 1)
                if "prep" in parts:
                    y_low(b + (B + 2), 2 * KC, 4)
                if "att" in parts:
                    o_low(n)
                if "sh2" in parts:
                    sh_zlow(b - 2)
                if "next" in parts:
                    maxima(n + 1)
                if "att" in parts:
                    x3(n, b)
                if "sh1" in parts:
                    sh_gated(b - 1)
                if "sh2" in parts:
                    sh_sum(b - 2)
                if "att" in parts:
                    sh_y(b)
                if "sh1" in parts:
                    sh_gnorm(b - 1)

            y_stats_of(at(0), 0)
            y_of(at(0), 0)
            y_low(0, KC)
            e0 = expert(0) * V_EXP
            bias_qk(0, vec, e0)
            bias_v(0, vec, e0)
            qk_low(0)
            maxima(0)
            block(0, 0, 1, None, None, 1, at(1))
            block(1, 1, 2, 0, None, None, None)
            with dve.Fori(1, B - 1) as b:
                block(b * 2, 0, b * 2 + 1, (b - 1) * 2 + 1, ((b - 1) * 2, at(b - 1)), b + 1, at(b + 1))
                block(b * 2 + 1, 1, b * 2 + 2, b * 2, ((b - 1) * 2 + 1, at(b - 1)), None, None)
            dve.wait_ge(vc_in, 16)
            block(UNITS - 2, 0, UNITS - 1, UNITS - 3, (UNITS - 4, at(B - 2)), B, at(0))
            block(UNITS - 1, 1, UNITS, UNITS - 2, (UNITS - 3, at(B - 2)), B + 1, at(1), causal_m=True)
            block(UNITS, None, UNITS + 1, UNITS - 1, (UNITS - 2, at(B - 1)), B + 2, at(2), causal_m=True)
            sh_y(0)
            add_expert(UNITS - 1, at(B - 1))
            dve.wait_ge(tvec_in, 16)
            block_c(1, ("att", "next", "prep", "sh1"))
            with dve.Fori(2, B - 2) as b:
                block_c(b, ("att", "next", "prep", "sh1", "sh2"))
            block_c(B - 2, ("att", "next", "sh1", "sh2"))
            links = [0]

            def i_link(ins):
                links[0] += 1
                ins.then_inc(d_idx, 1)
                dve.wait_ge(d_idx, links[0])

            def rows_of(src_b, src_t, fb, ft, tmp, flat, key):
                for src, f, size in ((src_b, fb, B), (src_t, ft, S)):
                    i_link(cp(f, src))
                    i_link(ts(tmp, f, 0.0, float(size), ALU.is_lt, ALU.mult))
                    i_link(tt(f, f, tmp, ALU.add))
                i_link(ts(tmp, fb, 0.0, None, ALU.is_lt))
                i_link(ts(flat, fb, float(B - 1), None, ALU.is_gt))
                i_link(tt(tmp, tmp, flat, ALU.add))
                i_link(ts(flat, ft, 0.0, None, ALU.is_lt))
                i_link(tt(tmp, tmp, flat, ALU.add))
                i_link(ts(flat, ft, float(S - 1), None, ALU.is_gt))
                i_link(tt(tmp, tmp, flat, ALU.add))
                i_link(ts(key, tmp, float(4 * B * S), None, ALU.mult))
                i_link(ts(fb, fb, 0.0, float(B - 1), ALU.max, ALU.min))
                i_link(ts(ft, ft, 0.0, float(S - 1), ALU.max, ALU.min))
                i_link(ts(fb, fb, float(S), None, ALU.mult))
                i_link(tt(flat, fb, ft, ALU.add))
                i_link(tt(key, key, flat, ALU.add))

            dve.wait_ge(idx_in, 32)
            rows_of(idx_i[:, 0, :], idx_i[:, 1, :], ids[:, 0, :], ids[:, 1, :], ids[:, 2, :], ids[:, 3, :], ids[:, 4, :])
            i_link(cp(gidx[:, :], ids[:, 3, :]))
            nc.vector.memset(junk[:, 0:1], 0.0).then_inc(d_gidx, 1)
            block_c(B - 1, ("att", "sh1", "sh2"))
            block_c(B, ("sh1", "sh2"))
            block_c(B + 1, ("sh2",))

            dve.wait_ge(tg_hi, 1)
            tt(tg_l[:, :, :], tg[:, :, :], tg_h[:, :, :], ALU.subtract).then_inc(tg_split, 1)

            for i in range(2):
                dve.wait_ge(d_xhi, D1 + i)
                tt(xT[:, 2 * i:2 * i + 2, KC:2 * KC, :], ps[:, 4 + i, :].rearrange("p (t c k) -> p t c k", t=2, k=128),
                   xT[:, 2 * i:2 * i + 2, 0:KC, :], ALU.subtract).then_inc(d_xsplit, 1)
            step = [0]

            def link(ins):
                step[0] += 1
                ins.then_inc(d_chain, 1)
                dve.wait_ge(d_chain, step[0])

            def per_token(k):
                return dsm[:, k, :].rearrange("p (t o) -> p t o", o=1).broadcast_to([128, MT, EM])

            def const_t(c0, n, src):
                return src[:, c0:c0 + n].rearrange("p (o e) -> p o e", o=1).broadcast_to([128, MT, n])
            dve.wait_ge(d_gl, D1)
            tt(dg[:, 0, :, :], ps[:, 3, 0:16 * MT].rearrange("p (t k) -> p t k", k=16)[:, :, 0:EM + 1],
               const_t(U_GB, EM + 1, tvec), ALU.add).then_inc(d_gb, 1)
            dve.wait_ge(d_ge, D1)
            link(ts(dg[:, 2, :, :], dg[:, 1, :, :], 1.0, None, ALU.add))
            link(nc.vector.reciprocal(dg[:, 3, :, :], dg[:, 2, :, :]))
            link(tt(dg[:, 4, :, 0:EM], dg[:, 3, :, 1:EM + 1], const_t(U_XB, EM, tvec), ALU.add))
            link(nc.vector.tensor_reduce(dsm[:, 0, :], dg[:, 4, :, 0:EM], AX.X, ALU.max))
            link(tt(dg[:, 5, :, 0:EM], dg[:, 4, :, 0:EM], per_token(0), ALU.is_equal))
            link(tt(dg[:, 6, :, 0:EM], dg[:, 5, :, 0:EM], const_t(C_RNK8, EM, cst), ALU.mult))
            link(nc.vector.tensor_reduce(dsm[:, 1, :], dg[:, 6, :, 0:EM], AX.X, ALU.max))
            tt(dg[:, 7, :, 0:EM], dg[:, 6, :, 0:EM], per_token(1), ALU.is_equal).then_inc(d_sel, 1)
            dve.wait_ge(d_sel, D1)
            link(tt(dg[:, 8, :, 0:EM], dg[:, 7, :, 0:EM], dg[:, 3, :, 1:EM + 1], ALU.mult))
            link(nc.vector.tensor_reduce(dsm[:, 2, :], dg[:, 8, :, 0:EM], AX.X, ALU.add))
            tt(dsm[:, 3, :], dg[:, 3, :, 0], dsm[:, 2, :], ALU.subtract).then_inc(d_diff, 1)
            dve.wait_ge(d_we, D1)
            link(ts(dsm[:, 5, :], dsm[:, 4, :], 1.0, None, ALU.add))
            link(nc.vector.reciprocal(dsm[:, 4, :], dsm[:, 5, :]))
            link(ts(dsm[:, 5, :], dsm[:, 4, :], -1.0, 1.0, ALU.mult, ALU.add))

            def mask_tokens(t):
                dve.wait_ge(d_ohb, D1 + t)
                if t >= 2:
                    dve.wait_ge(d_h, D1 + t - 2)
                oh = ohb[:, t, :, :].rearrange("p e (o k) -> p e o k", o=1)
                tt(xm[:, t % 2], xT[:, t, :, :].rearrange("p (o c) k -> p o c k", o=1).broadcast_to([128, EM, 2 * KC, 128]),
                   oh.broadcast_to([128, EM, 2 * KC, 128]), ALU.mult).then_inc(d_xm, 1)

            def gated(t):
                h12 = qk[:, 256 * (t % 2):256 * (t % 2) + 256]
                dve.wait_ge(d_e, D1 + t)
                link(ts(h[:, 0:HM], de[:, HM * (t % 2):HM * (t % 2) + HM], 1.0, None, ALU.add))
                link(nc.vector.reciprocal(h[:, HM:2 * HM], h[:, 0:HM]))
                link(tt(h[:, 0:HM], h12[:, 0:HM], h[:, HM:2 * HM], ALU.mult))
                link(tt(h[:, 2 * HM:3 * HM], h[:, 0:HM], h12[:, HM:2 * HM], ALU.mult))
                link(nc.vector.bn_stats(st[:, 2, :], h[:, 2 * HM:3 * HM]))
                nc.vector.bn_aggr(mv[:, 2, :], st[:, 2, :]).then_inc(d_var, 1)

            def gated_norm(t):
                dve.wait_ge(d_rstd, D1 + t)
                normalized(h[:, 3 * HM:4 * HM], h[:, 2 * HM:3 * HM], 2).then_inc(d_gn, 1)

            def mask_z(t):
                dve.wait_ge(d_zhi, D1 + t)
                tt(zT[:, t % 2, 1, :], ps[:, 4 + t % 2, 0:HM], zT[:, t % 2, 0, :], ALU.subtract).then_inc(d_zsplit, 1)
                dve.wait_ge(d_zsplit, D1 + t)
                oh = ohb[:, t, :, :].rearrange("p e (o k) -> p e o k", o=1)
                tt(zm[:, t % 2], zT[:, t % 2, :, :].rearrange("p (o c) k -> p o c k", o=1).broadcast_to([128, EM, 2, 128]),
                   oh.broadcast_to([128, EM, 2, 128]), ALU.mult).then_inc(d_zm, 1)

            def final(t):
                shared = (t2, acc)[t % 2]
                if t == 0:
                    dve.wait_ge(d_gshared, 16 * MT)
                link(stt(shared[:, :], comb[:, t * 3 * D + 2 * D:(t + 1) * 3 * D], dsm[:, 4, t:t + 1],
                         comb[:, t * 3 * D:t * 3 * D + D], ALU.mult, ALU.add))
                dve.wait_ge(d_o, D1 + t)
                stt(finD[:, t * D:(t + 1) * D], ps[:, 2 + t % 2, 0:D], dsm[:, 5, t:t + 1], shared[:, :],
                    ALU.mult, ALU.add).then_inc(d_fin, 1)

            def keys_as_rows(t):
                dve.wait_ge(row_in, 16 * 3)
                rows_of(row_i[:, 0, :], row_i[:, 1, :], row_f[:, 0, :], row_f[:, 1, :], row_tmp, row_flat,
                        row_key)

            def last_of_equal(t):
                i_link(stt(row_tmp, row_key, ids[:, 4, t:t + 1], pos, ALU.is_equal, ALU.mult))
                i_link(nc.vector.tensor_reduce(ids[:, 5, t:t + 1], row_tmp, AX.X, ALU.max))

            def stored_rows(t):
                i_link(tt(ids[:, 6, :], ids[:, 5, :], cst[:, C_M:C_M + MT], ALU.is_gt))
                i_link(ts(ids[:, 7, :], ids[:, 6, :], float(4 * B * S), None, ALU.mult))
                i_link(tt(ids[:, 8, :], ids[:, 7, :], ids[:, 4, :], ALU.add))
                i_link(cp(sidx[:, :], ids[:, 8, :]))
                nc.vector.memset(junk[:, 0:1], 0.0).then_inc(d_sidx, 1)

            for step_of, t in ((mask_tokens, 0), (mask_tokens, 1), (keys_as_rows, None), (gated, 0),
                               (mask_tokens, 2), (gated_norm, 0), (mask_z, 0), (gated, 1), (mask_tokens, 3),
                               (gated_norm, 1), (last_of_equal, 0), (mask_z, 1), (gated, 2), (gated_norm, 2),
                               (last_of_equal, 1), (final, 0), (mask_z, 2), (gated, 3), (gated_norm, 3),
                               (last_of_equal, 2), (final, 1), (mask_z, 3), (last_of_equal, 3), (stored_rows, None),
                               (final, 2), (final, 3)):
                step_of(t)

        @block.gpsimd
        def _(pool):
            tt = nc.gpsimd.tensor_tensor

            def rstd(i, n, var, veps, done):
                pool.wait_ge(var, n)
                tt(rs[:, i, :], mv[:, i, 1:2], cst[:, C_EPS:C_EPS + 1], ALU.add).then_inc(veps, 1)
                pool.wait_ge(veps, n)
                tt(rs[:, i, :], rs[:, i, :], halves, ALU.pow).then_inc(done, 1)

            pool.wait_ge(cst_in, 16)

            def pair_roots(i):
                for j in range(2):
                    rstd(j, i * 2 + (j + 1), a_var, a_veps, a_rstd)

            def gate_roots(i):
                for j in range(2):
                    rstd(2 + j, i * 2 + (j + 1), a_gvar, a_gveps, a_grstd)

            def weights_low(i, j):
                pool.wait_ge(w_hi_ready, i * 2 + (j + 1))
                tt(w_lo[:, ds(i * (2 * WCH) + j * WCH, WCH)], stage[:, j, :], w_hi[:, ds(i * (2 * WCH) + j * WCH, WCH)],
                   ALU.subtract).then_inc(w_lo_ready, 1)

            pair_roots(0)
            weights_low(0, 0)
            pair_roots(1)
            weights_low(0, 1)
            with pool.Fori(1, PAIRS - 1) as i:
                gate_roots(i - 1)
                weights_low(i, 0)
                pair_roots(i + 1)
                weights_low(i, 1)
            gate_roots(PAIRS - 2)
            weights_low(PAIRS - 1, 0)
            weights_low(PAIRS - 1, 1)
            gate_roots(PAIRS - 1)
            pool.wait_ge(wc_hi_ready, 1)
            tt(wc_lo, wc_raw, wc_hi, ALU.subtract).then_inc(wc_ready, 1)

            def expert(u):
                return pool.value_load(chosen[0:1, ds(u, 1)], min_val=0, max_val=E - 1)

            def at(b):
                return x[:, ds(b * D, D)]

            def y_bias(u, k, slot, base):
                if not isinstance(u, int) or u > 0:
                    pool.wait_ge(res1, (k - 1) * 2 + (slot + 1) if not isinstance(k, int) else 2 * k + slot - 1)
                pool.wait_ge(y_ready, k + 1)
                tt(ybo[:, slot, :], y[:, :], vec[:, ds(base + V_OUT, D)], ALU.add).then_inc(ybo_ready, 1)

            def affine1(n, base):
                rstd(1, n + 1, l1_var, l1_veps, l1_rstd)
                pool.wait_ge(l1_xn, n + 1)
                tt(x1[:, :], x1[:, :], vec[:, ds(base + V_G1, D)], ALU.mult).then_inc(l1_g, 1)
                pool.wait_ge(l1_g, n + 1)
                tt(x1[:, :], x1[:, :], vec[:, ds(base + V_B1, D)], ALU.add).then_inc(x1_ready, 1)

            def x1_bias(n, base):
                pool.wait_ge(x1_ready, n + 1)
                tt(x1b[:, :], x1[:, :], vec[:, ds(base + V_L2, D)], ALU.add).then_inc(x1b_ready, 1)

            def affine2(n, base):
                pool.wait_ge(l2_xn, n + 1)
                tt(y2[:, :], y2[:, :], vec[:, ds(base + V_G2, D)], ALU.mult).then_inc(l2_g, 1)
                pool.wait_ge(l2_g, n + 1)
                tt(y2[:, :], y2[:, :], vec[:, ds(base + V_B2, D)], ALU.add).then_inc(y2_ready, 1)

            def y_root(k):
                rstd(0, k + 1, y_var, y_veps, y_rstd)

            def block(n, f, bn, bf, next_k):
                if next_k is not None:
                    y_root(next_k)
                affine1(n, bn)
                if f is not None:
                    rstd(2, f + 1, l2_var, l2_veps, l2_rstd)
                x1_bias(n, bn)
                if f is not None:
                    affine2(f, bf)

            pool.wait_ge(g_ready, 1)
            y_root(0)
            bs = [expert(u) * V_EXP for u in range(2)]
            y_bias(0, 0, 0, bs[0])
            y_bias(0, 0, 1, bs[1])
            block(0, None, bs[0], None, 1)
            block(1, 0, bs[1], bs[0], None)
            with pool.Fori(1, B - 1) as b:
                u = [(b - 1) * 2 + 1, b * 2, b * 2 + 1]
                bs = [expert(i) * V_EXP for i in u]
                y_root(b + 1)
                y_bias(u[1], b, 0, bs[1])
                y_bias(u[2], b, 1, bs[2])
                block(u[1], u[0], bs[1], bs[0], None)
                block(u[2], u[1], bs[2], bs[1], None)
            u = [UNITS - 3, UNITS - 2, UNITS - 1]
            bs = [expert(i) * V_EXP for i in u]
            y_bias(u[1], B - 1, 0, bs[1])
            y_bias(u[2], B - 1, 1, bs[2])
            block(u[1], u[0], bs[1], bs[0], B)
            block(u[2], u[1], bs[2], bs[1], B + 1)

            def x_bias(b):
                pool.wait_ge(res1, b + UNITS)
                tt(ybo[:, 0, :], at(b), vc[:, V_OUT:V_OUT + D], ALU.add).then_inc(ybo_ready, 1)

            pool.wait_ge(vc_in, 16)
            x_bias(0)
            y_root(B + 2)
            rstd(1, C1, s_var, s_veps, s_rstd)
            rstd(2, UNITS, l2_var, l2_veps, l2_rstd)
            affine2(UNITS - 1, bs[2])

            def tw(c, j):
                pool.wait_ge(tw_hi, c + 1)
                tt(w_lo[:, ds(c * TCH, TCH)], tstage[:, j, :], w_hi[:, ds(c * TCH, TCH)], ALU.subtract).then_inc(tw_lo, 1)

            def sh_affine(f):
                pool.wait_ge(s_gn, f + C1)
                tt(h[:, 512:512 + HM], h[:, 2 * HM:3 * HM], tvec[:, U_SG:U_SG + HM], ALU.mult).then_inc(s_gg, 1)
                pool.wait_ge(s_gg, f + C1)
                tt(h[:, 512:512 + HM], h[:, 512:512 + HM], tvec[:, U_SB:U_SB + HM], ALU.add).then_inc(s_z, 1)

            def sh_sum(g):
                pool.wait_ge(s_sh, g + C1)
                pool.wait_ge(s_out, g * 16 + 16)
                tt(fin[:, :], acc[:, :], at(g), ALU.add).then_inc(s_sum, 1)

            def block_c(b, parts, weights):
                if "prep" in parts:
                    y_root(b + (B + 2))
                if "att" in parts:
                    x_bias(b)
                for w in weights:
                    tw(*w)
                if "sh1" in parts:
                    rstd(2, b + (C1 - 1), s_gvar, s_gveps, s_grs)
                if "att" in parts:
                    rstd(1, b + C1, s_var, s_veps, s_rstd)
                if "sh1" in parts:
                    sh_affine(b - 1)
                if "sh2" in parts:
                    sh_sum(b - 2)

            pool.wait_ge(tvec_in, 16)
            block_c(1, ("att", "next", "prep", "sh1"), [(0, 0), (1, 1)])
            with pool.Fori(1, B // 2 - 1) as i:
                for j in range(2):
                    block_c(i * 2 + j, ("att", "next", "prep", "sh1", "sh2"), [(i * 2 + j, j)])
            block_c(B - 2, ("att", "next", "sh1", "sh2"), [(B - 2, 0)])
            block_c(B - 1, ("att", "sh1", "sh2"), [(B - 1, 1)])
            def gather(c0, c1, rows_d, done):
                for t in range(MT):
                    nc.gpsimd.indirect_dma_start(out=comb[:, t * 3 * D + c0:t * 3 * D + c1], out_offset=None,
                                                 in_=rows_d[:, :],
                                                 in_offset=bass.IndirectOffsetOnAxis(ap=gidx[:, t:t + 1], axis=0)
                                                 ).then_inc(done, 16)

            pool.wait_ge(s_comb, 16 * 2 * B)
            pool.wait_ge(d_gidx, 1)
            gather(0, 2 * D, comb_d, d_gather)
            block_c(B, ("sh1", "sh2"), [])
            block_c(B + 1, ("sh2",), [])
            pool.wait_ge(s_shared, 16 * (B + 1))
            gather(2 * D, 3 * D, shared_d, d_gshared)
            for t in range(MT):
                rstd(2, t + D1, d_var, d_veps, d_rstd)
                pool.wait_ge(d_gn, t + D1)
                if t >= 2:
                    pool.wait_ge(d_zT, t + D1 - 2)
                z = y[:, 128 * (t % 2):128 * (t % 2) + 128]
                tt(z, h[:, 3 * HM:4 * HM], tvec[:, U_EG:U_EG + HM], ALU.mult).then_inc(d_gg, 1)
                pool.wait_ge(d_gg, t + D1)
                tt(z, z, tvec[:, U_EB:U_EB + HM], ALU.add).then_inc(d_z, 1)
            pool.wait_ge(d_sidx, 1)
            pool.wait_ge(s_out, 16 * (B + 1))
            for t in range(MT):
                pool.wait_ge(d_fin, t + D1)
                nc.gpsimd.indirect_dma_start(out=out[:, :],
                                             out_offset=bass.IndirectOffsetOnAxis(ap=sidx[:, t:t + 1], axis=0),
                                             in_=finD[:, t * D:(t + 1) * D], in_offset=None,
                                             bounds_check=B * S - 1, oob_is_err=False).then_inc(d_out, 16)


def _consts(np):
    p = np.arange(128)
    c = np.zeros((128, C_ALL), np.float32)
    c[:, C_ID:C_ID + 128] = np.eye(128)
    c[:, C_ME] = (p % 32) < 16
    c[:, C_MO] = (p % 32) >= 16
    c[:, C_RNK4:C_RNK4 + E] = [4, 3, 2, 1]
    c[:, C_ID4:C_ID4 + E] = [0, 1, 2, 3]
    c[:, C_RNK8:C_RNK8 + EM] = [8, 7, 6, 5, 4, 3, 2, 1]
    c[:, C_M:C_M + MT] = p[:, None] + 128 * np.arange(MT)[None, :]
    c[:, C_HALF] = -0.5
    c[:, C_EPS] = EPS
    k = np.zeros((128, K_ALL), np.float32)
    for s in range(4):
        k[:, K_SEL + 128 * s:K_SEL + 128 * (s + 1)] = ((p % 16) == 4 * (p // 32) + s)[:, None]
    k[:, K_CS:K_CS + 128] = np.where(p[None, :] > p[:, None], -1e30, 0)
    k[:, K_CT:K_CT + 128] = np.where(p[:, None] > p[None, :], -1e30, 0)
    for e in range(E):
        k[[e, 32 + e], K_ROW + 128 * e:K_ROW + 128 * (e + 1)] = 1
    return c, k, np.arange(M, dtype=np.float32)[None, :]


def _chunks(np, w):
    n = w.shape[0] // 128
    return np.concatenate([w[128 * c:128 * (c + 1)] for c in range(n)], axis=1)


def kernel(**inputs):
    import numpy as np
    import concourse.bacc as bacc
    from concourse.bass_utils import run_bass_kernel_spmd

    a = {k: np.asarray(v) for k, v in inputs.items()}
    f0 = {k[7:]: v for k, v in a.items() if k.startswith("L0_ffn_")}
    at = {k[9:]: v for k, v in a.items() if k.startswith("L1_xattn_")}
    f1 = {k[7:]: v for k, v in a.items() if k.startswith("L1_ffn_")}
    tokens = lambda t: np.ascontiguousarray(t.transpose(1, 0, 2).reshape(S, B * D))
    cat = np.concatenate
    w = cat([cat([_chunks(np, f0["in_proj_w"][e].T), _chunks(np, f0["out_proj_w"][e].T),
                  _chunks(np, f0["lin1_w"][e].T), _chunks(np, f0["lin2_w"][e].T)], axis=1) for e in range(E)], axis=1)
    wc = cat([_chunks(np, cat([at["Wq"], at["Wk"], at["Wv"]]).T), _chunks(np, at["Wo"].T)], axis=1)
    vec = cat([cat([f0["in_proj_b"][e], f0["out_proj_b"][e], f0["lin2_b"][e], f0["ln1_w"][e], f0["ln1_b"][e],
                    f0["ln2_w"][e], f0["ln2_b"][e]]) for e in range(E)])[None, :]
    vc = cat([at["bq"], at["bk"], at["bv"], at["bo"]])[None, :]
    e12 = cat([cat([f1["ew1"][e], f1["ew2"][e]]).T for e in range(EM)], axis=1)
    tw = cat([_chunks(np, cat([f1["sw1"], f1["sw2"]]).T), _chunks(np, f1["sw3"].T), _chunks(np, e12),
              cat([f1["ew3"][e].T for e in range(EM)], axis=1)], axis=1)
    tvec = cat([f1["sb1"], f1["sb2"], f1["sb3"], f1["s_ln_g"], f1["s_ln_b"], f1["sel_ln_g"], f1["sel_ln_b"],
                f1["sg_b"], f1["eg_b"], f1["exp_bias"]])[None, :]
    tg = cat([f1["sg_w"], f1["eg_w"]]).T.reshape(KC, 128, EM + 1).transpose(1, 0, 2)
    tb = cat([f1["eb1"], f1["eb2"], f1["eb3"]], axis=1)
    cst, kst, pos = _consts(np)
    arrays = {
        "x": tokens(a["x"]), "ctx": tokens(a["ctx_1024"]), "mask": a["mask_Bx1xS2_ik1"].reshape(1, B * S),
        "w": w, "wc": wc, "vec": vec, "vc": vc, "b1": f0["lin1_b"],
        "gw": f0["gate_w"].T.reshape(KC, 128, E).transpose(1, 0, 2), "gb": f0["gate_b"][None, :],
        "tw": tw, "tvec": tvec, "tg": tg, "tb": tb,
        "ib": f1["index_b"].reshape(MT, 128).T, "it": f1["index_t"].reshape(MT, 128).T,
        "ibr": f1["index_b"][None, :], "itr": f1["index_t"][None, :], "cst": cst, "kst": kst, "pos": pos,
    }
    arrays = {f"in_{k}": np.ascontiguousarray(v) for k, v in arrays.items()}
    nc = bacc.Bacc("TRN2", target_bir_lowering=False, num_devices=1)
    args = [nc.dram_tensor(k, v.shape, mybir.dt.from_np(v.dtype), kind="ExternalInput").ap() for k, v in arrays.items()]
    out = nc.dram_tensor("out", (B * S, D), mybir.dt.float32, kind="ExternalOutput").ap()
    comb = nc.dram_tensor("comb", (B * S, 2 * D), mybir.dt.float32, kind="Internal").ap()
    shared = nc.dram_tensor("shared", (B * S, D), mybir.dt.float32, kind="Internal").ap()
    encoder_kernel(nc, *args, out, comb, shared)
    r = run_bass_kernel_spmd(nc, [arrays], core_ids=[0])
    return np.asarray(r.results[0]["out"]).reshape(B, S, D)
```
